# Optimizing a Trainium2 kernel written in Bass

```python
import numpy as np
import jax
import jax.numpy as jnp

def _softmax(x, axis=-1):
    return jax.nn.softmax(x, axis=axis)

def _gelu(x):
    return jax.nn.gelu(x, approximate=True)

def _silu(x):
    return jax.nn.silu(x)

def _sigmoid(x):
    return jax.nn.sigmoid(x)

def _layernorm(x, axis=-1, eps=1e-05):
    m = jnp.mean(x, axis=axis, keepdims=True)
    v = jnp.var(x, axis=axis, keepdims=True)
    return (x - m) / jnp.sqrt(v + eps)

def _scatter_add(tgt, idx, src, axis=0):
    return tgt.at[idx].add(src)

def _segment_sum(src, seg, n):
    return jax.ops.segment_sum(src, seg, n)
kernel_name = 'mk_sandwich_d1_jaxref_r4_687e42'

def setup_inputs(seed: int=0):
    np.random.seed(seed)
    _w = jnp.asarray

    def _L0_attn_setup():
        import jax, jax.numpy as jnp
        import numpy as np
        B, T, D_MODEL = (2, 128, 256)
        D_INNER, D_HEAD, D_CONV = (512, 64, 4)
        N_HEADS, D_STATE = (32, 32)
        DT_MIN, DT_MAX, K_MAX, EPS = (0.0001, 0.1, 0.5, 1e-08)

        def _forward(x, W_in, dw_weight, dw_bias, W_bc, W_out, skip, A_log, dt_bias):
            Bsz, Tlen, D = x.shape
            DI, K = dw_weight.shape
            H, N = A_log.shape
            DH = DI // H
            proj = jnp.einsum('btd,od->bto', x, W_in)
            gate = proj[..., :DI]
            value_raw = proj[..., DI:2 * DI]
            params = proj[..., 2 * DI:].reshape(Bsz, Tlen, H, 2)
            xp = jnp.pad(value_raw, ((0, 0), (K - 1, 0), (0, 0)))
            conv = dw_bias + sum((xp[:, k:k + Tlen, :] * dw_weight[:, k] for k in range(K)))
            value = jax.nn.silu(conv)
            dt = jnp.clip(jax.nn.softplus(params[..., 0] + dt_bias), DT_MIN, DT_MAX)
            kd = K_MAX * jax.nn.sigmoid(params[..., 1])
            A = jnp.exp(A_log)
            bc = jnp.einsum('bti,oi->bto', value, W_bc).reshape(Bsz, Tlen, H, 4, N)
            bc = bc / (jnp.sqrt(jnp.sum(bc * bc, axis=-1, keepdims=True)) + EPS)
            Bz, Bx, Cz, Cx = (bc[..., 0, :], bc[..., 1, :], bc[..., 2, :], bc[..., 3, :])
            u = value.reshape(Bsz, Tlen, H, DH)

            def step(carry, inp):
                z, s = carry
                u_t, dt_t, k_t, Bz_t, Bx_t, Cz_t, Cx_t = inp
                dtE = dt_t[:, :, None, None]
                S = 1.0 / (1.0 + dt_t[..., None] * k_t[..., None] + (dt_t * dt_t)[..., None] * A)
                z = S[..., None] * (z - dtE * A[None, :, :, None] * s + dtE * (Bz_t[..., None] * u_t[:, :, None, :]))
                s = s + dtE * z + dtE * (Bx_t[..., None] * u_t[:, :, None, :])
                y = jnp.einsum('bhn,bhnd->bhd', Cz_t, z) + jnp.einsum('bhn,bhnd->bhd', Cx_t, s)
                return ((z, s), y)
            tm = lambda a: jnp.moveaxis(a, 1, 0)
            init = (jnp.zeros((Bsz, H, N, DH), x.dtype), jnp.zeros((Bsz, H, N, DH), x.dtype))
            _, ys = jax.lax.scan(step, init, (tm(u), tm(dt), tm(kd), tm(Bz), tm(Bx), tm(Cz), tm(Cx)))
            y = jnp.moveaxis(ys, 0, 1).reshape(Bsz, Tlen, DI)
            y = (y + skip * value) * jax.nn.silu(gate)
            return jnp.einsum('bti,oi->bto', y, W_out)
        key = jax.random.key(seed)
        ks = jax.random.split(key, 8)
        n = lambda k, sh, s=1.0: jax.random.normal(k, sh, jnp.float32) * s
        return {'x': n(ks[0], (B, T, D_MODEL)), 'W_in': n(ks[1], (2 * D_INNER + N_HEADS * 2, D_MODEL), D_MODEL ** (-0.5)), 'dw_weight': n(ks[2], (D_INNER, D_CONV), D_CONV ** (-0.5)), 'dw_bias': n(ks[3], (D_INNER,), 0.1), 'W_bc': n(ks[4], (N_HEADS * 4 * D_STATE, D_INNER), D_INNER ** (-0.5)), 'W_out': n(ks[5], (D_MODEL, D_INNER), D_INNER ** (-0.5)), 'skip': jnp.ones((D_INNER,), jnp.float32), 'A_log': n(ks[6], (N_HEADS, D_STATE), 0.5), 'dt_bias': n(ks[7], (N_HEADS,), 0.5)}
    _L0_attn_in = _L0_attn_setup()

    def _L0_ffn_setup():
        import jax, jax.numpy as jnp
        import numpy as np
        EMB = 256
        FF = 4 * EMB

        def _ternary(w):
            scale = jnp.maximum(jnp.mean(jnp.abs(w)), 1e-08)
            w_t = jnp.clip(jnp.round(w / scale), -1.0, 1.0)
            return w + jax.lax.stop_gradient(w_t - w)
        key = jax.random.key(seed)
        kx, k1, k2, kb1, kb2 = jax.random.split(key, 5)
        x = jax.random.normal(kx, (4, 512, EMB), dtype=jnp.float32)
        lim1 = 1.0 / np.sqrt(EMB)
        lim2 = 1.0 / np.sqrt(FF)
        W1 = jax.random.uniform(k1, (FF, EMB), jnp.float32, -lim1, lim1)
        b1 = jax.random.uniform(kb1, (FF,), jnp.float32, -lim1, lim1)
        W2 = jax.random.uniform(k2, (EMB, FF), jnp.float32, -lim2, lim2)
        b2 = jax.random.uniform(kb2, (EMB,), jnp.float32, -lim2, lim2)
        return {'x': x, 'W1': W1, 'b1': b1, 'W2': W2, 'b2': b2}
    _L0_ffn_in = _L0_ffn_setup()
    _d = {'L0_attn_x': _L0_attn_in['x'], 'L0_attn_W_in': _L0_attn_in['W_in'], 'L0_attn_dw_weight': _L0_attn_in['dw_weight'], 'L0_attn_dw_bias': _L0_attn_in['dw_bias'], 'L0_attn_W_bc': _L0_attn_in['W_bc'], 'L0_attn_W_out': _L0_attn_in['W_out'], 'L0_attn_skip': _L0_attn_in['skip'], 'L0_attn_A_log': _L0_attn_in['A_log'], 'L0_attn_dt_bias': _L0_attn_in['dt_bias'], 'L0_ffn_W1': _L0_ffn_in['W1'], 'L0_ffn_b1': _L0_ffn_in['b1'], 'L0_ffn_W2': _L0_ffn_in['W2'], 'L0_ffn_b2': _L0_ffn_in['b2']}
    _x0 = _d['L0_attn_x']
    _d['L0_attn_x'] = jax.random.normal(jax.random.fold_in(jax.random.key(seed), 1), (8, 512, 256), dtype=_x0.dtype)
    del _x0
    return _d

def reference(L0_attn_x, L0_attn_W_in, L0_attn_dw_weight, L0_attn_dw_bias, L0_attn_W_bc, L0_attn_W_out, L0_attn_skip, L0_attn_A_log, L0_attn_dt_bias, L0_ffn_W1, L0_ffn_b1, L0_ffn_W2, L0_ffn_b2):

    def _L0_attn_ref(x, W_in, dw_weight, dw_bias, W_bc, W_out, skip, A_log, dt_bias):
        import jax, jax.numpy as jnp
        import numpy as np
        B, T, D_MODEL = (2, 128, 256)
        D_INNER, D_HEAD, D_CONV = (512, 64, 4)
        N_HEADS, D_STATE = (32, 32)
        DT_MIN, DT_MAX, K_MAX, EPS = (0.0001, 0.1, 0.5, 1e-08)

        def _forward(x, W_in, dw_weight, dw_bias, W_bc, W_out, skip, A_log, dt_bias):
            Bsz, Tlen, D = x.shape
            DI, K = dw_weight.shape
            H, N = A_log.shape
            DH = DI // H
            proj = jnp.einsum('btd,od->bto', x, W_in)
            gate = proj[..., :DI]
            value_raw = proj[..., DI:2 * DI]
            params = proj[..., 2 * DI:].reshape(Bsz, Tlen, H, 2)
            xp = jnp.pad(value_raw, ((0, 0), (K - 1, 0), (0, 0)))
            conv = dw_bias + sum((xp[:, k:k + Tlen, :] * dw_weight[:, k] for k in range(K)))
            value = jax.nn.silu(conv)
            dt = jnp.clip(jax.nn.softplus(params[..., 0] + dt_bias), DT_MIN, DT_MAX)
            kd = K_MAX * jax.nn.sigmoid(params[..., 1])
            A = jnp.exp(A_log)
            bc = jnp.einsum('bti,oi->bto', value, W_bc).reshape(Bsz, Tlen, H, 4, N)
            bc = bc / (jnp.sqrt(jnp.sum(bc * bc, axis=-1, keepdims=True)) + EPS)
            Bz, Bx, Cz, Cx = (bc[..., 0, :], bc[..., 1, :], bc[..., 2, :], bc[..., 3, :])
            u = value.reshape(Bsz, Tlen, H, DH)

            def step(carry, inp):
                z, s = carry
                u_t, dt_t, k_t, Bz_t, Bx_t, Cz_t, Cx_t = inp
                dtE = dt_t[:, :, None, None]
                S = 1.0 / (1.0 + dt_t[..., None] * k_t[..., None] + (dt_t * dt_t)[..., None] * A)
                z = S[..., None] * (z - dtE * A[None, :, :, None] * s + dtE * (Bz_t[..., None] * u_t[:, :, None, :]))
                s = s + dtE * z + dtE * (Bx_t[..., None] * u_t[:, :, None, :])
                y = jnp.einsum('bhn,bhnd->bhd', Cz_t, z) + jnp.einsum('bhn,bhnd->bhd', Cx_t, s)
                return ((z, s), y)
            tm = lambda a: jnp.moveaxis(a, 1, 0)
            init = (jnp.zeros((Bsz, H, N, DH), x.dtype), jnp.zeros((Bsz, H, N, DH), x.dtype))
            _, ys = jax.lax.scan(step, init, (tm(u), tm(dt), tm(kd), tm(Bz), tm(Bx), tm(Cz), tm(Cx)))
            y = jnp.moveaxis(ys, 0, 1).reshape(Bsz, Tlen, DI)
            y = (y + skip * value) * jax.nn.silu(gate)
            return jnp.einsum('bti,oi->bto', y, W_out)
        return _forward(x, W_in, dw_weight, dw_bias, W_bc, W_out, skip, A_log, dt_bias)

    def _L0_ffn_ref(x, W1, b1, W2, b2):
        import jax, jax.numpy as jnp
        import numpy as np
        EMB = 256
        FF = 4 * EMB

        def _ternary(w):
            scale = jnp.maximum(jnp.mean(jnp.abs(w)), 1e-08)
            w_t = jnp.clip(jnp.round(w / scale), -1.0, 1.0)
            return w + jax.lax.stop_gradient(w_t - w)
        h = jnp.einsum('bsd,fd->bsf', x, _ternary(W1)) + b1
        h = jax.nn.gelu(h, approximate=False)
        out = jnp.einsum('bsf,df->bsd', h, _ternary(W2)) + b2
        return out
    x = L0_attn_x
    x = x + _layernorm(_L0_attn_ref(_layernorm(x, axis=-1), L0_attn_W_in, L0_attn_dw_weight, L0_attn_dw_bias, L0_attn_W_bc, L0_attn_W_out, L0_attn_skip, L0_attn_A_log, L0_attn_dt_bias), axis=-1)
    x = x + _layernorm(_L0_ffn_ref(_layernorm(x, axis=-1), L0_ffn_W1, L0_ffn_b1, L0_ffn_W2, L0_ffn_b2), axis=-1)
    return x

_drawn_inputs = setup_inputs


def setup_inputs(seed=0):
    import zlib

    import numpy as np

    out = dict(_drawn_inputs(seed))
    spreads = {'L0_attn_skip': (1.0, 0.2)}
    factors = {'L0_attn_dt_bias': 8.0, 'L0_ffn_b1': 39.858, 'L0_ffn_b2': 64.0}
    for name, (base, spread) in spreads.items():
        noise = np.random.default_rng([zlib.crc32(name.encode()), seed]).standard_normal(out[name].shape)
        drawn = base * np.exp(spread * noise) if base else spread * noise
        out[name] = jnp.asarray(drawn.astype(out[name].dtype))
    for name, factor in factors.items():
        out[name] = (out[name] * factor).astype(out[name].dtype)
    return out
```

```python
from contextlib import ExitStack

import concourse.bass as bass
from concourse import mybir

F32 = mybir.dt.float32
ALU = mybir.AluOpType
ACT = mybir.ActivationFunctionType
AX = mybir.AxisListType

P = 128
B, T, D = 8, 512, 256
TT = T // P
KD = D // P
DI = 512
KI = DI // P
H, N, DH = 32, 32, 16
HP = P // N
HG = H // HP
NJ = 4
TAPS = 4
FF = 1024
KF = FF // P
C = P
LN_EPS = 1e-5
NORM_EPS = 1e-8
DT_MIN, DT_MAX, K_MAX = 1e-4, 0.1, 0.5
SOFTPLUS_CAP = 10.0
TINY = 1e-12


class Signal:

    def __init__(self, ctx, nc, name, per, step=1, credited=True):
        self.sem, self.per, self.step = ctx.enter_context(nc.semaphore(name)), per, step
        self.given = per if credited else 0

    def at(self, b, item):
        return (b * self.per + self.given + item + 1) * self.step


class Own:

    def __init__(self, sem):
        self.sem, self.n = sem, 0

    def one(self):
        self.n += 1
        return 1


def project(nc, a, dram):
    with ExitStack() as ctx:
        def sb(name, shape):
            return ctx.enter_context(nc.sbuf_tensor(name, shape, F32))

        def sem(name):
            return ctx.enter_context(nc.semaphore(name))

        ident = sb("p_ident", [P, P])
        w_in = sb("w_in", [P, KD, 2 * DI + 2 * H])
        taps = sb("taps", [P, KI, TAPS])
        dw_bias = sb("dw_bias", [P, KI])
        skip = sb("skip", [P, KI])
        dt_bias = sb("dt_bias", [H, 1])
        x = sb("p_x", [P, TT, D])
        stats = sb("p_stats", [P, TT, 6])
        mv = sb("p_mv", [P, TT, 2])
        sd = sb("p_sd", [P, TT])
        rstd = sb("p_rstd", [P, TT])
        xn = sb("p_xn", [P, TT, D])
        xnT = sb("p_xnT", [P, KD, T])
        vraw = sb("vraw", [P, KI, T + TAPS - 1])
        conv = sb("conv", [P, KI, T])
        val = sb("val", [P, KI, T])
        gate = sb("gate", [P, KI, T])
        svg = sb("svg", [P, KI, T])
        u = sb("p_u", [P, TT, DI])
        z = sb("z", [H, T])
        ez = sb("ez", [H, T])
        ek = sb("ek", [H, T])
        lz = sb("lz", [H, T])
        w = sb("w", [H, T])
        dt = sb("dt", [H, T])
        kd = sb("kd", [H, T])
        zero = sb("zero", [H, T])
        E = sb("E", [H, TT, C + 1])
        e_inv = sb("e_inv", [H, TT, C])
        e_end = sb("e_end", [H, TT])
        n_alpha = sb("n_alpha", [H, T])
        beta = sb("beta", [H, T])
        eps = sb("p_eps", [P, 1])
        ps_x = [ctx.enter_context(nc.psum_tensor(f"ps_x{k}", [P, T], F32)) for k in range(KD)]
        ps_w = [ctx.enter_context(nc.psum_tensor(f"ps_w{k}", [P, T], F32)) for k in range(2)]
        ps_dt = ctx.enter_context(nc.psum_tensor("ps_dt", [P, T], F32))
        ps_k = ctx.enter_context(nc.psum_tensor("ps_k", [P, T], F32))
        ps_u = [ctx.enter_context(nc.psum_tensor(f"ps_u{k}", [P, T], F32)) for k in range(2)]

        def sig(name, per, step=1, credited=True):
            return Signal(ctx, nc, "p_" + name, per, step, credited)

        consts_in = sem("p_consts_in")
        const_set = sem("p_const_set")
        x_in = sig("x_in", 1, 16, credited=False)
        xn_ready = sig("xn_ready", TT)
        var_ready = sig("var_ready", 1)
        sd_ready = sig("sd_ready", 1)
        xT_made = sig("xT_made", 1)
        xnT_ready = sig("xnT_ready", KD)
        logit_made = sig("logit_made", 2)
        z_ready = sig("z_ready", 1)
        exps_ready = sig("exps_ready", 3)
        one_ez_ready = sig("one_ez_ready", 1)
        tile_made = sig("tile_made", 2 * KI)
        vraw_ready = sig("vraw_ready", KI)
        gate_ready = sig("gate_ready", KI)
        conv_ready = sig("conv_ready", KI)
        val_ready = sig("val_ready", KI)
        svg_ready = sig("svg_ready", KI)
        steps_ready = sig("steps_ready", 1)
        u_made = sig("u_made", TT)
        u_ready = sig("u_ready", TT)
        steps_stored = sig("steps_stored", 5, 16)
        val_stored = sig("val_stored", 1, 16)
        gate_stored = sig("gate_stored", 1, 16)
        svg_stored = sig("svg_stored", 1, 16)
        u_stored = sig("u_stored", 1, 16)
        own_dve = sem("p_own_dve")

        with nc.Block() as block:
            @block.sync
            def _(sp):
                for dst, src in ((ident, a["ident"]), (taps, a["taps"]), (dw_bias, a["dw_bias"]),
                                 (skip, a["skip"]), (dt_bias, a["dt_bias"])):
                    sp.dma_start(dst.ap(), src).then_inc(consts_in, 16)
                sp.dma_start(w_in.ap(), a["w_inT"].rearrange("(k p) o -> p k o", p=P)).then_inc(consts_in, 16)
                for s in (steps_stored, val_stored, gate_stored, svg_stored, u_stored):
                    sp.sem_inc(s.sem, s.given * s.step)
                with sp.Fori(0, B) as b:
                    sp.wait_ge(steps_ready.sem, steps_ready.at(b, 0))
                    for name, src in (("n_alpha", n_alpha.ap()), ("beta", beta.ap()), ("dt", dt.ap()),
                                      ("e_inv", e_inv.ap().rearrange("h c t -> h (c t)")), ("e_end", e_end.ap())):
                        sp.dma_start(dram[name][b], src).then_inc(steps_stored.sem, steps_stored.step)
                    sp.wait_ge(gate_ready.sem, gate_ready.at(b, KI - 1))
                    sp.dma_start(dram["gateT"][b], gate.ap()).then_inc(gate_stored.sem, gate_stored.step)
                    sp.wait_ge(val_ready.sem, val_ready.at(b, KI - 1))
                    sp.dma_start(dram["valT"][b], val.ap()).then_inc(val_stored.sem, val_stored.step)
                    sp.wait_ge(svg_ready.sem, svg_ready.at(b, KI - 1))
                    sp.dma_start(dram["svgT"][b], svg.ap()).then_inc(svg_stored.sem, svg_stored.step)
                    sp.wait_ge(u_ready.sem, u_ready.at(b, TT - 1))
                    sp.dma_start(dram["u"][b], u.ap()).then_inc(u_stored.sem, u_stored.step)
                for s in (steps_stored, val_stored, gate_stored, svg_stored, u_stored):
                    sp.wait_ge(s.sem, s.at(B - 1, s.per - 1))

            @block.gpsimd
            def _(pool):
                with pool.Fori(0, B) as b:
                    pool.wait_ge(xn_ready.sem, xn_ready.at(b, -1))
                    pool.dma_start(x.ap(), a["x"][b].rearrange("(t p) d -> p t d", p=P)).then_inc(x_in.sem, x_in.step)

            @block.tensor
            def _(pe):
                for s in (xT_made, logit_made, tile_made, u_made):
                    pe.sem_inc(s.sem, s.given * s.step)
                pe.wait_ge(consts_in, 96)
                with pe.Fori(0, B) as b:
                    pe.wait_ge(xn_ready.sem, xn_ready.at(b, TT - 1))
                    pe.wait_ge(xnT_ready.sem, xnT_ready.at(b, -1))
                    for k in range(KD):
                        for t in range(TT):
                            mm = pe.transpose(ps_x[k][:, t * P:(t + 1) * P], xn[:, t, k * P:(k + 1) * P], ident.ap())
                    mm.then_inc(xT_made.sem, xT_made.step)
                    pe.wait_ge(xnT_ready.sem, xnT_ready.at(b, KD - 1))
                    pe.wait_ge(z_ready.sem, z_ready.at(b, -1))
                    pe.wait_ge(exps_ready.sem, exps_ready.at(b, -1))
                    for ps, col in ((ps_dt, 2 * DI), (ps_k, 2 * DI + H)):
                        for k in range(KD):
                            mm = pe.matmul(ps[0:H, :], w_in[:, k, col:col + H], xnT[:, k, :],
                                           start=(k == 0), stop=(k == KD - 1))
                        mm.then_inc(logit_made.sem, logit_made.step)
                    for i in range(2 * KI):
                        if i < 2:
                            pe.wait_ge(gate_ready.sem, gate_ready.at(b, KI * 0 - 2 + i))
                        elif i < KI + 2:
                            pe.wait_ge(vraw_ready.sem, vraw_ready.at(b, i - 2))
                        else:
                            pe.wait_ge(gate_ready.sem, gate_ready.at(b, i - 2 - KI))
                        col = (DI + i * P) if i < KI else (i - KI) * P
                        for k in range(KD):
                            mm = pe.matmul(ps_w[i % 2].ap(), w_in[:, k, col:col + P], xnT[:, k, :],
                                           start=(k == 0), stop=(k == KD - 1))
                        mm.then_inc(tile_made.sem, tile_made.step)
                    pe.wait_ge(val_ready.sem, val_ready.at(b, KI - 1))
                    for t in range(TT):
                        pe.wait_ge(u_ready.sem, u_ready.at(b, t - 2))
                        for k in range(KI):
                            mm = pe.transpose(ps_u[t % 2][:, k * P:(k + 1) * P], val[:, k, t * P:(t + 1) * P], ident.ap())
                        mm.then_inc(u_made.sem, u_made.step)

            @block.scalar
            def _(act):
                for s in (sd_ready, xnT_ready, exps_ready, vraw_ready, gate_ready, val_ready, u_ready):
                    act.sem_inc(s.sem, s.given * s.step)
                act.wait_ge(consts_in, 96)
                act.wait_ge(const_set, 4)
                with act.Fori(0, B) as b:
                    act.wait_ge(var_ready.sem, var_ready.at(b, 0))
                    act.wait_ge(sd_ready.sem, sd_ready.at(b, -1))
                    act.activation(sd.ap(), mv[:, :, 1], ACT.Sqrt, bias=eps.ap()).then_inc(sd_ready.sem, sd_ready.step)
                    act.wait_ge(xT_made.sem, xT_made.at(b, 0))
                    act.wait_ge(tile_made.sem, tile_made.at(b, -1))
                    for k in range(KD):
                        act.activation(xnT[:, k, :], ps_x[k].ap(), ACT.Copy).then_inc(xnT_ready.sem, xnT_ready.step)
                    act.wait_ge(z_ready.sem, z_ready.at(b, 0))
                    act.activation(ez.ap(), z.ap(), ACT.Exp).then_inc(exps_ready.sem, exps_ready.step)
                    act.wait_ge(logit_made.sem, logit_made.at(b, 1))
                    act.wait_ge(steps_ready.sem, steps_ready.at(b, -1))
                    act.activation(ek.ap(), ps_k[0:H, :], ACT.Exp, scale=-1.0).then_inc(exps_ready.sem, exps_ready.step)
                    act.wait_ge(one_ez_ready.sem, one_ez_ready.at(b, 0))
                    act.activation(lz.ap(), w.ap(), ACT.Ln).then_inc(exps_ready.sem, exps_ready.step)
                    for i in range(KI):
                        act.wait_ge(tile_made.sem, tile_made.at(b, i))
                        act.wait_ge(conv_ready.sem, conv_ready.at(b, -1))
                        act.activation(vraw[:, i, TAPS - 1:], ps_w[i % 2].ap(), ACT.Copy).then_inc(vraw_ready.sem, vraw_ready.step)
                    act.wait_ge(gate_stored.sem, gate_stored.at(b, -1))
                    act.wait_ge(svg_ready.sem, svg_ready.at(b, -1))
                    for i in range(KI):
                        act.wait_ge(tile_made.sem, tile_made.at(b, KI + i))
                        act.activation(gate[:, i, :], ps_w[i % 2].ap(), ACT.Silu).then_inc(gate_ready.sem, gate_ready.step)
                    act.wait_ge(val_stored.sem, val_stored.at(b, -1))
                    act.wait_ge(u_made.sem, u_made.at(b, -1))
                    for i in range(KI):
                        act.wait_ge(conv_ready.sem, conv_ready.at(b, i))
                        act.activation(val[:, i, :], conv[:, i, :], ACT.Silu).then_inc(val_ready.sem, val_ready.step)
                    act.wait_ge(u_stored.sem, u_stored.at(b, -1))
                    for t in range(TT):
                        act.wait_ge(u_made.sem, u_made.at(b, t))
                        act.activation(u[:, t, :], ps_u[t % 2].ap(), ACT.Copy).then_inc(u_ready.sem, u_ready.step)

            @block.vector
            def _(dve):
                for s in (var_ready, xn_ready, z_ready, one_ez_ready, steps_ready, conv_ready, svg_ready):
                    dve.sem_inc(s.sem, s.given * s.step)
                dve.memset(vraw.ap(), 0.0).then_inc(const_set, 1)
                dve.memset(zero.ap(), 0.0).then_inc(const_set, 1)
                dve.memset(E.ap(), 1.0).then_inc(const_set, 1)
                dve.memset(eps.ap(), LN_EPS).then_inc(const_set, 1)
                dve.wait_ge(consts_in, 96)
                dve.wait_ge(const_set, 4)
                own = Own(own_dve)
                with dve.Fori(0, B) as b:
                    dve.wait_ge(x_in.sem, x_in.at(b, 0))
                    dve.wait_ge(sd_ready.sem, sd_ready.at(b, -1))
                    for t in range(TT):
                        dve.bn_stats(stats[:, t, :], x[:, t, :]).then_inc(own.sem, own.one())
                    dve.wait_ge(own.sem, own.n)
                    for t in range(TT):
                        ins = dve.bn_aggr(mv[:, t, :], stats[:, t, :])
                        if t < TT - 1:
                            ins.then_inc(own.sem, own.one())
                    ins.then_inc(var_ready.sem, var_ready.step)
                    dve.wait_ge(sd_ready.sem, sd_ready.at(b, 0))
                    dve.reciprocal(rstd.ap(), sd.ap()).then_inc(own.sem, own.one())
                    dve.wait_ge(own.sem, own.n)
                    dve.wait_ge(xT_made.sem, xT_made.at(b, -1))
                    for t in range(TT):
                        dve.tensor_scalar(xn[:, t, :], x[:, t, :], mv[:, t, 0:1], rstd[:, t:t + 1],
                                                      ALU.subtract, ALU.mult).then_inc(xn_ready.sem, xn_ready.step)
                    dve.wait_ge(logit_made.sem, logit_made.at(b, 0))
                    dve.tensor_scalar(z.ap(), ps_dt[0:H, :], dt_bias.ap(), SOFTPLUS_CAP, ALU.add, ALU.min).then_inc(z_ready.sem, z_ready.step)
                    dve.wait_ge(exps_ready.sem, exps_ready.at(b, 0))
                    dve.tensor_scalar(w.ap(), ez.ap(), 1.0, None, ALU.add).then_inc(one_ez_ready.sem, one_ez_ready.step)
                    dve.wait_ge(one_ez_ready.sem, one_ez_ready.at(b, 0))
                    dve.wait_ge(steps_stored.sem, steps_stored.at(b, -1))
                    dve.tensor_scalar(kd.ap(), w.ap(), 1.0, TINY, ALU.subtract, ALU.max).then_inc(own.sem, own.one())
                    dve.wait_ge(own.sem, own.n)
                    dve.reciprocal(dt.ap(), kd.ap()).then_inc(own.sem, own.one())
                    dve.wait_ge(own.sem, own.n)
                    dve.tensor_tensor(dt.ap(), dt.ap(), ez.ap(), ALU.mult).then_inc(own.sem, own.one())
                    dve.wait_ge(exps_ready.sem, exps_ready.at(b, 2))
                    dve.wait_ge(own.sem, own.n)
                    dve.tensor_tensor(dt.ap(), dt.ap(), lz.ap(), ALU.mult).then_inc(own.sem, own.one())
                    dve.wait_ge(own.sem, own.n)
                    dve.tensor_scalar(dt.ap(), dt.ap(), DT_MIN, DT_MAX, ALU.max, ALU.min).then_inc(own.sem, own.one())
                    dve.tensor_scalar(kd.ap(), ek.ap(), 1.0, 1.0 / K_MAX, ALU.add, ALU.mult).then_inc(own.sem, own.one())
                    dve.wait_ge(own.sem, own.n)
                    dve.reciprocal(kd.ap(), kd.ap()).then_inc(own.sem, own.one())
                    dve.wait_ge(own.sem, own.n)
                    dve.tensor_tensor(kd.ap(), kd.ap(), dt.ap(), ALU.mult).then_inc(own.sem, own.one())
                    dve.wait_ge(own.sem, own.n)
                    dve.tensor_scalar(kd.ap(), kd.ap(), 1.0, None, ALU.add).then_inc(own.sem, own.one())
                    dve.wait_ge(own.sem, own.n)
                    for c in range(TT):
                        dve.tensor_tensor_scan(E[:, c, 1:], kd[:, c * C:(c + 1) * C], zero[:, 0:C], 1.0,
                                                   ALU.mult, ALU.add).then_inc(own.sem, own.one())
                    dve.wait_ge(own.sem, own.n)
                    dve.reciprocal(e_inv.ap(), E[:, :, 1:]).then_inc(own.sem, own.one())
                    dt4, na4, be4 = (v.ap().rearrange("h (c t) -> h c t", c=TT) for v in (dt, n_alpha, beta))
                    dve.tensor_tensor(be4, dt4, E[:, :, 0:C], ALU.mult).then_inc(own.sem, own.one())
                    dve.wait_ge(own.sem, own.n)
                    dve.tensor_copy(e_end.ap(), e_inv[:, :, C - 1]).then_inc(own.sem, own.one())
                    dve.scalar_tensor_tensor(out=na4, in0=dt4, scalar=-1.0, in1=e_inv.ap(), op0=ALU.mult, op1=ALU.mult).then_inc(own.sem, own.one())
                    dve.wait_ge(own.sem, own.n)
                    dve.tensor_copy(z[:, 0:1], e_end[:, 0:1]).then_inc(steps_ready.sem, steps_ready.step)
                    dve.wait_ge(vraw_ready.sem, vraw_ready.at(b, KI - 1))
                    dve.wait_ge(val_ready.sem, val_ready.at(b, -1))
                    for k in range(TAPS):
                        for i in range(KI):
                            src = vraw[:, i, k:k + T]
                            if k == 0:
                                dve.tensor_scalar(conv[:, i, :], src, taps[:, i, 0:1], dw_bias[:, i:i + 1],
                                                      ALU.mult, ALU.add).then_inc(own.sem, own.one())
                            else:
                                ins = dve.scalar_tensor_tensor(out=conv[:, i, :], in0=src, scalar=taps[:, i, k:k + 1],
                                                               in1=conv[:, i, :], op0=ALU.mult, op1=ALU.add)
                                ins.then_inc(conv_ready.sem, conv_ready.step) if k == TAPS - 1 else ins.then_inc(own.sem, own.one())
                            if k < TAPS - 1 and i == KI - 1:
                                dve.wait_ge(own.sem, own.n)
                    dve.wait_ge(svg_stored.sem, svg_stored.at(b, -1))
                    dve.wait_ge(gate_ready.sem, gate_ready.at(b, KI - 1))
                    for i in range(KI):
                        dve.wait_ge(val_ready.sem, val_ready.at(b, i))
                        dve.scalar_tensor_tensor(out=svg[:, i, :], in0=val[:, i, :], scalar=skip[:, i:i + 1],
                                                              in1=gate[:, i, :], op0=ALU.mult, op1=ALU.mult).then_inc(svg_ready.sem, svg_ready.step)
                    dve.wait_ge(own.sem, own.n)
                    dve.sem_clear(own.sem)
                    own.n = 0


def mix(nc, a, dram):
    LAST = HG - 1
    with ExitStack() as ctx:
        def sb(name, shape):
            return ctx.enter_context(nc.sbuf_tensor("m_" + name, shape, F32))

        def ps(name):
            return ctx.enter_context(nc.psum_tensor("m_ps_" + name, [P, T], F32))

        def sem(name):
            return ctx.enter_context(nc.semaphore("m_" + name))

        def sig(name, per, step=1, credited=True):
            return Signal(ctx, nc, "m_" + name, per, step, credited)

        ident = sb("ident", [P, P])
        head_sum = sb("head_sum", [P, N])
        causal = sb("causal", [P, C])
        head_block = sb("head_block", [P, HP, DH])
        carry = sb("carry", [P, TT, C])
        A = sb("A", [P, HG])
        one = sb("one", [P, 1])
        psi = sb("psi", [P, 2, 2, HG, TT, C + 1])
        shear = sb("shear", [P, 2, HG, T])
        prod = sb("prod", [P, 2, 2, 2, HG * TT // 2])
        e_end = sb("e_end", [P, HG, TT])
        w_bc = sb("w_bc", [P, NJ, KI, P])
        valT = sb("valT", [P, KI, T])
        u = sb("u", [P, TT, DI])
        raw = [sb(f"raw{s}", [P, NJ, T]) for s in range(2)]
        sq = sb("sq", [P, NJ, T])
        scale = sb("scale", [P, NJ, T])
        rows_ = sb("rows", [P, T])
        factor = sb("factor", [P, T])
        k = [sb(f"k{s}", [P, 2, T]) for s in range(2)]
        q = [sb(f"q{s}", [P, 2, T]) for s in range(2)]
        kx = sb("kx", [P, 2, T])
        qx = sb("qx", [P, 2, T])
        g = sb("g", [P, HP, T])
        kT = sb("kT", [P, 2, (TT - 1) * P])
        dX = sb("dX", [P, TT - 1, 2, DH])
        X = sb("X", [P, TT - 1, 2, DH])
        tmp = sb("tmp", [P, 2, DH])
        Xb = sb("Xb", [P, TT - 1, 2, HP, N])
        end = sb("end", [P, TT])
        coef = sb("coef", [P, 2, 2, TT])
        y = sb("y", [P, T])
        ps_a = [ps(f"a{n}") for n in range(2)]
        ps_s = ps("s")
        ps_g = [ps(f"g{n}") for n in range(2)]
        ps_k = [ps(f"k{n}") for n in range(2)]
        ps_y = ps("y")
        KW = (TT - 1) * P
        ps_dX = ps_k[0][:, KW:KW + (TT - 1) * 2 * DH]

        consts_in = sem("consts_in")
        const_set = sem("const_set")
        w_in = [sig(f"w_in{j}", HG, 16) for j in range(NJ)]
        val_in = sig("val_in", 1, 16)
        u_in = sig("u_in", 1, 16)
        n_alpha_in = sig("n_alpha_in", HP, 16)
        beta_in = [sig(f"beta_in{n}", HP, 16) for n in range(HG)]
        e_end_in = sig("e_end_in", HP, 16)
        factor_in = sig("factor_in", 3 * HG, 16)
        beta_scaled = sig("beta_scaled", HG)
        stepped = sig("stepped", 1)
        ab_ready = sig("ab_ready", HG)
        log_ready = sig("log_ready", HG)
        sum_ready = sig("sum_ready", HG)
        det_ready = sig("det_ready", HG)
        a_made = sig("a_made", HG * NJ)
        raw_ready = sig("raw_ready", HG * NJ)
        sq_ready = sig("sq_ready", HG * NJ)
        sums_made = sig("sums_made", HG)
        norm_ready = sig("norm_ready", HG)
        rows_ready = sig("rows_ready", HG)
        rows_stored = sig("rows_stored", HG * NJ, 16)
        scale_in = sig("scale_in", HG * HP, 16)
        b_scaled = sig("b_scaled", HG)
        c_scaled = sig("c_scaled", HG)
        kx_ready = sig("kx_ready", HG)
        qx_ready = sig("qx_ready", HG)
        raw_used = sig("raw_used", HG)
        k_ready = sig("k_ready", HG)
        q_ready = sig("q_ready", HG)
        g_made = sig("g_made", HG * HP)
        g_ready = sig("g_ready", HG * HP)
        kT_made = sig("kT_made", HG * 2)
        kT_ready = sig("kT_ready", HG * 2)
        dX_made = sig("dX_made", HG)
        dX_ready = sig("dX_ready", HG)
        coef_ready = sig("coef_ready", HG)
        X_ready = sig("X_ready", HG * (TT - 1))
        Xb_ready = sig("Xb_ready", HG * (TT - 1))
        y_made = sig("y_made", HG)
        y_ready = sig("y_ready", HG)
        y_stored = sig("y_stored", HG * HP, 16)
        steps_dve, own_dve, own_pool = sem("steps_dve"), sem("own_dve"), sem("own_pool")

        def over_rows(eng, body):
            with eng.Fori(0, B - 1) as b:
                body(b, False)
            body(B - 1, True)

        def chunks(v):
            return v.rearrange("p (c t) -> p c t", c=TT)

        def spread(src, parts=N):
            return src.unsqueeze(0).to_broadcast([parts, *src.shape])

        with nc.Block() as block:
            @block.sync
            def _(sp):
                for dst, name in ((ident, "ident"), (head_sum, "head_sum"), (causal, "causal"), (A, "a_log")):
                    sp.dma_start(dst.ap(), a[name]).then_inc(consts_in, 16)
                sp.dma_start(head_block.ap().rearrange("p h d -> p (h d)"), a["head_block"]).then_inc(consts_in, 16)
                for s in (*w_in, val_in, u_in, n_alpha_in, *beta_in, e_end_in, factor_in, rows_stored, scale_in):
                    sp.sem_inc(s.sem, s.given * s.step)

                def heads(name, b, h):
                    return dram[name][b].rearrange("(g h) t -> h g t", h=HP)[h]

                def load_w(group, j):
                    sp.dma_start(w_bc[:, j, :, :].rearrange("p k m -> p (k m)"), a["w_bcT"][group, j]).then_inc(w_in[j].sem, w_in[j].step)

                def load_n_alpha(b):
                    for h in range(HP):
                        sp.dma_start(shear[h * N:(h + 1) * N, 1, :, :], spread(heads("n_alpha", b, h))).then_inc(n_alpha_in.sem, n_alpha_in.step)

                def load_beta(b, group):
                    for h in range(HP):
                        sp.dma_start(shear[h * N:(h + 1) * N, 0, group, :],
                                                           spread(dram["beta"][b, group * HP + h])).then_inc(beta_in[group].sem, beta_in[group].step)

                def load_e_end(b):
                    for h in range(HP):
                        sp.dma_start(e_end[h * N:(h + 1) * N, :, :], spread(heads("e_end", b, h))).then_inc(e_end_in.sem, e_end_in.step)

                def load_factor(b, group):
                    for j, name in enumerate(("beta", "dt", "e_inv")):
                        sp.dma_start(factor[j * N:j * N + HP, :],
                                                  dram[name][b, group * HP:(group + 1) * HP, :]).then_inc(factor_in.sem, factor_in.step)

                def spread_scales(b, group, u_):
                    sp.wait_ge(rows_ready.sem, rows_ready.at(b, group))
                    for j in range(NJ):
                        sp.dma_start(dram["norm"][u_, j * HP:(j + 1) * HP, :],
                                                      rows_[j * N:j * N + HP, :]).then_inc(rows_stored.sem, rows_stored.step)
                    sp.wait_ge(rows_stored.sem, rows_stored.at(b, (group + 1) * NJ - 1))
                    sp.wait_ge(b_scaled.sem, b_scaled.at(b, group - 1))
                    sp.wait_ge(c_scaled.sem, c_scaled.at(b, group - 1))
                    for h in range(HP):
                        src = dram["norm"][u_, 0:NJ * HP, :].rearrange("(j h) t -> h j t", h=HP)[h]
                        sp.dma_start(scale[h * N:(h + 1) * N, :, :], spread(src)).then_inc(scale_in.sem, scale_in.step)

                for j in range(NJ):
                    load_w(0, j)
                sp.dma_start(valT.ap(), dram["valT"][0]).then_inc(val_in.sem, val_in.step)
                load_n_alpha(0)
                for group in range(HG):
                    load_beta(0, group)
                load_e_end(0)
                sp.wait_ge(const_set, 4)
                load_factor(0, 0)
                for j in range(NJ):
                    sp.wait_ge(a_made.sem, a_made.at(0, j))
                    load_w(1, j)
                sp.dma_start(u.ap(), dram["u"][0]).then_inc(u_in.sem, u_in.step)
                spread_scales(0, 0, 0)

                def body(b, last):
                    for group in range(HG):
                        ahead = not (last and group == LAST)
                        if ahead:
                            nb, ng = (b, group + 1) if group < LAST else (b + 1, 0)
                            sp.wait_ge(rows_ready.sem, rows_ready.at(b, group))
                            load_factor(nb, ng)
                        if not (last and group >= LAST - 1):
                            for j in range(NJ):
                                sp.wait_ge(a_made.sem, a_made.at(b, (group + 1) * NJ + j))
                                load_w((group + 2) % HG, j)
                        if not last:
                            if group == 0:
                                sp.wait_ge(ab_ready.sem, ab_ready.at(b, LAST))
                                load_n_alpha(b + 1)
                            if group == LAST - 1:
                                sp.wait_ge(a_made.sem, a_made.at(b, HG * NJ - 1))
                                sp.dma_start(valT.ap(), dram["valT"][b + 1]).then_inc(val_in.sem, val_in.step)
                            sp.wait_ge(c_scaled.sem, c_scaled.at(b, group))
                            sp.wait_ge(coef_ready.sem, coef_ready.at(b, group))
                            load_beta(b + 1, group)
                        if ahead:
                            spread_scales(b, group + 1, (group + 1) % 2)
                    if not last:
                        load_e_end(b + 1)
                        sp.wait_ge(y_made.sem, y_made.at(b, LAST))
                        sp.dma_start(u.ap(), dram["u"][b + 1]).then_inc(u_in.sem, u_in.step)
                over_rows(sp, body)

            @block.gpsimd
            def _(pool):
                for s in (ab_ready, c_scaled, kx_ready, qx_ready, Xb_ready):
                    pool.sem_inc(s.sem, s.given * s.step)
                own = Own(own_pool)
                pool.wait_ge(consts_in, 80)
                pool.wait_ge(const_set, 5)

                def body(b, last):
                    pool.wait_ge(stepped.sem, stepped.at(b, 0))
                    for group in range(HG):
                        pool.tensor_tensor(shear[:, 0, group, :], shear[:, 0, group, :],
                                                       shear[:, 1, group, :], ALU.mult).then_inc(ab_ready.sem, ab_ready.step)
                    for group in range(HG):
                        s = group % 2
                        r4 = raw[s]
                        pool.wait_ge(scale_in.sem, scale_in.at(b, (group + 1) * HP - 1))
                        pool.wait_ge(raw_ready.sem, raw_ready.at(b, group * NJ + 3))
                        pool.tensor_tensor(r4[:, 2:4, :], r4[:, 2:4, :], scale[:, 2:4, :], ALU.mult).then_inc(own.sem, own.one())
                        pool.wait_ge(det_ready.sem, det_ready.at(b, group))
                        pool.wait_ge(own.sem, own.n)
                        pool.tensor_tensor(
                            r4[:, 2:4, :], r4[:, 2:4, :],
                            shear[:, 0, group, :].unsqueeze(1).to_broadcast([P, 2, T]), ALU.mult).then_inc(c_scaled.sem, c_scaled.step)

                        pool.wait_ge(b_scaled.sem, b_scaled.at(b, group))
                        pool.wait_ge(k_ready.sem, k_ready.at(b, group - 1))
                        for row in range(2):
                            ins = pool.tensor_tensor(chunks(kx[:, row, :]), chunks(r4[:, 1, :]),
                                                     psi[:, row, 1, group, :, 1:], ALU.mult)
                            ins.then_inc(own.sem, own.one()) if row == 0 else ins.then_inc(kx_ready.sem, kx_ready.step)
                        pool.wait_ge(c_scaled.sem, c_scaled.at(b, group))
                        pool.wait_ge(q_ready.sem, q_ready.at(b, group - 1))
                        for row in range(2):
                            ins = pool.tensor_tensor(chunks(qx[:, row, :]), chunks(r4[:, 3, :]),
                                                     psi[:, row, 0, group, :, 1:], ALU.mult)
                            ins.then_inc(own.sem, own.one()) if row == 0 else ins.then_inc(qx_ready.sem, qx_ready.step)
                        for c in range(TT - 1):
                            pool.wait_ge(X_ready.sem, X_ready.at(b, group * (TT - 1) + c))
                            pool.wait_ge(y_made.sem, y_made.at(b, group - 1))
                            for part in range(2):
                                ins = pool.tensor_tensor(
                                    Xb[:, c, part, :, 0:DH], X[:, c, part, :].unsqueeze(1).to_broadcast([P, HP, DH]),
                                    head_block.ap(), ALU.mult)
                                ins.then_inc(own.sem, own.one()) if part == 0 else ins.then_inc(Xb_ready.sem, Xb_ready.step)
                    pool.wait_ge(own.sem, own.n)
                    pool.sem_clear(own.sem)
                    own.n = 0
                over_rows(pool, body)

            @block.tensor
            def _(pe):
                for s in (a_made, sums_made, g_made, kT_made, dX_made, y_made):
                    pe.sem_inc(s.sem, s.given * s.step)
                pe.wait_ge(consts_in, 80)
                pe.wait_ge(const_set, 5)

                def products(b, group):
                    for j in range(NJ):
                        pe.wait_ge(w_in[j].sem, w_in[j].at(b, group))
                        if group % HG == 0 and j == 0:
                            pe.wait_ge(val_in.sem, val_in.at(b, group // HG))
                        pe.wait_ge(sq_ready.sem, sq_ready.at(b, group * NJ + j - 2))
                        for kt in range(KI):
                            mm = pe.matmul(ps_a[j % 2].ap(), w_bc[:, j, kt, :], valT[:, kt, :],
                                           start=(kt == 0), stop=(kt == KI - 1))
                        mm.then_inc(a_made.sem, a_made.step)
                    pe.wait_ge(sq_ready.sem, sq_ready.at(b, group * NJ + NJ - 1))
                    pe.wait_ge(norm_ready.sem, norm_ready.at(b, group - 1))
                    for j in range(NJ):
                        mm = pe.matmul(ps_s[j * N:(j + 1) * N, :], head_sum.ap(), sq[:, j, :],
                                       start=True, stop=True, skip_group_check=True)
                    mm.then_inc(sums_made.sem, sums_made.step)

                def scores(b, group, h, s):
                    pe.wait_ge(g_ready.sem, g_ready.at(b, group * HP + h - 2))
                    rows = slice(h * N, (h + 1) * N)
                    for c in range(TT):
                        cols = slice(c * C, (c + 1) * C)
                        for part in range(2):
                            mm = pe.matmul(ps_g[h % 2][:, cols], k[s][rows, part, cols], q[s][rows, part, cols],
                                           start=(part == 0), stop=(part == 1), skip_group_check=True)
                    mm.then_inc(g_made.sem, g_made.step)

                products(0, 0)

                def body(b, last):
                    for group in range(HG):
                        s = group % 2
                        if not (last and group == LAST):
                            products(b, group + 1)
                        pe.wait_ge(k_ready.sem, k_ready.at(b, group))
                        pe.wait_ge(kT_ready.sem, kT_ready.at(b, group * 2 - 1))
                        pe.wait_ge(dX_ready.sem, dX_ready.at(b, group - 1))
                        for part in range(2):
                            for c in range(TT - 1):
                                mm = pe.transpose(ps_k[part][:, c * P:(c + 1) * P],
                                                  k[s][:, part, c * C:(c + 1) * C], ident.ap())
                            mm.then_inc(kT_made.sem, kT_made.step)
                        pe.wait_ge(q_ready.sem, q_ready.at(b, group))
                        for h in range(2):
                            scores(b, group, h, s)
                        pe.wait_ge(kT_ready.sem, kT_ready.at(b, group * 2 + 1))
                        if group == 0:
                            pe.wait_ge(u_in.sem, u_in.at(b, 0))
                        for c in range(TT - 1):
                            for part in range(2):
                                for h in range(HP):
                                    ch = (group * HP + h) * DH
                                    col = KW + (c * 2 + part) * DH
                                    mm = pe.matmul(ps_k[0][h * N:(h + 1) * N, col:col + DH],
                                                   kT[:, part, c * P + h * N:c * P + (h + 1) * N],
                                                   u[:, c, ch:ch + DH], start=True, stop=True, skip_group_check=True)
                        mm.then_inc(dX_made.sem, dX_made.step)
                        for h in range(2, HP):
                            scores(b, group, h, s)
                        pe.wait_ge(g_ready.sem, g_ready.at(b, group * HP + HP - 1))
                        pe.wait_ge(y_ready.sem, y_ready.at(b, group - 1))
                        for c in range(TT):
                            cols = slice(c * C, (c + 1) * C)
                            for h in range(HP):
                                ch = (group * HP + h) * DH
                                pe.matmul(ps_y[h * N:h * N + DH, cols], u[:, c, ch:ch + DH], g[:, h, cols],
                                          start=(c == 0), stop=False, skip_group_check=True)
                        for c in range(1, TT):
                            cols = slice(c * C, (c + 1) * C)
                            pe.wait_ge(Xb_ready.sem, Xb_ready.at(b, group * (TT - 1) + c - 1))
                            for part in range(2):
                                mm = pe.matmul(ps_y[:, cols], Xb[:, c - 1, part, :, :].rearrange("p h d -> p (h d)"),
                                               q[s][:, part, cols], start=False, stop=(part == 1),
                                               skip_group_check=True)
                        mm.then_inc(y_made.sem, y_made.step)
                over_rows(pe, body)

            @block.scalar
            def _(act):
                for s in (beta_scaled, log_ready, det_ready, raw_ready, sq_ready, norm_ready, kT_ready, y_ready,
                          y_stored):
                    act.sem_inc(s.sem, s.given * s.step)
                act.wait_ge(consts_in, 80)
                act.wait_ge(const_set, 5)
                own_a = sem("own_act")
                act.activation(A.ap(), A.ap(), ACT.Exp).then_inc(own_a, 1)
                act.wait_ge(own_a, 1)

                def scale_beta(b, group):
                    act.wait_ge(beta_in[group].sem, beta_in[group].at(b, HP - 1))
                    act.activation(shear[:, 0, group, :], shear[:, 0, group, :], ACT.Copy,
                                                  scale=A[:, group:group + 1]).then_inc(beta_scaled.sem, beta_scaled.step)

                def evacuate(b, group, s):
                    act.wait_ge(raw_used.sem, raw_used.at(b, group - 2))
                    act.wait_ge(kx_ready.sem, kx_ready.at(b, group - 2))
                    act.wait_ge(qx_ready.sem, qx_ready.at(b, group - 2))
                    act.wait_ge(sums_made.sem, sums_made.at(b, group - 1))
                    for j in range(NJ):
                        act.wait_ge(a_made.sem, a_made.at(b, group * NJ + j))
                        act.activation(raw[s][:, j, :], ps_a[j % 2].ap(), ACT.Copy).then_inc(raw_ready.sem, raw_ready.step)
                        act.activation(sq[:, j, :], ps_a[j % 2].ap(), ACT.Square).then_inc(sq_ready.sem, sq_ready.step)
                    act.wait_ge(sums_made.sem, sums_made.at(b, group))
                    act.wait_ge(rows_stored.sem, rows_stored.at(b, group * NJ - 1))
                    act.activation(rows_.ap(), ps_s.ap(), ACT.Sqrt).then_inc(norm_ready.sem, norm_ready.step)

                for group in range(HG):
                    scale_beta(0, group)
                evacuate(0, 0, 0)

                def body(b, last):
                    for group in range(HG):
                        act.wait_ge(ab_ready.sem, ab_ready.at(b, group))
                        act.activation(shear[:, 0, group, :], shear[:, 0, group, :], ACT.Ln,
                                                    bias=one[:, :], scale=-1.0).then_inc(log_ready.sem, log_ready.step)
                    for group in range(HG):
                        s = group % 2
                        act.wait_ge(sum_ready.sem, sum_ready.at(b, group))
                        act.activation(shear[:, 0, group, :], shear[:, 0, group, :], ACT.Exp, scale=-1.0).then_inc(det_ready.sem, det_ready.step)
                        if not (last and group == LAST):
                            evacuate(b, group + 1, 1 - s)
                        for part in range(2):
                            act.wait_ge(kT_made.sem, kT_made.at(b, group * 2 + part))
                            act.wait_ge(dX_made.sem, dX_made.at(b, group - 1))
                            act.activation(kT[:, part, :], ps_k[part][:, 0:KW], ACT.Copy).then_inc(kT_ready.sem, kT_ready.step)
                        if not last and group > 0:
                            scale_beta(b + 1, group - 1)
                        act.wait_ge(y_made.sem, y_made.at(b, group))
                        act.wait_ge(y_stored.sem, y_stored.at(b, group * HP - 1))
                        act.activation(y.ap(), ps_y.ap(), ACT.Copy).then_inc(y_ready.sem, y_ready.step)
                        act.wait_ge(y_ready.sem, y_ready.at(b, group))
                        for h in range(HP):
                            act.dma_start(dram["yT"][b, group, h * DH:(h + 1) * DH, :],
                                                      y[h * N:h * N + DH, :]).then_inc(y_stored.sem, y_stored.step)
                    if not last:
                        scale_beta(b + 1, LAST)
                over_rows(act, body)
                act.wait_ge(y_stored.sem, y_stored.at(B - 1, HG * HP - 1))

            @block.vector
            def _(dve):
                for s in (stepped, sum_ready, rows_ready, b_scaled, raw_used, k_ready, q_ready, g_ready, dX_ready,
                          coef_ready, X_ready):
                    dve.sem_inc(s.sem, s.given * s.step)
                dve.memset(one.ap(), 1.0).then_inc(const_set, 1)
                dve.memset(Xb.ap(), 0.0).then_inc(const_set, 1)
                dve.memset(factor.ap(), 1.0).then_inc(const_set, 1)
                dve.memset(ps_y.ap(), 0.0).then_inc(const_set, 1)
                dve.memset(carry.ap(), 1.0).then_inc(const_set, 1)
                own = Own(own_dve)
                dve.wait_ge(const_set, 5)
                dve.memset(carry[:, :, 0:1], 0.0).then_inc(own.sem, own.one())
                for row in range(2):
                    for comp in range(2):
                        dve.memset(psi[:, row, comp, :, :, 0:1], 1.0 if row == comp else 0.0).then_inc(own.sem, own.one())
                dve.wait_ge(own.sem, own.n)
                dve.sem_clear(own.sem)
                own.n = 0
                steps = Own(steps_dve)
                HALF = HG * TT // 2
                psi_t = [psi.ap().rearrange("p r k g c t -> p r k (g c) t")[:, :, :, n * HALF:(n + 1) * HALF, :]
                         for n in range(2)]
                shear_t = [shear.ap().rearrange("p k g (c t) -> p k (g c) t", c=TT)[:, :, n * HALF:(n + 1) * HALF, :]
                           for n in range(2)]

                def recurrence(b):
                    dve.wait_ge(n_alpha_in.sem, n_alpha_in.at(b, HP - 1))
                    dve.wait_ge(beta_scaled.sem, beta_scaled.at(b, LAST))
                    dve.wait_ge(kx_ready.sem, kx_ready.at(b, -1))
                    dve.wait_ge(qx_ready.sem, qx_ready.at(b, -1))
                    for t in range(C):
                        for n in range(2):
                            if t:
                                dve.wait_ge(steps.sem, 4 * (t - 1) + 3 + n)
                            dve.tensor_tensor(prod[:, n], psi_t[n][:, :, :, :, t],
                                                    shear_t[n][:, :, :, t].unsqueeze(1).to_broadcast([P, 2, 2, HALF]),
                                                    ALU.mult).then_inc(steps.sem, steps.one())
                        for n in range(2):
                            dve.wait_ge(steps.sem, 4 * t + 1 + n)
                            dve.tensor_tensor(psi_t[n][:, :, :, :, t + 1], psi_t[n][:, :, :, :, t],
                                                    prod[:, n, :, ::-1, :], ALU.add).then_inc(steps.sem, steps.one())
                    dve.wait_ge(steps.sem, steps.n)
                    dve.tensor_copy(tmp[:, 0, 0:1], carry[:, 0, 0:1]).then_inc(stepped.sem, stepped.step)
                    dve.wait_ge(steps.sem, steps.n)
                    dve.sem_clear(steps.sem)
                    steps.n = 0

                def log_sum(b, group):
                    dve.wait_ge(log_ready.sem, log_ready.at(b, group))
                    dve.tensor_tensor_scan(shear[:, 0, group, :], carry.ap().rearrange("p c t -> p (c t)"),
                                                        shear[:, 0, group, :], 0.0, ALU.mult, ALU.add).then_inc(sum_ready.sem, sum_ready.step)

                def scales(b, group):
                    dve.wait_ge(norm_ready.sem, norm_ready.at(b, group))
                    dve.tensor_scalar(rows_.ap(), rows_.ap(), NORM_EPS, None, ALU.add).then_inc(own.sem, own.one())
                    dve.wait_ge(own.sem, own.n)
                    dve.reciprocal(rows_.ap(), rows_.ap()).then_inc(own.sem, own.one())
                    dve.wait_ge(factor_in.sem, factor_in.at(b, 3 * (group + 1) - 1))
                    dve.wait_ge(own.sem, own.n)
                    dve.tensor_tensor(rows_.ap(), rows_.ap(), factor.ap(), ALU.mult).then_inc(rows_ready.sem, rows_ready.step)

                scales(0, 0)
                dve.wait_ge(own.sem, own.n)
                dve.sem_clear(own.sem)
                own.n = 0

                def body(b, last):
                    recurrence(b)
                    log_sum(b, 0)
                    dve.wait_ge(e_end_in.sem, e_end_in.at(b, HP - 1))
                    for group in range(HG):
                        s = group % 2
                        r4 = raw[s]
                        dve.wait_ge(scale_in.sem, scale_in.at(b, (group + 1) * HP - 1))
                        dve.wait_ge(raw_ready.sem, raw_ready.at(b, group * NJ + 1))
                        dve.tensor_tensor(r4[:, 0:2, :], r4[:, 0:2, :], scale[:, 0:2, :], ALU.mult).then_inc(b_scaled.sem, b_scaled.step)
                        dve.wait_ge(b_scaled.sem, b_scaled.at(b, group))
                        dve.wait_ge(kT_made.sem, kT_made.at(b, 2 * (group - 2) + 1))
                        dve.wait_ge(g_made.sem, g_made.at(b, (group - 1) * HP - 1))
                        dve.wait_ge(y_made.sem, y_made.at(b, group - 2))
                        for row in range(2):
                            dve.tensor_tensor(chunks(k[s][:, row, :]), chunks(r4[:, 0, :]),
                                                  psi[:, row, 0, group, :, 0:C], ALU.mult).then_inc(own.sem, own.one())
                        dve.wait_ge(kx_ready.sem, kx_ready.at(b, group))
                        dve.wait_ge(own.sem, own.n)
                        dve.tensor_tensor(k[s].ap(), k[s].ap(), kx.ap(), ALU.add).then_inc(k_ready.sem, k_ready.step)
                        dve.wait_ge(c_scaled.sem, c_scaled.at(b, group))
                        for row in range(2):
                            ins = dve.tensor_tensor(chunks(q[s][:, 1 - row, :]), chunks(r4[:, 2, :]),
                                                    psi[:, row, 1, group, :, 1:], ALU.mult)
                            ins.then_inc(own.sem, own.one()) if row == 0 else ins.then_inc(raw_used.sem, raw_used.step)
                        dve.wait_ge(raw_used.sem, raw_used.at(b, group))
                        dve.wait_ge(own.sem, own.n)
                        dve.wait_ge(qx_ready.sem, qx_ready.at(b, group))
                        dve.tensor_tensor(q[s][:, 0, :], q[s][:, 0, :], qx[:, 1, :], ALU.subtract).then_inc(own.sem, own.one())
                        dve.tensor_tensor(q[s][:, 1, :], qx[:, 0, :], q[s][:, 1, :], ALU.subtract).then_inc(q_ready.sem, q_ready.step)
                        dve.wait_ge(det_ready.sem, det_ready.at(b, group))
                        det_end = chunks(shear[:, 0, group, :])[:, :, C - 1]
                        dve.tensor_tensor(end.ap(), det_end, e_end[:, group, :], ALU.mult).then_inc(own.sem, own.one())
                        dve.wait_ge(own.sem, own.n)
                        for comp, by in ((1, end.ap()), (0, det_end)):
                            ins = dve.tensor_tensor(coef[:, comp, :, :], psi[:, :, comp, group, :, C],
                                                    by.unsqueeze(1).to_broadcast([P, 2, TT]), ALU.mult)
                            ins.then_inc(own.sem, own.one()) if comp else ins.then_inc(coef_ready.sem, coef_ready.step)
                        if group < LAST:
                            log_sum(b, group + 1)
                        if not (last and group == LAST):
                            scales(b, group + 1)

                        def mask(h):
                            dve.wait_ge(g_made.sem, g_made.at(b, group * HP + h))
                            dve.wait_ge(y_made.sem, y_made.at(b, group - 1))
                            dve.tensor_tensor(chunks(g[:, h, :]), chunks(ps_g[h % 2].ap()),
                                                         causal.ap().unsqueeze(1).to_broadcast([P, TT, C]), ALU.mult).then_inc(g_ready.sem, g_ready.step)

                        for h in range(2):
                            mask(h)
                        dve.wait_ge(dX_made.sem, dX_made.at(b, group))
                        dve.tensor_copy(dX.ap().rearrange("p c r d -> p (c r d)"), ps_dX).then_inc(dX_ready.sem, dX_ready.step)
                        dve.wait_ge(dX_ready.sem, dX_ready.at(b, group))
                        dve.wait_ge(coef_ready.sem, coef_ready.at(b, group))
                        dve.wait_ge(Xb_ready.sem, Xb_ready.at(b, group * (TT - 1) - 1))
                        for h in range(2, HP):
                            mask(h)
                        for c in range(TT - 1):
                            if c:
                                dve.wait_ge(X_ready.sem, X_ready.at(b, group * (TT - 1) + c - 1))
                                dve.tensor_tensor(dX[:, c], dX[:, c], X[:, c - 1], ALU.add).then_inc(own.sem, own.one())
                                dve.wait_ge(own.sem, own.n)
                            for part in range(2):
                                comp, row = (1, 0) if part == 0 else (0, 1)
                                dve.tensor_scalar(tmp[:, part, :], dX[:, c, 1 - part, :],
                                                      coef[:, comp, row, c:c + 1], None, ALU.mult).then_inc(own.sem, own.one())
                            dve.wait_ge(own.sem, own.n)
                            for part in range(2):
                                comp, row = (1, 1) if part == 0 else (0, 0)
                                ins = dve.scalar_tensor_tensor(
                                    out=X[:, c, part, :], in0=dX[:, c, part, :], scalar=coef[:, comp, row, c:c + 1],
                                    in1=tmp[:, part, :], op0=ALU.mult, op1=ALU.subtract)
                                ins.then_inc(own.sem, own.one()) if part == 0 else ins.then_inc(X_ready.sem, X_ready.step)
                            dve.wait_ge(own.sem, own.n)
                    dve.wait_ge(X_ready.sem, X_ready.at(b, HG * (TT - 1) - 1))
                    dve.wait_ge(own.sem, own.n)
                    dve.sem_clear(own.sem)
                    own.n = 0
                over_rows(dve, body)


def ffn(nc, a, dram, out):
    F32R = mybir.dt.float32r
    with ExitStack() as ctx:
        def sb(name, shape, dt=F32):
            return ctx.enter_context(nc.sbuf_tensor("f_" + name, shape, dt))

        def sem(name):
            return ctx.enter_context(nc.semaphore("f_" + name))

        def sig(name, per, step=1, credited=True):
            return Signal(ctx, nc, "f_" + name, per, step, credited)

        ident = sb("ident", [P, P])
        ones = sb("ones", [P, P])
        w_out = sb("w_out", [P, KI, D])
        w1 = sb("w1", [P, KD, FF])
        w2 = sb("w2", [P, KF, D])
        above = sb("above", [P, KD * FF])
        below = sb("below", [P, KD * FF])
        t1 = sb("t1", [P, KD, FF], F32R)
        t2 = sb("t2", [P, KF, D], F32R)
        b1 = sb("b1", [P, KF])
        b2 = sb("b2", [P, D])
        eps = sb("eps", [P, 1])
        total = sb("total", [P, 2])
        half = sb("half", [P, 2])
        nhalf = sb("nhalf", [P, 2])
        y = [sb(f"y{s}", [P, KI, T]) for s in range(2)]
        gate = [sb(f"gate{s}", [P, KI, T]) for s in range(2)]
        svg = [sb(f"svg{s}", [P, KI, T]) for s in range(2)]
        x = [sb(f"x{s}", [P, TT, D]) for s in range(2)]
        stats = sb("stats", [P, TT, 6])
        mv = [sb(f"mv{n}", [P, TT, 2]) for n in range(3)]
        sd = [sb(f"sd{n}", [P, TT]) for n in range(3)]
        rstd = [sb(f"rstd{n}", [P, TT]) for n in range(3)]
        on = sb("on", [P, TT, D])
        xn = sb("xn", [P, TT, D])
        xh = sb("xh", [P, KD, T], F32R)
        xl = sb("xl", [P, KD, T], F32R)
        g = [sb(f"g{s}", [P, T]) for s in range(2)]
        gh = sb("gh", [P, KF, T], F32R)
        gl = sb("gl", [P, KF, T], F32R)
        o2 = sb("o2", [P, TT, D])
        res = sb("res", [P, TT, D])
        ps_o = [ctx.enter_context(nc.psum_tensor(f"f_ps_o{k}", [P, 2, D], F32)) for k in range(2)]
        ps_x = [ctx.enter_context(nc.psum_tensor(f"f_ps_x{k}", [P, T], F32)) for k in range(KD)]
        ps_h = [ctx.enter_context(nc.psum_tensor(f"f_ps_h{k}", [P, T], F32)) for k in range(2)]
        ps_2 = [ctx.enter_context(nc.psum_tensor(f"f_ps_2{k}", [P, 2, D], F32)) for k in range(2)]

        consts_in = sem("consts_in")
        weights_in = sem("weights_in")
        const_set = sem("const_set")
        sums_made = sem("sums_made")
        ternary_ready = sem("ternary_ready")
        x_in = [sig(f"x_in{s}", 1, 16) for s in range(2)]
        y_in = [sig(f"y_in{s}", 3, 16) for s in range(2)]
        gated = sig("gated", 1)
        proj_made = sig("proj_made", 1)
        var_ready = sig("var_ready", 2)
        sd_ready = sig("sd_ready", 2)
        var2_ready = sig("var2_ready", 1)
        sd2_ready = sig("sd2_ready", 1)
        xn_ready = sig("xn_ready", 1)
        xT_made = sig("xT_made", 1)
        xh_ready = sig("xh_ready", KD)
        xl_ready = sig("xl_ready", KD)
        h_made = sig("h_made", KF)
        g_ready = sig("g_ready", KF)
        gh_ready = sig("gh_ready", KF)
        gl_ready = sig("gl_ready", KF)
        o2_made = sig("o2_made", 1)
        o2_ready = sig("o2_ready", 1)
        res_ready = sig("res_ready", 1)
        res_stored = sig("res_stored", 1, 16)
        own_dve, own_pool = sem("own_dve"), sem("own_pool")

        def rows(eng, body):
            with eng.Fori(0, B // 2 - 1) as i:
                for s in range(2):
                    body(i * 2 + s, s, i, False)
            for s in range(2):
                body(B - 2 + s, s, B // 2 - 1, s == 1)

        with nc.Block() as block:
            @block.sync
            def _(sp):
                for dst, src in ((ident, a["ident"]), (b1, a["b1"])):
                    sp.dma_start(dst.ap(), src).then_inc(consts_in, 16)
                sp.dma_start(b2.ap(), a["b2"].to_broadcast([P, D])).then_inc(consts_in, 16)
                sp.dma_start(w_out.ap(), a["w_outT"].rearrange("(k p) o -> p k o", p=P)).then_inc(consts_in, 16)
                for s in (*x_in, *y_in, res_stored):
                    sp.sem_inc(s.sem, s.given * s.step)

                def load(b, s, pair, before):
                    sp.wait_ge(gated.sem, gated.at(before, 0))
                    sp.wait_ge(proj_made.sem, proj_made.at(before, 0))
                    for dst, name in ((y, "yT"), (gate, "gateT"), (svg, "svgT")):
                        src = dram[name][b]
                        if name == "yT":
                            src = src.rearrange("g c t -> (g c) t").rearrange("(k p) t -> p k t", p=P)
                        sp.dma_start(dst[s].ap(), src).then_inc(y_in[s].sem, y_in[s].step)
                    sp.wait_ge(res_ready.sem, res_ready.at(before, 0))
                    sp.dma_start(x[s].ap(), a["x"][b].rearrange("(t p) d -> p t d", p=P)).then_inc(x_in[s].sem, x_in[s].step)

                for s in range(2):
                    for dst, name in ((y, "yT"), (gate, "gateT"), (svg, "svgT")):
                        src = dram[name][s]
                        if name == "yT":
                            src = src.rearrange("g c t -> (g c) t").rearrange("(k p) t -> p k t", p=P)
                        sp.dma_start(dst[s].ap(), src).then_inc(y_in[s].sem, y_in[s].step)
                    sp.dma_start(x[s].ap(), a["x"][s].rearrange("(t p) d -> p t d", p=P)).then_inc(x_in[s].sem, x_in[s].step)
                    if s == 0:
                        sp.dma_start(w1.ap(), a["w1T"].rearrange("(k p) o -> p k o", p=P)).then_inc(weights_in, 16)
                        sp.dma_start(w2.ap(), a["w2T"].rearrange("(k p) o -> p k o", p=P)).then_inc(weights_in, 16)

                def store(b):
                    sp.wait_ge(res_ready.sem, res_ready.at(b, 0))
                    sp.dma_start(out[b].rearrange("(t p) d -> p t d", p=P), res.ap()).then_inc(res_stored.sem, res_stored.step)

                with sp.Fori(0, B // 2 - 1) as i:
                    for s in range(2):
                        store(i * 2 + s)
                        load(i * 2 + s + 2, s, i + 1, i * 2 + s)
                for s in range(2):
                    store(B - 2 + s)
                sp.wait_ge(res_stored.sem, res_stored.at(B - 1, 0))

            @block.gpsimd
            def _(pool):
                pool.sem_inc(gated.sem, gated.given * gated.step)
                own = Own(own_pool)

                def body(b, s, i, last):
                    pool.wait_ge(y_in[s].sem, y_in[s].at(i, 2))
                    pool.tensor_tensor(y[s].ap(), y[s].ap(), gate[s].ap(), ALU.mult).then_inc(own.sem, own.one())
                    pool.wait_ge(own.sem, own.n)
                    pool.tensor_tensor(y[s].ap(), y[s].ap(), svg[s].ap(), ALU.add).then_inc(gated.sem, gated.step)
                    pool.wait_ge(own.sem, own.n)
                    pool.sem_clear(own.sem)
                    own.n = 0
                rows(pool, body)

            @block.tensor
            def _(pe):
                for s in (proj_made, xT_made, h_made, o2_made):
                    pe.sem_inc(s.sem, s.given * s.step)
                pe.wait_ge(consts_in, 64)

                def project_out(b, s):
                    pe.wait_ge(gated.sem, gated.at(b, 0))
                    pe.wait_ge(xn_ready.sem, xn_ready.at(b, -1))
                    for t in range(TT):
                        for k in range(KI):
                            mm = pe.matmul(ps_o[t // 2][:, t % 2, :], y[s][:, k, t * P:(t + 1) * P], w_out[:, k, :],
                                           start=(k == 0), stop=(k == KI - 1), skip_group_check=True)
                    mm.then_inc(proj_made.sem, proj_made.step)

                project_out(0, 0)
                pe.wait_ge(const_set, 4)
                pe.matmul(ps_h[0][:, 0:2], ones.ap(), total.ap(), start=True, stop=True).then_inc(sums_made, 1)
                pe.wait_ge(ternary_ready, 2)

                def body(b, s, i, last):
                    pe.wait_ge(xn_ready.sem, xn_ready.at(b, 0))
                    pe.wait_ge(xl_ready.sem, xl_ready.at(b, -1))
                    for k in range(KD):
                        for t in range(TT):
                            mm = pe.transpose(ps_x[k][:, t * P:(t + 1) * P], xn[:, t, k * P:(k + 1) * P], ident.ap())
                    mm.then_inc(xT_made.sem, xT_made.step)
                    pe.wait_ge(xl_ready.sem, xl_ready.at(b, KD - 1))
                    for f in range(KF):
                        pe.wait_ge(g_ready.sem, g_ready.at(b, f - 2))
                        for k in range(KD):
                            for part in (xh, xl):
                                mm = pe.matmul(ps_h[f % 2].ap(), t1[:, k, f * P:(f + 1) * P], part[:, k, :],
                                               start=(k == 0 and part is xh), stop=(k == KD - 1 and part is xl))
                        mm.then_inc(h_made.sem, h_made.step)
                    if not last:
                        project_out(b + 1, 1 - s)
                    pe.wait_ge(gl_ready.sem, gl_ready.at(b, KF - 1))
                    pe.wait_ge(o2_ready.sem, o2_ready.at(b, -1))
                    for t in range(TT):
                        for f in range(KF):
                            for part in (gh, gl):
                                mm = pe.matmul(ps_2[t // 2][:, t % 2, :], part[:, f, t * P:(t + 1) * P], t2[:, f, :],
                                               start=(f == 0 and part is gh), stop=(f == KF - 1 and part is gl),
                                               skip_group_check=True)
                    mm.then_inc(o2_made.sem, o2_made.step)
                rows(pe, body)

            @block.scalar
            def _(act):
                for s in (sd_ready, sd2_ready, xh_ready, g_ready, gh_ready):
                    act.sem_inc(s.sem, s.given * s.step)
                act.wait_ge(consts_in, 64)
                act.wait_ge(const_set, 4)

                def deviation(b, n):
                    act.wait_ge(var_ready.sem, var_ready.at(b, n))
                    act.activation(sd[n].ap(), mv[n][:, :, 1], ACT.Sqrt, bias=eps.ap()).then_inc(sd_ready.sem, sd_ready.step)

                deviation(0, 0)
                deviation(0, 1)

                def body(b, s, i, last):
                    act.wait_ge(xT_made.sem, xT_made.at(b, 0))
                    act.wait_ge(h_made.sem, h_made.at(b, -1))
                    for k in range(KD):
                        act.activation(xh[:, k, :], ps_x[k].ap(), ACT.Copy).then_inc(xh_ready.sem, xh_ready.step)
                    act.wait_ge(o2_made.sem, o2_made.at(b, -1))
                    for f in range(KF):
                        act.wait_ge(h_made.sem, h_made.at(b, f))
                        act.wait_ge(gl_ready.sem, gl_ready.at(b, f - 2))
                        act.wait_ge(gh_ready.sem, gh_ready.at(b, f - 2))
                        act.activation(g[f % 2].ap(), ps_h[f % 2].ap(), ACT.Gelu, bias=b1[:, f:f + 1]).then_inc(g_ready.sem, g_ready.step)
                        act.wait_ge(g_ready.sem, g_ready.at(b, f))
                        act.activation(gh[:, f, :], g[f % 2].ap(), ACT.Copy).then_inc(gh_ready.sem, gh_ready.step)
                    if not last:
                        deviation(b + 1, 0)
                        deviation(b + 1, 1)
                    act.wait_ge(var2_ready.sem, var2_ready.at(b, 0))
                    act.activation(sd[2].ap(), mv[2][:, :, 1], ACT.Sqrt, bias=eps.ap()).then_inc(sd2_ready.sem, sd2_ready.step)
                rows(act, body)

            @block.vector
            def _(dve):
                for s in (var_ready, var2_ready, xn_ready, xl_ready, gl_ready, o2_ready, res_ready):
                    dve.sem_inc(s.sem, s.given * s.step)
                own = Own(own_dve)
                dve.memset(ones.ap(), 1.0).then_inc(const_set, 1)
                dve.memset(eps.ap(), LN_EPS).then_inc(const_set, 1)
                dve.wait_ge(weights_in, 32)
                flat = [w.ap().rearrange("p k o -> p (k o)") for w in (w1, w2)]
                for n in range(2):
                    dve.tensor_reduce(total[:, n:n + 1], flat[n], AX.X, ALU.add,
                                      apply_absolute_value=True).then_inc(const_set, 1)
                dve.wait_ge(sums_made, 1)
                dve.tensor_scalar(half.ap(), ps_h[0][:, 0:2], 1.0 / (D * FF), NORM_EPS, ALU.mult, ALU.max).then_inc(own.sem, own.one())
                dve.wait_ge(own.sem, own.n)
                dve.tensor_scalar(nhalf.ap(), half.ap(), -0.5, None, ALU.mult).then_inc(own.sem, own.one())
                dve.wait_ge(own.sem, own.n)
                dve.tensor_scalar(half.ap(), half.ap(), 0.5, None, ALU.mult).then_inc(own.sem, own.one())
                dve.wait_ge(own.sem, own.n)
                for n, (w, tern) in enumerate(((flat[0], t1), (flat[1], t2))):
                    dve.tensor_scalar(above.ap(), w, half[:, n:n + 1], None, ALU.is_gt).then_inc(own.sem, own.one())
                    dve.tensor_scalar(below.ap(), w, nhalf[:, n:n + 1], None, ALU.is_lt).then_inc(own.sem, own.one())
                    dve.wait_ge(own.sem, own.n)
                    dve.tensor_tensor(tern.ap().rearrange("p k o -> p (k o)"), above.ap(), below.ap(),
                                      ALU.subtract).then_inc(ternary_ready, 1)
                    dve.wait_ge(ternary_ready, n + 1)
                dve.wait_ge(own.sem, own.n)
                dve.sem_clear(own.sem)
                own.n = 0

                def moments(src, n, signal):
                    for t in range(TT):
                        dve.bn_stats(stats[:, t, :], src(t)).then_inc(own.sem, own.one())
                    dve.wait_ge(own.sem, own.n)
                    for t in range(TT):
                        ins = dve.bn_aggr(mv[n][:, t, :], stats[:, t, :])
                        ins.then_inc(own.sem, own.one()) if t < TT - 1 else ins.then_inc(signal.sem, signal.step)

                def normalise(dst, src, n, count=None):
                    for t in range(TT):
                        ins = dve.tensor_scalar(dst[:, t, :], src(t), mv[n][:, t, 0:1], rstd[n][:, t:t + 1],
                                                ALU.subtract, ALU.mult)
                        ins.then_inc(own.sem, own.one()) if count is None or t < TT - 1 else ins.then_inc(count.sem, count.step)

                def first_norms(b, s, i):
                    dve.wait_ge(proj_made.sem, proj_made.at(b, 0))
                    moments(lambda t: ps_o[t // 2][:, t % 2, :], 0, var_ready)
                    dve.wait_ge(sd_ready.sem, sd_ready.at(b, 0))
                    dve.reciprocal(rstd[0].ap(), sd[0].ap()).then_inc(own.sem, own.one())
                    dve.wait_ge(own.sem, own.n)
                    normalise(on, lambda t: ps_o[t // 2][:, t % 2, :], 0)
                    dve.wait_ge(own.sem, own.n)
                    dve.wait_ge(x_in[s].sem, x_in[s].at(i, 0))
                    dve.tensor_tensor(x[s].ap(), x[s].ap(), on.ap(), ALU.add).then_inc(own.sem, own.one())
                    dve.wait_ge(own.sem, own.n)
                    moments(lambda t: x[s][:, t, :], 1, var_ready)
                    dve.wait_ge(sd_ready.sem, sd_ready.at(b, 1))
                    dve.reciprocal(rstd[1].ap(), sd[1].ap()).then_inc(own.sem, own.one())
                    dve.wait_ge(own.sem, own.n)
                    dve.wait_ge(xT_made.sem, xT_made.at(b, -1))
                    normalise(xn, lambda t: x[s][:, t, :], 1, xn_ready)

                first_norms(0, 0, 0)
                dve.wait_ge(own.sem, own.n)
                dve.sem_clear(own.sem)
                own.n = 0

                def body(b, s, i, last):
                    dve.wait_ge(h_made.sem, h_made.at(b, -1))
                    for k in range(KD):
                        dve.wait_ge(xh_ready.sem, xh_ready.at(b, k))
                        dve.tensor_tensor(xl[:, k, :], ps_x[k].ap(), xh[:, k, :].bitcast(F32), ALU.subtract).then_inc(xl_ready.sem, xl_ready.step)
                    dve.wait_ge(o2_made.sem, o2_made.at(b, -1))
                    for f in range(KF):
                        dve.wait_ge(gh_ready.sem, gh_ready.at(b, f))
                        dve.tensor_tensor(gl[:, f, :], g[f % 2].ap(), gh[:, f, :].bitcast(F32), ALU.subtract).then_inc(gl_ready.sem, gl_ready.step)
                    if not last:
                        first_norms(b + 1, 1 - s, i + s)
                    dve.wait_ge(o2_made.sem, o2_made.at(b, 0))
                    for half_ in range(2):
                        ins = dve.tensor_tensor(o2[:, 2 * half_:2 * half_ + 2, :], ps_2[half_].ap(),
                                                b2.ap().unsqueeze(1).to_broadcast([P, 2, D]), ALU.add)
                        ins.then_inc(o2_ready.sem, o2_ready.step) if half_ else ins.then_inc(own.sem, own.one())
                    dve.wait_ge(own.sem, own.n)
                    dve.wait_ge(o2_ready.sem, o2_ready.at(b, 0))
                    moments(lambda t: o2[:, t, :], 2, var2_ready)
                    dve.wait_ge(sd2_ready.sem, sd2_ready.at(b, 0))
                    dve.reciprocal(rstd[2].ap(), sd[2].ap()).then_inc(own.sem, own.one())
                    dve.wait_ge(own.sem, own.n)
                    normalise(o2, lambda t: o2[:, t, :], 2)
                    dve.wait_ge(own.sem, own.n)
                    dve.wait_ge(res_stored.sem, res_stored.at(b, -1))
                    dve.tensor_tensor(res.ap(), x[s].ap(), o2.ap(), ALU.add).then_inc(res_ready.sem, res_ready.step)
                    dve.wait_ge(own.sem, own.n)
                    dve.sem_clear(own.sem)
                    own.n = 0
                rows(dve, body)


def build(nc, a, out):
    def scratch(name, *shape):
        return nc.dram_tensor("scratch_" + name, shape, F32, kind="Internal").ap()

    dram = {
        "n_alpha": scratch("n_alpha", B, H, T), "beta": scratch("beta", B, H, T), "dt": scratch("dt", B, H, T),
        "e_inv": scratch("e_inv", B, H, T), "e_end": scratch("e_end", B, H, TT),
        "valT": scratch("valT", B, P, KI, T), "gateT": scratch("gateT", B, P, KI, T),
        "svgT": scratch("svgT", B, P, KI, T), "u": scratch("u", B, P, TT, DI),
        "norm": scratch("norm", 2, P, T), "yT": scratch("yT", B, HG, HP * DH, T),
    }
    project(nc, a, dram)
    mix(nc, a, dram)
    ffn(nc, a, dram, out)


_OUTS = [((B, T, D), "float32")]


def kernel(L0_attn_x, L0_attn_W_in, L0_attn_dw_weight, L0_attn_dw_bias, L0_attn_W_bc, L0_attn_W_out, L0_attn_skip,
           L0_attn_A_log, L0_attn_dt_bias, L0_ffn_W1, L0_ffn_b1, L0_ffn_W2, L0_ffn_b2):
    import numpy as np
    import concourse.bacc as _bacc
    from concourse.bass_utils import run_bass_kernel_spmd as _run

    def tiles(v):
        v = np.asarray(v)
        return v.reshape(-1, P, *v.shape[1:]).swapaxes(0, 1)

    w_in = np.asarray(L0_attn_W_in)
    steps = w_in[2 * DI:].reshape(H, 2, D)
    w_bc = np.asarray(L0_attn_W_bc).reshape(HG, HP, NJ, N, KI, P)
    p = np.arange(P)
    arrays = {
        "x": L0_attn_x,
        "w_inT": np.concatenate([w_in[:2 * DI], steps[:, 0], steps[:, 1]]).T,
        "taps": tiles(L0_attn_dw_weight), "dw_bias": tiles(L0_attn_dw_bias), "skip": tiles(L0_attn_skip),
        "dt_bias": np.asarray(L0_attn_dt_bias).reshape(H, 1),
        "w_bcT": w_bc.transpose(0, 2, 5, 4, 1, 3).reshape(HG, NJ, P, KI * P),
        "a_log": np.asarray(L0_attn_A_log).reshape(HG, P).T,
        "w_outT": np.asarray(L0_attn_W_out).T,
        "w1T": np.asarray(L0_ffn_W1).T, "b1": tiles(L0_ffn_b1),
        "w2T": np.asarray(L0_ffn_W2).T, "b2": np.asarray(L0_ffn_b2).reshape(1, D),
        "ident": np.eye(P, dtype=np.float32),
        "head_sum": (p[:, None] // N == np.arange(N)[None]).astype(np.float32),
        "causal": (p[:, None] <= p[None]).astype(np.float32),
        "head_block": np.repeat((p[:, None] // N == np.arange(HP)[None]).astype(np.float32), DH, axis=1),
    }
    arrays = {k: np.ascontiguousarray(v) for k, v in arrays.items()}
    nc = _bacc.Bacc("TRN2", target_bir_lowering=False, num_devices=1)
    a = {k: nc.dram_tensor("in_" + k, v.shape, mybir.dt.from_np(v.dtype), kind="ExternalInput").ap()
         for k, v in arrays.items()}
    out = nc.dram_tensor("out_0", _OUTS[0][0], F32, kind="ExternalOutput").ap()
    build(nc, a, out)
    r = _run(nc, [{"in_" + k: v for k, v in arrays.items()}], core_ids=[0])
    return r.results[0]["out_0"]
```

```python
from contextlib import ExitStack

import concourse.bass as bass
from concourse import mybir

F32 = mybir.dt.float32
ALU = mybir.AluOpType
ACT = mybir.ActivationFunctionType
AX = mybir.AxisListType

P = 128
B, T, D = 8, 512, 256
TT = T // P
KD = D // P
DI = 512
KI = DI // P
H, N, DH = 32, 32, 16
HP = P // N
HG = H // HP
NJ = 4
TAPS = 4
FF = 1024
KF = FF // P
C = P
LN_EPS = 1e-5
NORM_EPS = 1e-8
DT_MIN, DT_MAX, K_MAX = 1e-4, 0.1, 0.5
SOFTPLUS_CAP = 10.0
TINY = 1e-12


class Signal:

    def __init__(self, ctx, nc, name, per, step=1, credited=True):
        self.sem, self.per, self.step = ctx.enter_context(nc.semaphore(name)), per, step
        self.given = per if credited else 0

    def at(self, b, item):
        return (b * self.per + self.given + item + 1) * self.step


class Own:

    def __init__(self, sem):
        self.sem, self.n = sem, 0

    def one(self):
        self.n += 1
        return 1


def project(nc, a, dram):
    with ExitStack() as ctx:
        def sb(name, shape):
            return ctx.enter_context(nc.sbuf_tensor(name, shape, F32))

        def sem(name):
            return ctx.enter_context(nc.semaphore(name))

        ident = sb("p_ident", [P, P])
        w_in = sb("w_in", [P, KD, 2 * DI + 2 * H])
        taps = sb("taps", [P, KI, TAPS])
        dw_bias = sb("dw_bias", [P, KI])
        skip = sb("skip", [P, KI])
        dt_bias = sb("dt_bias", [H, 1])
        x = sb("p_x", [P, TT, D])
        stats = sb("p_stats", [P, TT, 6])
        mv = sb("p_mv", [P, TT, 2])
        sd = sb("p_sd", [P, TT])
        rstd = sb("p_rstd", [P, TT])
        xn = sb("p_xn", [P, TT, D])
        xnT = sb("p_xnT", [P, KD, T])
        vraw = sb("vraw", [P, KI, T + TAPS - 1])
        conv = sb("conv", [P, KI, T])
        val = sb("val", [P, KI, T])
        gate = sb("gate", [P, KI, T])
        svg = sb("svg", [P, KI, T])
        u = sb("p_u", [P, TT, DI])
        z = sb("z", [H, T])
        ez = sb("ez", [H, T])
        ek = sb("ek", [H, T])
        lz = sb("lz", [H, T])
        w = sb("w", [H, T])
        dt = sb("dt", [H, T])
        kd = sb("kd", [H, T])
        zero = sb("zero", [H, T])
        E = sb("E", [H, TT, C + 1])
        e_inv = sb("e_inv", [H, TT, C])
        e_end = sb("e_end", [H, TT])
        n_alpha = sb("n_alpha", [H, T])
        beta = sb("beta", [H, T])
        eps = sb("p_eps", [P, 1])
        ps_x = [ctx.enter_context(nc.psum_tensor(f"ps_x{k}", [P, T], F32)) for k in range(KD)]
        ps_w = [ctx.enter_context(nc.psum_tensor(f"ps_w{k}", [P, T], F32)) for k in range(2)]
        ps_dt = ctx.enter_context(nc.psum_tensor("ps_dt", [P, T], F32))
        ps_k = ctx.enter_context(nc.psum_tensor("ps_k", [P, T], F32))
        ps_u = [ctx.enter_context(nc.psum_tensor(f"ps_u{k}", [P, T], F32)) for k in range(2)]

        def sig(name, per, step=1, credited=True):
            return Signal(ctx, nc, "p_" + name, per, step, credited)

        consts_in = sem("p_consts_in")
        const_set = sem("p_const_set")
        x_in = sig("x_in", 1, 16, credited=False)
        xn_ready = sig("xn_ready", TT)
        var_ready = sig("var_ready", 1)
        sd_ready = sig("sd_ready", 1)
        xT_made = sig("xT_made", 1)
        xnT_ready = sig("xnT_ready", KD)
        logit_made = sig("logit_made", 2)
        z_ready = sig("z_ready", 1)
        exps_ready = sig("exps_ready", 3)
        one_ez_ready = sig("one_ez_ready", 1)
        tile_made = sig("tile_made", 2 * KI)
        vraw_ready = sig("vraw_ready", KI)
        gate_ready = sig("gate_ready", KI)
        conv_ready = sig("conv_ready", KI)
        val_ready = sig("val_ready", KI)
        svg_ready = sig("svg_ready", KI)
        steps_ready = sig("steps_ready", 1)
        u_made = sig("u_made", TT)
        u_ready = sig("u_ready", TT)
        steps_stored = sig("steps_stored", 5, 16)
        val_stored = sig("val_stored", 1, 16)
        gate_stored = sig("gate_stored", 1, 16)
        svg_stored = sig("svg_stored", 1, 16)
        u_stored = sig("u_stored", 1, 16)
        own_dve = sem("p_own_dve")

        with nc.Block() as block:
            @block.sync
            def _(sp):
                for dst, src in ((ident, a["ident"]), (taps, a["taps"]), (dw_bias, a["dw_bias"]),
                                 (skip, a["skip"]), (dt_bias, a["dt_bias"])):
                    sp.dma_start(dst.ap(), src).then_inc(consts_in, 16)
                sp.dma_start(w_in.ap(), a["w_inT"].rearrange("(k p) o -> p k o", p=P)).then_inc(consts_in, 16)
                for s in (steps_stored, val_stored, gate_stored, svg_stored, u_stored):
                    sp.sem_inc(s.sem, s.given * s.step)
                with sp.Fori(0, B) as b:
                    sp.wait_ge(steps_ready.sem, steps_ready.at(b, 0))
                    for name, src in (("n_alpha", n_alpha.ap()), ("beta", beta.ap()), ("dt", dt.ap()),
                                      ("e_inv", e_inv.ap().rearrange("h c t -> h (c t)")), ("e_end", e_end.ap())):
                        sp.dma_start(dram[name][b], src).then_inc(steps_stored.sem, steps_stored.step)
                    sp.wait_ge(gate_ready.sem, gate_ready.at(b, KI - 1))
                    sp.dma_start(dram["gateT"][b], gate.ap()).then_inc(gate_stored.sem, gate_stored.step)
                    sp.wait_ge(val_ready.sem, val_ready.at(b, KI - 1))
                    sp.dma_start(dram["valT"][b], val.ap()).then_inc(val_stored.sem, val_stored.step)
                    sp.wait_ge(svg_ready.sem, svg_ready.at(b, KI - 1))
                    sp.dma_start(dram["svgT"][b], svg.ap()).then_inc(svg_stored.sem, svg_stored.step)
                    sp.wait_ge(u_ready.sem, u_ready.at(b, TT - 1))
                    sp.dma_start(dram["u"][b], u.ap()).then_inc(u_stored.sem, u_stored.step)
                for s in (steps_stored, val_stored, gate_stored, svg_stored, u_stored):
                    sp.wait_ge(s.sem, s.at(B - 1, s.per - 1))

            @block.gpsimd
            def _(pool):
                with pool.Fori(0, B) as b:
                    pool.wait_ge(xn_ready.sem, xn_ready.at(b, -1))
                    pool.dma_start(x.ap(), a["x"][b].rearrange("(t p) d -> p t d", p=P)).then_inc(x_in.sem, x_in.step)

            @block.tensor
            def _(pe):
                for s in (xT_made, logit_made, tile_made, u_made):
                    pe.sem_inc(s.sem, s.given * s.step)
                pe.wait_ge(consts_in, 96)
                with pe.Fori(0, B) as b:
                    pe.wait_ge(xn_ready.sem, xn_ready.at(b, TT - 1))
                    pe.wait_ge(xnT_ready.sem, xnT_ready.at(b, -1))
                    for k in range(KD):
                        for t in range(TT):
                            mm = pe.transpose(ps_x[k][:, t * P:(t + 1) * P], xn[:, t, k * P:(k + 1) * P], ident.ap())
                    mm.then_inc(xT_made.sem, xT_made.step)
                    pe.wait_ge(xnT_ready.sem, xnT_ready.at(b, KD - 1))
                    pe.wait_ge(z_ready.sem, z_ready.at(b, -1))
                    pe.wait_ge(exps_ready.sem, exps_ready.at(b, -1))
                    for ps, col in ((ps_dt, 2 * DI), (ps_k, 2 * DI + H)):
                        for k in range(KD):
                            mm = pe.matmul(ps[0:H, :], w_in[:, k, col:col + H], xnT[:, k, :],
                                           start=(k == 0), stop=(k == KD - 1))
                        mm.then_inc(logit_made.sem, logit_made.step)
                    for i in range(2 * KI):
                        if i < 2:
                            pe.wait_ge(gate_ready.sem, gate_ready.at(b, KI * 0 - 2 + i))
                        elif i < KI + 2:
                            pe.wait_ge(vraw_ready.sem, vraw_ready.at(b, i - 2))
                        else:
                            pe.wait_ge(gate_ready.sem, gate_ready.at(b, i - 2 - KI))
                        col = (DI + i * P) if i < KI else (i - KI) * P
                        for k in range(KD):
                            mm = pe.matmul(ps_w[i % 2].ap(), w_in[:, k, col:col + P], xnT[:, k, :],
                                           start=(k == 0), stop=(k == KD - 1))
                        mm.then_inc(tile_made.sem, tile_made.step)
                    pe.wait_ge(val_ready.sem, val_ready.at(b, KI - 1))
                    for t in range(TT):
                        pe.wait_ge(u_ready.sem, u_ready.at(b, t - 2))
                        for k in range(KI):
                            mm = pe.transpose(ps_u[t % 2][:, k * P:(k + 1) * P], val[:, k, t * P:(t + 1) * P], ident.ap())
                        mm.then_inc(u_made.sem, u_made.step)

            @block.scalar
            def _(act):
                for s in (sd_ready, xnT_ready, exps_ready, vraw_ready, gate_ready, val_ready, u_ready):
                    act.sem_inc(s.sem, s.given * s.step)
                act.wait_ge(consts_in, 96)
                act.wait_ge(const_set, 4)
                with act.Fori(0, B) as b:
                    act.wait_ge(var_ready.sem, var_ready.at(b, 0))
                    act.wait_ge(sd_ready.sem, sd_ready.at(b, -1))
                    act.activation(sd.ap(), mv[:, :, 1], ACT.Sqrt, bias=eps.ap()).then_inc(sd_ready.sem, sd_ready.step)
                    act.wait_ge(xT_made.sem, xT_made.at(b, 0))
                    act.wait_ge(tile_made.sem, tile_made.at(b, -1))
                    for k in range(KD):
                        act.activation(xnT[:, k, :], ps_x[k].ap(), ACT.Copy).then_inc(xnT_ready.sem, xnT_ready.step)
                    act.wait_ge(z_ready.sem, z_ready.at(b, 0))
                    act.activation(ez.ap(), z.ap(), ACT.Exp).then_inc(exps_ready.sem, exps_ready.step)
                    act.wait_ge(logit_made.sem, logit_made.at(b, 1))
                    act.wait_ge(steps_ready.sem, steps_ready.at(b, -1))
                    act.activation(ek.ap(), ps_k[0:H, :], ACT.Exp, scale=-1.0).then_inc(exps_ready.sem, exps_ready.step)
                    act.wait_ge(one_ez_ready.sem, one_ez_ready.at(b, 0))
                    act.activation(lz.ap(), w.ap(), ACT.Ln).then_inc(exps_ready.sem, exps_ready.step)
                    for i in range(KI):
                        act.wait_ge(tile_made.sem, tile_made.at(b, i))
                        act.wait_ge(conv_ready.sem, conv_ready.at(b, -1))
                        act.activation(vraw[:, i, TAPS - 1:], ps_w[i % 2].ap(), ACT.Copy).then_inc(vraw_ready.sem, vraw_ready.step)
                    act.wait_ge(gate_stored.sem, gate_stored.at(b, -1))
                    act.wait_ge(svg_ready.sem, svg_ready.at(b, -1))
                    for i in range(KI):
                        act.wait_ge(tile_made.sem, tile_made.at(b, KI + i))
                        act.activation(gate[:, i, :], ps_w[i % 2].ap(), ACT.Silu).then_inc(gate_ready.sem, gate_ready.step)
                    act.wait_ge(val_stored.sem, val_stored.at(b, -1))
                    act.wait_ge(u_made.sem, u_made.at(b, -1))
                    for i in range(KI):
                        act.wait_ge(conv_ready.sem, conv_ready.at(b, i))
                        act.activation(val[:, i, :], conv[:, i, :], ACT.Silu).then_inc(val_ready.sem, val_ready.step)
                    act.wait_ge(u_stored.sem, u_stored.at(b, -1))
                    for t in range(TT):
                        act.wait_ge(u_made.sem, u_made.at(b, t))
                        act.activation(u[:, t, :], ps_u[t % 2].ap(), ACT.Copy).then_inc(u_ready.sem, u_ready.step)

            @block.vector
            def _(dve):
                for s in (var_ready, xn_ready, z_ready, one_ez_ready, steps_ready, conv_ready, svg_ready):
                    dve.sem_inc(s.sem, s.given * s.step)
                dve.memset(vraw.ap(), 0.0).then_inc(const_set, 1)
                dve.memset(zero.ap(), 0.0).then_inc(const_set, 1)
                dve.memset(E.ap(), 1.0).then_inc(const_set, 1)
                dve.memset(eps.ap(), LN_EPS).then_inc(const_set, 1)
                dve.wait_ge(consts_in, 96)
                dve.wait_ge(const_set, 4)
                own = Own(own_dve)
                with dve.Fori(0, B) as b:
                    dve.wait_ge(x_in.sem, x_in.at(b, 0))
                    dve.wait_ge(sd_ready.sem, sd_ready.at(b, -1))
                    for t in range(TT):
                        dve.bn_stats(stats[:, t, :], x[:, t, :]).then_inc(own.sem, own.one())
                    dve.wait_ge(own.sem, own.n)
                    for t in range(TT):
                        ins = dve.bn_aggr(mv[:, t, :], stats[:, t, :])
                        if t < TT - 1:
                            ins.then_inc(own.sem, own.one())
                    ins.then_inc(var_ready.sem, var_ready.step)
                    dve.wait_ge(sd_ready.sem, sd_ready.at(b, 0))
                    dve.reciprocal(rstd.ap(), sd.ap()).then_inc(own.sem, own.one())
                    dve.wait_ge(own.sem, own.n)
                    dve.wait_ge(xT_made.sem, xT_made.at(b, -1))
                    for t in range(TT):
                        dve.tensor_scalar(xn[:, t, :], x[:, t, :], mv[:, t, 0:1], rstd[:, t:t + 1],
                                                      ALU.subtract, ALU.mult).then_inc(xn_ready.sem, xn_ready.step)
                    dve.wait_ge(logit_made.sem, logit_made.at(b, 0))
                    dve.tensor_scalar(z.ap(), ps_dt[0:H, :], dt_bias.ap(), SOFTPLUS_CAP, ALU.add, ALU.min).then_inc(z_ready.sem, z_ready.step)
                    dve.wait_ge(exps_ready.sem, exps_ready.at(b, 0))
                    dve.tensor_scalar(w.ap(), ez.ap(), 1.0, None, ALU.add).then_inc(one_ez_ready.sem, one_ez_ready.step)
                    dve.wait_ge(one_ez_ready.sem, one_ez_ready.at(b, 0))
                    dve.wait_ge(steps_stored.sem, steps_stored.at(b, -1))
                    dve.tensor_scalar(kd.ap(), w.ap(), 1.0, TINY, ALU.subtract, ALU.max).then_inc(own.sem, own.one())
                    dve.wait_ge(own.sem, own.n)
                    dve.reciprocal(dt.ap(), kd.ap()).then_inc(own.sem, own.one())
                    dve.wait_ge(own.sem, own.n)
                    dve.tensor_tensor(dt.ap(), dt.ap(), ez.ap(), ALU.mult).then_inc(own.sem, own.one())
                    dve.wait_ge(exps_ready.sem, exps_ready.at(b, 2))
                    dve.wait_ge(own.sem, own.n)
                    dve.tensor_tensor(dt.ap(), dt.ap(), lz.ap(), ALU.mult).then_inc(own.sem, own.one())
                    dve.wait_ge(own.sem, own.n)
                    dve.tensor_scalar(dt.ap(), dt.ap(), DT_MIN, DT_MAX, ALU.max, ALU.min).then_inc(own.sem, own.one())
                    dve.tensor_scalar(kd.ap(), ek.ap(), 1.0, 1.0 / K_MAX, ALU.add, ALU.mult).then_inc(own.sem, own.one())
                    dve.wait_ge(own.sem, own.n)
                    dve.reciprocal(kd.ap(), kd.ap()).then_inc(own.sem, own.one())
                    dve.wait_ge(own.sem, own.n)
                    dve.tensor_tensor(kd.ap(), kd.ap(), dt.ap(), ALU.mult).then_inc(own.sem, own.one())
                    dve.wait_ge(own.sem, own.n)
                    dve.tensor_scalar(kd.ap(), kd.ap(), 1.0, None, ALU.add).then_inc(own.sem, own.one())
                    dve.wait_ge(own.sem, own.n)
                    for c in range(TT):
                        dve.tensor_tensor_scan(E[:, c, 1:], kd[:, c * C:(c + 1) * C], zero[:, 0:C], 1.0,
                                                   ALU.mult, ALU.add).then_inc(own.sem, own.one())
                    dve.wait_ge(own.sem, own.n)
                    dve.reciprocal(e_inv.ap(), E[:, :, 1:]).then_inc(own.sem, own.one())
                    dt4, na4, be4 = (v.ap().rearrange("h (c t) -> h c t", c=TT) for v in (dt, n_alpha, beta))
                    dve.tensor_tensor(be4, dt4, E[:, :, 0:C], ALU.mult).then_inc(own.sem, own.one())
                    dve.wait_ge(own.sem, own.n)
                    dve.tensor_copy(e_end.ap(), e_inv[:, :, C - 1]).then_inc(own.sem, own.one())
                    dve.scalar_tensor_tensor(out=na4, in0=dt4, scalar=-1.0, in1=e_inv.ap(), op0=ALU.mult, op1=ALU.mult).then_inc(own.sem, own.one())
                    dve.wait_ge(own.sem, own.n)
                    dve.tensor_copy(z[:, 0:1], e_end[:, 0:1]).then_inc(steps_ready.sem, steps_ready.step)
                    dve.wait_ge(vraw_ready.sem, vraw_ready.at(b, KI - 1))
                    dve.wait_ge(val_ready.sem, val_ready.at(b, -1))
                    for k in range(TAPS):
                        for i in range(KI):
                            src = vraw[:, i, k:k + T]
                            if k == 0:
                                dve.tensor_scalar(conv[:, i, :], src, taps[:, i, 0:1], dw_bias[:, i:i + 1],
                                                      ALU.mult, ALU.add).then_inc(own.sem, own.one())
                            else:
                                ins = dve.scalar_tensor_tensor(out=conv[:, i, :], in0=src, scalar=taps[:, i, k:k + 1],
                                                               in1=conv[:, i, :], op0=ALU.mult, op1=ALU.add)
                                ins.then_inc(conv_ready.sem, conv_ready.step) if k == TAPS - 1 else ins.then_inc(own.sem, own.one())
                            if k < TAPS - 1 and i == KI - 1:
                                dve.wait_ge(own.sem, own.n)
                    dve.wait_ge(svg_stored.sem, svg_stored.at(b, -1))
                    dve.wait_ge(gate_ready.sem, gate_ready.at(b, KI - 1))
                    for i in range(KI):
                        dve.wait_ge(val_ready.sem, val_ready.at(b, i))
                        dve.scalar_tensor_tensor(out=svg[:, i, :], in0=val[:, i, :], scalar=skip[:, i:i + 1],
                                                              in1=gate[:, i, :], op0=ALU.mult, op1=ALU.mult).then_inc(svg_ready.sem, svg_ready.step)
                    dve.wait_ge(own.sem, own.n)
                    dve.sem_clear(own.sem)
                    own.n = 0


def mix(nc, a, dram):
    LAST = HG - 1
    HALF = HG // 2
    SEG = NJ * HP * T // P
    STEPS = (36, 36, 36, 20)
    assert sum(STEPS) == C
    with ExitStack() as ctx:
        def sb(name, shape):
            return ctx.enter_context(nc.sbuf_tensor("m_" + name, shape, F32))

        def ps(name):
            return ctx.enter_context(nc.psum_tensor("m_ps_" + name, [P, T], F32))

        def sem(name):
            return ctx.enter_context(nc.semaphore("m_" + name))

        def sig(name, per, step=1, credited=True):
            return Signal(ctx, nc, "m_" + name, per, step, credited)

        ident = sb("ident", [P, P])
        head_sum = sb("head_sum", [P, N])
        causal = sb("causal", [P, C])
        head_block = sb("head_block", [P, HP, DH])
        carry = sb("carry", [P, TT, C])
        A = sb("A", [P, HG])
        one = sb("one", [P, 1])
        psi = sb("psi", [P, 2, 2, HG, TT, C + 1])
        shear = sb("shear", [P, 2, HG, T])
        prod = sb("prod", [P, 2, 2, HALF * TT])
        e_end = sb("e_end", [P, HG, TT])
        w_bc = sb("w_bc", [P, NJ, KI, P])
        valT = sb("valT", [P, KI, T])
        u = sb("u", [P, 2, TT, HP * DH])
        raw = [sb(f"raw{s}", [P, NJ, T]) for s in range(2)]
        sq = sb("sq", [P, 2, T])
        scale = sb("scale", [P, NJ, T])
        rows_ = sb("rows", [P, T])
        compact = sb("compact", [P, SEG])
        factor = sb("factor", [P, SEG])
        k = [sb(f"k{s}", [P, 2, T]) for s in range(2)]
        q = [sb(f"q{s}", [P, 2, T]) for s in range(2)]
        k_head = sb("k_head", [P, HP, 2, T])
        kx = sb("kx", [P, 2, T])
        qx = sb("qx", [P, 2, T])
        g = sb("g", [P, HP, T])
        kT = sb("kT", [P, 2, (TT - 1) * P])
        dX = sb("dX", [P, TT - 1, 2, DH])
        X = sb("X", [P, TT - 1, 2, DH])
        tmp = sb("tmp", [P, 2, DH])
        Xb = sb("Xb", [P, TT - 1, 2, HP, N])
        end = sb("end", [P, TT])
        coef = sb("coef", [P, 2, 2, TT])
        y = sb("y", [P, T])
        ps_a = [ps(f"a{n}") for n in range(2)]
        ps_s = ps("s")
        ps_g = [ps(f"g{n}") for n in range(2)]
        ps_k = [ps(f"k{n}") for n in range(2)]
        ps_y = ps("y")
        KW = (TT - 1) * P
        ps_dX = ps_k[0][:, KW:KW + (TT - 1) * 2 * DH]

        consts_in = sem("consts_in")
        const_set = sem("const_set")
        w_in = [sig(f"w_in{j}", HG, 16) for j in range(NJ)]
        val_in = sig("val_in", 1, 16)
        u_in = [sig(f"u_in{s}", HG // 2, 16) for s in range(2)]
        n_alpha_in = [sig(f"n_alpha_in{n}", HP, 16) for n in range(2)]
        beta_in = [sig(f"beta_in{n}", HP, 16) for n in range(HG)]
        e_end_in = sig("e_end_in", HP, 16)
        factor_in = sig("factor_in", 3 * HG, 16)
        beta_scaled = sig("beta_scaled", HG)
        stepped = sig("stepped", 2)
        ab_ready = sig("ab_ready", HG)
        log_ready = sig("log_ready", HG)
        sum_ready = sig("sum_ready", HG)
        det_ready = sig("det_ready", HG)
        a_made = sig("a_made", HG * NJ)
        raw_ready = sig("raw_ready", HG * NJ)
        sq_ready = sig("sq_ready", HG * NJ)
        sums_made = sig("sums_made", HG * NJ)
        norm_ready = sig("norm_ready", HG)
        rows_ready = sig("rows_ready", HG)
        compact_in = sig("compact_in", HG * NJ, 16)
        rows_stored = sig("rows_stored", HG, 16)
        scale_in = sig("scale_in", HG * HP, 16)
        b_scaled = sig("b_scaled", HG)
        c_scaled = sig("c_scaled", HG)
        kx_ready = sig("kx_ready", HG)
        qx_ready = sig("qx_ready", HG)
        raw_used = sig("raw_used", HG)
        k_ready = sig("k_ready", HG)
        k_head_ready = sig("k_head_ready", HG * HP)
        q_ready = sig("q_ready", HG)
        g_made = sig("g_made", HG * HP)
        g_ready = sig("g_ready", HG * HP)
        kT_made = sig("kT_made", HG * 2)
        kT_ready = sig("kT_ready", HG * 2)
        dX_made = sig("dX_made", HG)
        dX_ready = sig("dX_ready", HG)
        coef_ready = sig("coef_ready", HG)
        X_ready = sig("X_ready", HG * (TT - 1))
        Xb_ready = sig("Xb_ready", HG * (TT - 1))
        y_made = sig("y_made", HG)
        y_ready = sig("y_ready", HG)
        y_stored = sig("y_stored", HG * HP, 16)
        steps_dve, own_dve, own_pool = sem("steps_dve"), sem("own_dve"), sem("own_pool")

        def over_rows(eng, body):
            with eng.Fori(0, B - 1) as b:
                body(b, False)
            body(B - 1, True)

        def chunks(v):
            return v.rearrange("p (c t) -> p c t", c=TT)

        def spread(src, parts=N):
            return src.unsqueeze(0).to_broadcast([parts, *src.shape])

        with nc.Block() as block:
            @block.sync
            def _(sp):
                for dst, name in ((ident, "ident"), (head_sum, "head_sum"), (causal, "causal"), (A, "a_log")):
                    sp.dma_start(dst.ap(), a[name]).then_inc(consts_in, 16)
                sp.dma_start(head_block.ap().rearrange("p h d -> p (h d)"), a["head_block"]).then_inc(consts_in, 16)
                for s in (*w_in, val_in, *u_in, *n_alpha_in, *beta_in, e_end_in, factor_in, compact_in, rows_stored,
                          scale_in):
                    sp.sem_inc(s.sem, s.given * s.step)

                def heads(name, b, h, groups):
                    return dram[name][b].rearrange("(g h) t -> h g t", h=HP)[h, groups]

                def load_w(group, j):
                    sp.dma_start(w_bc[:, j, :, :].rearrange("p k m -> p (k m)"), a["w_bcT"][group, j]).then_inc(w_in[j].sem, w_in[j].step)

                def load_u(b, group):
                    heads_of_group = slice(group * HP * DH, (group + 1) * HP * DH)
                    sp.dma_start(u[:, group % 2], dram["u"][b][:, :, heads_of_group]
                                 ).then_inc(u_in[group % 2].sem, u_in[group % 2].step)

                def load_n_alpha(b, half):
                    groups = slice(half * HALF, (half + 1) * HALF)
                    for h in range(HP):
                        sp.dma_start(shear[h * N:(h + 1) * N, 1, groups, :],
                                     spread(heads("n_alpha", b, h, groups))).then_inc(n_alpha_in[half].sem, n_alpha_in[half].step)

                def load_beta(b, group):
                    for h in range(HP):
                        sp.dma_start(shear[h * N:(h + 1) * N, 0, group, :],
                                                           spread(dram["beta"][b, group * HP + h])).then_inc(beta_in[group].sem, beta_in[group].step)

                def load_e_end(b):
                    for h in range(HP):
                        sp.dma_start(e_end[h * N:(h + 1) * N, :, :], spread(heads("e_end", b, h, slice(0, HG)))).then_inc(e_end_in.sem, e_end_in.step)

                def load_factor(b, group):
                    for j, name in enumerate(("beta", "dt", "e_inv")):
                        src = dram[name][b, group * HP:(group + 1) * HP, :].rearrange("h (s t) -> (h s) t", t=SEG)
                        sp.dma_start(factor[j * N:(j + 1) * N, :], src).then_inc(factor_in.sem, factor_in.step)

                def compact_norms(b, group):
                    sp.wait_ge(norm_ready.sem, norm_ready.at(b, group))
                    for j in range(NJ):
                        sp.dma_start(compact[j * N:(j + 1) * N, :],
                                     rows_[j * N:j * N + HP, :].rearrange("h (s t) -> h s t", t=SEG)
                                     ).then_inc(compact_in.sem, compact_in.step)

                def spread_scales(b, group, u_):
                    sp.wait_ge(rows_ready.sem, rows_ready.at(b, group))
                    sp.dma_start(dram["norm"][u_].rearrange("r (s t) -> (r s) t", t=SEG),
                                 compact.ap()).then_inc(rows_stored.sem, rows_stored.step)
                    sp.wait_ge(rows_stored.sem, rows_stored.at(b, group))
                    sp.wait_ge(b_scaled.sem, b_scaled.at(b, group - 1))
                    sp.wait_ge(c_scaled.sem, c_scaled.at(b, group - 1))
                    for h in range(HP):
                        src = dram["norm"][u_].rearrange("(j h) t -> h j t", h=HP)[h]
                        sp.dma_start(scale[h * N:(h + 1) * N, :, :], spread(src)).then_inc(scale_in.sem, scale_in.step)

                for j in range(NJ):
                    load_w(0, j)
                sp.dma_start(valT.ap(), dram["valT"][0]).then_inc(val_in.sem, val_in.step)
                for half in range(2):
                    load_n_alpha(0, half)
                for group in range(HG):
                    load_beta(0, group)
                load_e_end(0)
                sp.wait_ge(const_set, 6)
                load_factor(0, 0)
                for j in range(NJ):
                    sp.wait_ge(a_made.sem, a_made.at(0, j))
                    load_w(1, j)
                load_u(0, 0)
                compact_norms(0, 0)
                spread_scales(0, 0, 0)

                def body(b, last):
                    for group in range(HG):
                        ahead = not (last and group == LAST)
                        if ahead:
                            nb, ng = (b, group + 1) if group < LAST else (b + 1, 0)
                            sp.wait_ge(y_made.sem, y_made.at(b, group - 1))
                            load_u(nb, ng)
                            sp.wait_ge(rows_ready.sem, rows_ready.at(b, group))
                            load_factor(nb, ng)
                        if not last:
                            if group % HALF == 0:
                                half = group // HALF
                                sp.wait_ge(ab_ready.sem, ab_ready.at(b, half * HALF + HALF - 1))
                                load_n_alpha(b + 1, half)
                            if group == LAST - 1:
                                sp.wait_ge(a_made.sem, a_made.at(b, HG * NJ - 1))
                                sp.dma_start(valT.ap(), dram["valT"][b + 1]).then_inc(val_in.sem, val_in.step)
                            sp.wait_ge(c_scaled.sem, c_scaled.at(b, group))
                            sp.wait_ge(coef_ready.sem, coef_ready.at(b, group))
                            load_beta(b + 1, group)
                        if not (last and group >= LAST - 1):
                            for j in range(NJ):
                                sp.wait_ge(a_made.sem, a_made.at(b, (group + 1) * NJ + j))
                                load_w((group + 2) % HG, j)
                        if ahead:
                            compact_norms(b, group + 1)
                            spread_scales(b, group + 1, (group + 1) % 2)
                    if not last:
                        load_e_end(b + 1)
                over_rows(sp, body)

            @block.gpsimd
            def _(pool):
                for s in (ab_ready, c_scaled, kx_ready, qx_ready, Xb_ready):
                    pool.sem_inc(s.sem, s.given * s.step)
                own = Own(own_pool)
                pool.wait_ge(consts_in, 80)
                pool.wait_ge(const_set, 6)

                def det_steps(b, half):
                    pool.wait_ge(stepped.sem, stepped.at(b, half))
                    for group in range(half * HALF, (half + 1) * HALF):
                        pool.tensor_tensor(shear[:, 0, group, :], shear[:, 0, group, :],
                                                       shear[:, 1, group, :], ALU.mult).then_inc(ab_ready.sem, ab_ready.step)

                det_steps(0, 0)

                def body(b, last):
                    for group in range(HG):
                        s = group % 2
                        r4 = raw[s]
                        pool.wait_ge(scale_in.sem, scale_in.at(b, (group + 1) * HP - 1))
                        pool.wait_ge(raw_ready.sem, raw_ready.at(b, group * NJ + 3))
                        pool.tensor_tensor(r4[:, 2:4, :], r4[:, 2:4, :], scale[:, 2:4, :], ALU.mult).then_inc(own.sem, own.one())
                        pool.wait_ge(det_ready.sem, det_ready.at(b, group))
                        pool.wait_ge(own.sem, own.n)
                        pool.tensor_tensor(
                            r4[:, 2:4, :], r4[:, 2:4, :],
                            shear[:, 0, group, :].unsqueeze(1).to_broadcast([P, 2, T]), ALU.mult).then_inc(c_scaled.sem, c_scaled.step)

                        pool.wait_ge(b_scaled.sem, b_scaled.at(b, group))
                        pool.wait_ge(k_ready.sem, k_ready.at(b, group - 1))
                        for row in range(2):
                            ins = pool.tensor_tensor(chunks(kx[:, row, :]), chunks(r4[:, 1, :]),
                                                     psi[:, row, 1, group, :, 1:], ALU.mult)
                            ins.then_inc(own.sem, own.one()) if row == 0 else ins.then_inc(kx_ready.sem, kx_ready.step)
                        pool.wait_ge(c_scaled.sem, c_scaled.at(b, group))
                        pool.wait_ge(q_ready.sem, q_ready.at(b, group - 1))
                        for row in range(2):
                            ins = pool.tensor_tensor(chunks(qx[:, row, :]), chunks(r4[:, 3, :]),
                                                     psi[:, row, 0, group, :, 1:], ALU.mult)
                            ins.then_inc(own.sem, own.one()) if row == 0 else ins.then_inc(qx_ready.sem, qx_ready.step)
                        if group == HALF - 1:
                            det_steps(b, 1)
                        if group == LAST and not last:
                            det_steps(b + 1, 0)
                        for c in range(TT - 1):
                            pool.wait_ge(X_ready.sem, X_ready.at(b, group * (TT - 1) + c))
                            pool.wait_ge(y_made.sem, y_made.at(b, group - 1))
                            for part in range(2):
                                ins = pool.tensor_tensor(
                                    Xb[:, c, part, :, 0:DH], X[:, c, part, :].unsqueeze(1).to_broadcast([P, HP, DH]),
                                    head_block.ap(), ALU.mult)
                                ins.then_inc(own.sem, own.one()) if part == 0 else ins.then_inc(Xb_ready.sem, Xb_ready.step)
                    pool.wait_ge(own.sem, own.n)
                    pool.sem_clear(own.sem)
                    own.n = 0
                over_rows(pool, body)

            @block.tensor
            def _(pe):
                for s in (a_made, sums_made, g_made, kT_made, dX_made, y_made):
                    pe.sem_inc(s.sem, s.given * s.step)
                pe.wait_ge(consts_in, 80)
                pe.wait_ge(const_set, 6)

                def products(b, group):
                    for j in range(NJ):
                        pe.wait_ge(w_in[j].sem, w_in[j].at(b, group))
                        if group % HG == 0 and j == 0:
                            pe.wait_ge(val_in.sem, val_in.at(b, group // HG))
                        pe.wait_ge(sq_ready.sem, sq_ready.at(b, group * NJ + j - 2))
                        for kt in range(KI):
                            mm = pe.matmul(ps_a[j % 2].ap(), w_bc[:, j, kt, :], valT[:, kt, :],
                                           start=(kt == 0), stop=(kt == KI - 1))
                        mm.then_inc(a_made.sem, a_made.step)
                        if j:
                            sum_squares(b, group, j - 1)
                    sum_squares(b, group, NJ - 1)

                def sum_squares(b, group, j):
                    pe.wait_ge(sq_ready.sem, sq_ready.at(b, group * NJ + j))
                    pe.wait_ge(norm_ready.sem, norm_ready.at(b, group - 1))
                    pe.matmul(ps_s[j * N:(j + 1) * N, :], head_sum.ap(), sq[:, j % 2, :],
                              start=True, stop=True, skip_group_check=True).then_inc(sums_made.sem, sums_made.step)

                def scores(b, group, h, s):
                    pe.wait_ge(g_ready.sem, g_ready.at(b, group * HP + h - 2))
                    pe.wait_ge(k_head_ready.sem, k_head_ready.at(b, group * HP + h))
                    for c in range(TT):
                        cols = slice(c * C, (c + 1) * C)
                        for part in range(2):
                            mm = pe.matmul(ps_g[h % 2][:, cols], k_head[:, h, part, cols], q[s][:, part, cols],
                                           start=(part == 0), stop=(part == 1), skip_group_check=True)
                    mm.then_inc(g_made.sem, g_made.step)

                products(0, 0)

                def body(b, last):
                    for group in range(HG):
                        s = group % 2
                        if not (last and group == LAST):
                            products(b, group + 1)
                        pe.wait_ge(k_ready.sem, k_ready.at(b, group))
                        pe.wait_ge(kT_ready.sem, kT_ready.at(b, group * 2 - 1))
                        pe.wait_ge(dX_ready.sem, dX_ready.at(b, group - 1))
                        for part in range(2):
                            for c in range(TT - 1):
                                mm = pe.transpose(ps_k[part][:, c * P:(c + 1) * P],
                                                  k[s][:, part, c * C:(c + 1) * C], ident.ap())
                            mm.then_inc(kT_made.sem, kT_made.step)
                        pe.wait_ge(q_ready.sem, q_ready.at(b, group))
                        for h in range(2):
                            scores(b, group, h, s)
                        pe.wait_ge(kT_ready.sem, kT_ready.at(b, group * 2 + 1))
                        pe.wait_ge(u_in[s].sem, u_in[s].at(b, group // 2))
                        for c in range(TT - 1):
                            for part in range(2):
                                for h in range(HP):
                                    ch = h * DH
                                    col = KW + (c * 2 + part) * DH
                                    mm = pe.matmul(ps_k[0][h * N:(h + 1) * N, col:col + DH],
                                                   kT[:, part, c * P + h * N:c * P + (h + 1) * N],
                                                   u[:, s, c, ch:ch + DH], start=True, stop=True, skip_group_check=True)
                        mm.then_inc(dX_made.sem, dX_made.step)
                        for h in range(2, HP):
                            scores(b, group, h, s)
                        pe.wait_ge(g_ready.sem, g_ready.at(b, group * HP + HP - 1))
                        pe.wait_ge(y_ready.sem, y_ready.at(b, group - 1))
                        for c in range(TT):
                            cols = slice(c * C, (c + 1) * C)
                            for h in range(HP):
                                ch = h * DH
                                pe.matmul(ps_y[h * N:h * N + DH, cols], u[:, s, c, ch:ch + DH], g[:, h, cols],
                                          start=(c == 0), stop=False, skip_group_check=True)
                        for c in range(1, TT):
                            cols = slice(c * C, (c + 1) * C)
                            pe.wait_ge(Xb_ready.sem, Xb_ready.at(b, group * (TT - 1) + c - 1))
                            for part in range(2):
                                mm = pe.matmul(ps_y[:, cols], Xb[:, c - 1, part, :, :].rearrange("p h d -> p (h d)"),
                                               q[s][:, part, cols], start=False, stop=(part == 1),
                                               skip_group_check=True)
                        mm.then_inc(y_made.sem, y_made.step)
                over_rows(pe, body)

            @block.scalar
            def _(act):
                for s in (beta_scaled, log_ready, det_ready, raw_ready, sq_ready, norm_ready, kT_ready, y_ready,
                          y_stored, k_head_ready):
                    act.sem_inc(s.sem, s.given * s.step)
                act.wait_ge(consts_in, 80)
                act.wait_ge(const_set, 6)
                own_a = sem("own_act")
                act.activation(A.ap(), A.ap(), ACT.Exp).then_inc(own_a, 1)
                act.wait_ge(own_a, 1)

                def scale_beta(b, group):
                    act.wait_ge(beta_in[group].sem, beta_in[group].at(b, HP - 1))
                    act.activation(shear[:, 0, group, :], shear[:, 0, group, :], ACT.Copy,
                                                  scale=A[:, group:group + 1]).then_inc(beta_scaled.sem, beta_scaled.step)

                HEADS_AFTER = ((), (0,), (1, 2), (3,))

                def split_head(b, group, h):
                    if h == 0:
                        act.wait_ge(k_ready.sem, k_ready.at(b, group))
                    act.wait_ge(g_made.sem, g_made.at(b, (group - 1) * HP + h))
                    rows = slice(h * N, (h + 1) * N)
                    act.activation(k_head[rows, h], k[group % 2][rows], ACT.Copy).then_inc(k_head_ready.sem, k_head_ready.step)

                def evacuate(b, group, s, heads_of=None):
                    act.wait_ge(raw_used.sem, raw_used.at(b, group - 2))
                    act.wait_ge(kx_ready.sem, kx_ready.at(b, group - 2))
                    act.wait_ge(qx_ready.sem, qx_ready.at(b, group - 2))
                    for j in range(NJ):
                        act.wait_ge(a_made.sem, a_made.at(b, group * NJ + j))
                        act.activation(raw[s][:, j, :], ps_a[j % 2].ap(), ACT.Copy).then_inc(raw_ready.sem, raw_ready.step)
                        act.wait_ge(sums_made.sem, sums_made.at(b, group * NJ + j - 2))
                        act.activation(sq[:, j % 2, :], ps_a[j % 2].ap(), ACT.Square).then_inc(sq_ready.sem, sq_ready.step)
                        if heads_of and j:
                            for h in HEADS_AFTER[j]:
                                split_head(*heads_of, h)
                    act.wait_ge(sums_made.sem, sums_made.at(b, group * NJ + NJ - 1))
                    act.wait_ge(compact_in.sem, compact_in.at(b, group * NJ - 1))
                    act.activation(rows_.ap(), ps_s.ap(), ACT.Sqrt).then_inc(norm_ready.sem, norm_ready.step)

                def det_logs(b, half):
                    for group in range(half * HALF, (half + 1) * HALF):
                        act.wait_ge(ab_ready.sem, ab_ready.at(b, group))
                        act.activation(shear[:, 0, group, :], shear[:, 0, group, :], ACT.Ln,
                                       bias=one[:, :], scale=-1.0).then_inc(log_ready.sem, log_ready.step)

                def det_inverses(b, half):
                    for group in range(half * HALF, (half + 1) * HALF):
                        act.wait_ge(sum_ready.sem, sum_ready.at(b, group))
                        act.activation(shear[:, 0, group, :], shear[:, 0, group, :], ACT.Exp,
                                       scale=-1.0).then_inc(det_ready.sem, det_ready.step)

                for group in range(HG):
                    scale_beta(0, group)
                evacuate(0, 0, 0)
                det_logs(0, 0)
                det_inverses(0, 0)

                def body(b, last):
                    for group in range(HG):
                        s = group % 2
                        if not (last and group == LAST):
                            evacuate(b, group + 1, 1 - s, (b, group))
                        else:
                            for h in range(HP):
                                split_head(b, group, h)
                        for part in range(2):
                            act.wait_ge(kT_made.sem, kT_made.at(b, group * 2 + part))
                            act.wait_ge(dX_made.sem, dX_made.at(b, group - 1))
                            act.activation(kT[:, part, :], ps_k[part][:, 0:KW], ACT.Copy).then_inc(kT_ready.sem, kT_ready.step)
                        if not last:
                            scale_beta(b + 1, group)
                        if group == HALF - 1:
                            det_logs(b, 1)
                        if group == LAST and not last:
                            det_logs(b + 1, 0)
                        act.wait_ge(y_made.sem, y_made.at(b, group))
                        act.wait_ge(y_stored.sem, y_stored.at(b, group * HP - 1))
                        act.activation(y.ap(), ps_y.ap(), ACT.Copy).then_inc(y_ready.sem, y_ready.step)
                        if group == HALF - 1:
                            det_inverses(b, 1)
                        if group == LAST and not last:
                            det_inverses(b + 1, 0)
                        act.wait_ge(y_ready.sem, y_ready.at(b, group))
                        for h in range(HP):
                            act.dma_start(dram["yT"][b, group, h * DH:(h + 1) * DH, :],
                                                      y[h * N:h * N + DH, :]).then_inc(y_stored.sem, y_stored.step)
                over_rows(act, body)
                act.wait_ge(y_stored.sem, y_stored.at(B - 1, HG * HP - 1))

            @block.vector
            def _(dve):
                for s in (stepped, sum_ready, rows_ready, b_scaled, raw_used, k_ready, q_ready, g_ready, dX_ready,
                          coef_ready, X_ready):
                    dve.sem_inc(s.sem, s.given * s.step)
                dve.memset(one.ap(), 1.0).then_inc(const_set, 1)
                dve.memset(Xb.ap(), 0.0).then_inc(const_set, 1)
                dve.memset(k_head.ap(), 0.0).then_inc(const_set, 1)
                dve.memset(factor.ap(), 1.0).then_inc(const_set, 1)
                dve.memset(ps_y.ap(), 0.0).then_inc(const_set, 1)
                dve.memset(carry.ap(), 1.0).then_inc(const_set, 1)
                own = Own(own_dve)
                dve.wait_ge(const_set, 6)
                dve.memset(carry[:, :, 0:1], 0.0).then_inc(own.sem, own.one())
                for row in range(2):
                    for comp in range(2):
                        dve.memset(psi[:, row, comp, :, :, 0:1], 1.0 if row == comp else 0.0).then_inc(own.sem, own.one())
                dve.wait_ge(own.sem, own.n)
                dve.sem_clear(own.sem)
                own.n = 0
                steps = Own(steps_dve)
                psi_t = [psi.ap().rearrange("p r k g c t -> p r k (g c) t")[:, :, :, n * HALF * TT:(n + 1) * HALF * TT, :]
                         for n in range(2)]
                shear_t = [shear.ap().rearrange("p k g (c t) -> p k (g c) t", c=TT)[:, :, n * HALF * TT:(n + 1) * HALF * TT, :]
                           for n in range(2)]

                def start_psi(b, half):
                    dve.wait_ge(n_alpha_in[half].sem, n_alpha_in[half].at(b, HP - 1))
                    dve.wait_ge(beta_scaled.sem, beta_scaled.at(b, half * HALF + HALF - 1))
                    dve.wait_ge(kx_ready.sem, kx_ready.at(b - 1, half * HALF + HALF - 1))
                    dve.wait_ge(qx_ready.sem, qx_ready.at(b - 1, half * HALF + HALF - 1))

                def step_psi(b, half, first, last):
                    for i in range(first, last):
                        t = i // 2
                        if i:
                            dve.wait_ge(steps.sem, steps.n)
                        if i % 2 == 0:
                            dve.tensor_tensor(prod.ap(), psi_t[half][:, :, :, :, t],
                                              shear_t[half][:, :, :, t].unsqueeze(1).to_broadcast([P, 2, 2, HALF * TT]),
                                              ALU.mult).then_inc(steps.sem, steps.one())
                        else:
                            ins = dve.tensor_tensor(psi_t[half][:, :, :, :, t + 1], psi_t[half][:, :, :, :, t],
                                                    prod[:, :, ::-1, :], ALU.add)
                            ins.then_inc(steps.sem, steps.one()) if t < C - 1 else ins.then_inc(stepped.sem, stepped.step)

                def log_sum(b, half):
                    for group in range(half * HALF, (half + 1) * HALF):
                        dve.wait_ge(log_ready.sem, log_ready.at(b, group))
                        dve.tensor_tensor_scan(shear[:, 0, group, :], carry.ap().rearrange("p c t -> p (c t)"),
                                               shear[:, 0, group, :], 0.0, ALU.mult, ALU.add).then_inc(sum_ready.sem, sum_ready.step)

                def clear_counts():
                    dve.wait_ge(own.sem, own.n)
                    dve.sem_clear(own.sem)
                    own.n = 0
                    dve.wait_ge(steps.sem, steps.n)
                    dve.sem_clear(steps.sem)
                    steps.n = 0

                def scales(b, group, between):
                    dve.wait_ge(compact_in.sem, compact_in.at(b, (group + 1) * NJ - 1))
                    dve.tensor_scalar(compact.ap(), compact.ap(), NORM_EPS, None, ALU.add).then_inc(own.sem, own.one())
                    between(1)
                    dve.wait_ge(own.sem, own.n)
                    dve.reciprocal(compact.ap(), compact.ap()).then_inc(own.sem, own.one())
                    between(1)
                    dve.wait_ge(factor_in.sem, factor_in.at(b, 3 * (group + 1) - 1))
                    dve.wait_ge(own.sem, own.n)
                    dve.tensor_tensor(compact.ap(), compact.ap(), factor.ap(), ALU.mult).then_inc(rows_ready.sem, rows_ready.step)
                    between(1)

                scales(0, 0, lambda n: None)
                start_psi(0, 0)
                step_psi(0, 0, 0, 2 * C)
                log_sum(0, 0)
                clear_counts()

                def body(b, last):
                    dve.wait_ge(e_end_in.sem, e_end_in.at(b, HP - 1))
                    for group in range(HG):
                        s = group % 2
                        r4 = raw[s]
                        psi_b, half, slot = (b, 1, group) if group < HALF else (b + 1, 0, group - HALF)
                        done, end_at = 2 * sum(STEPS[:slot]), 2 * sum(STEPS[:slot + 1])
                        if last and half == 0:
                            done = end_at
                        elif slot == 0:
                            start_psi(psi_b, half)

                        def advance(n):
                            nonlocal done
                            n = min(n, end_at - done)
                            step_psi(psi_b, half, done, done + n)
                            done += n

                        advance(16)
                        dve.wait_ge(scale_in.sem, scale_in.at(b, (group + 1) * HP - 1))
                        for j in range(2):
                            dve.wait_ge(raw_ready.sem, raw_ready.at(b, group * NJ + j))
                            ins = dve.tensor_tensor(r4[:, 1 - j, :], r4[:, 1 - j, :], scale[:, 1 - j, :], ALU.mult)
                            ins.then_inc(own.sem, own.one()) if j == 0 else ins.then_inc(b_scaled.sem, b_scaled.step)
                            advance(1)
                        dve.wait_ge(b_scaled.sem, b_scaled.at(b, group))
                        dve.wait_ge(kT_made.sem, kT_made.at(b, 2 * (group - 2) + 1))
                        dve.wait_ge(g_made.sem, g_made.at(b, (group - 1) * HP - 1))
                        dve.wait_ge(y_made.sem, y_made.at(b, group - 2))
                        for row in range(2):
                            dve.tensor_tensor(chunks(k[s][:, row, :]), chunks(r4[:, 0, :]),
                                                  psi[:, row, 0, group, :, 0:C], ALU.mult).then_inc(own.sem, own.one())
                            advance(2)
                        dve.wait_ge(kx_ready.sem, kx_ready.at(b, group))
                        dve.wait_ge(own.sem, own.n)
                        dve.tensor_tensor(k[s].ap(), k[s].ap(), kx.ap(), ALU.add).then_inc(k_ready.sem, k_ready.step)
                        advance(1)
                        dve.wait_ge(c_scaled.sem, c_scaled.at(b, group))
                        for row in range(2):
                            ins = dve.tensor_tensor(chunks(q[s][:, 1 - row, :]), chunks(r4[:, 2, :]),
                                                    psi[:, row, 1, group, :, 1:], ALU.mult)
                            ins.then_inc(own.sem, own.one()) if row == 0 else ins.then_inc(raw_used.sem, raw_used.step)
                            advance(1)
                        dve.wait_ge(raw_used.sem, raw_used.at(b, group))
                        dve.wait_ge(own.sem, own.n)
                        dve.wait_ge(qx_ready.sem, qx_ready.at(b, group))
                        dve.tensor_tensor(q[s][:, 0, :], q[s][:, 0, :], qx[:, 1, :], ALU.subtract).then_inc(own.sem, own.one())
                        advance(1)
                        dve.tensor_tensor(q[s][:, 1, :], qx[:, 0, :], q[s][:, 1, :], ALU.subtract).then_inc(q_ready.sem, q_ready.step)
                        advance(1)
                        dve.wait_ge(det_ready.sem, det_ready.at(b, group))
                        det_end = chunks(shear[:, 0, group, :])[:, :, C - 1]
                        dve.tensor_tensor(end.ap(), det_end, e_end[:, group, :], ALU.mult).then_inc(own.sem, own.one())
                        advance(1)
                        dve.wait_ge(own.sem, own.n)
                        for comp, by in ((1, end.ap()), (0, det_end)):
                            ins = dve.tensor_tensor(coef[:, comp, :, :], psi[:, :, comp, group, :, C],
                                                    by.unsqueeze(1).to_broadcast([P, 2, TT]), ALU.mult)
                            ins.then_inc(own.sem, own.one()) if comp else ins.then_inc(coef_ready.sem, coef_ready.step)
                            advance(1)

                        def mask(h):
                            dve.wait_ge(g_made.sem, g_made.at(b, group * HP + h))
                            dve.wait_ge(y_made.sem, y_made.at(b, group - 1))
                            dve.tensor_tensor(chunks(g[:, h, :]), chunks(ps_g[h % 2].ap()),
                                                         causal.ap().unsqueeze(1).to_broadcast([P, TT, C]), ALU.mult).then_inc(g_ready.sem, g_ready.step)
                            advance(1)

                        advance(12)
                        for h in range(2):
                            mask(h)
                        if not (last and group == LAST):
                            scales(b, group + 1, advance)
                        dve.wait_ge(dX_made.sem, dX_made.at(b, group))
                        dve.tensor_copy(dX.ap().rearrange("p c r d -> p (c r d)"), ps_dX).then_inc(dX_ready.sem, dX_ready.step)
                        advance(1)
                        for h in range(2, HP):
                            mask(h)
                        dve.wait_ge(dX_ready.sem, dX_ready.at(b, group))
                        dve.wait_ge(coef_ready.sem, coef_ready.at(b, group))
                        dve.wait_ge(Xb_ready.sem, Xb_ready.at(b, group * (TT - 1) - 1))
                        for c in range(TT - 1):
                            if c:
                                dve.wait_ge(X_ready.sem, X_ready.at(b, group * (TT - 1) + c - 1))
                                dve.tensor_tensor(dX[:, c], dX[:, c], X[:, c - 1], ALU.add).then_inc(own.sem, own.one())
                                advance(2)
                                dve.wait_ge(own.sem, own.n)
                            for part in range(2):
                                comp, row = (1, 0) if part == 0 else (0, 1)
                                dve.tensor_scalar(tmp[:, part, :], dX[:, c, 1 - part, :],
                                                      coef[:, comp, row, c:c + 1], None, ALU.mult).then_inc(own.sem, own.one())
                                advance(1)
                            dve.wait_ge(own.sem, own.n)
                            for part in range(2):
                                comp, row = (1, 1) if part == 0 else (0, 0)
                                ins = dve.scalar_tensor_tensor(
                                    out=X[:, c, part, :], in0=dX[:, c, part, :], scalar=coef[:, comp, row, c:c + 1],
                                    in1=tmp[:, part, :], op0=ALU.mult, op1=ALU.subtract)
                                ins.then_inc(own.sem, own.one()) if part == 0 else ins.then_inc(X_ready.sem, X_ready.step)
                                advance(1)
                            dve.wait_ge(own.sem, own.n)
                        advance(end_at - done)
                        if group == HALF - 1:
                            log_sum(b, 1)
                        if group == LAST and not last:
                            log_sum(b + 1, 0)
                    clear_counts()
                over_rows(dve, body)


def ffn(nc, a, dram, out):
    F32R = mybir.dt.float32r
    with ExitStack() as ctx:
        def sb(name, shape, dt=F32):
            return ctx.enter_context(nc.sbuf_tensor("f_" + name, shape, dt))

        def sem(name):
            return ctx.enter_context(nc.semaphore("f_" + name))

        def sig(name, per, step=1, credited=True):
            return Signal(ctx, nc, "f_" + name, per, step, credited)

        ident = sb("ident", [P, P])
        ones = sb("ones", [P, P])
        w_out = sb("w_out", [P, KI, D])
        w1 = sb("w1", [P, KD, FF])
        w2 = sb("w2", [P, KF, D])
        above = sb("above", [P, KD * FF])
        below = sb("below", [P, KD * FF])
        t1 = sb("t1", [P, KD, FF], F32R)
        t2 = sb("t2", [P, KF, D], F32R)
        b1 = sb("b1", [P, KF])
        b2 = sb("b2", [P, D])
        eps = sb("eps", [P, 1])
        total = sb("total", [P, 2])
        half = sb("half", [P, 2])
        nhalf = sb("nhalf", [P, 2])
        y = [sb(f"y{s}", [P, KI, T]) for s in range(2)]
        gate = [sb(f"gate{s}", [P, KI, T]) for s in range(2)]
        svg = [sb(f"svg{s}", [P, KI, T]) for s in range(2)]
        x = [sb(f"x{s}", [P, TT, D]) for s in range(2)]
        stats = sb("stats", [P, TT, 6])
        mv = [sb(f"mv{n}", [P, TT, 2]) for n in range(3)]
        sd = [sb(f"sd{n}", [P, TT]) for n in range(3)]
        rstd = [sb(f"rstd{n}", [P, TT]) for n in range(3)]
        on = sb("on", [P, TT, D])
        xn = sb("xn", [P, TT, D])
        xh = sb("xh", [P, KD, T], F32R)
        xl = sb("xl", [P, KD, T], F32R)
        g = [sb(f"g{s}", [P, T]) for s in range(2)]
        gh = sb("gh", [P, KF, T], F32R)
        gl = sb("gl", [P, KF, T], F32R)
        o2 = sb("o2", [P, TT, D])
        res = sb("res", [P, TT, D])
        ps_o = [ctx.enter_context(nc.psum_tensor(f"f_ps_o{k}", [P, 2, D], F32)) for k in range(2)]
        ps_x = [ctx.enter_context(nc.psum_tensor(f"f_ps_x{k}", [P, T], F32)) for k in range(KD)]
        ps_h = [ctx.enter_context(nc.psum_tensor(f"f_ps_h{k}", [P, T], F32)) for k in range(2)]
        ps_2 = [ctx.enter_context(nc.psum_tensor(f"f_ps_2{k}", [P, 2, D], F32)) for k in range(2)]

        consts_in = sem("consts_in")
        weights_in = sem("weights_in")
        const_set = sem("const_set")
        sums_made = sem("sums_made")
        ternary_ready = sem("ternary_ready")
        x_in = [sig(f"x_in{s}", 1, 16) for s in range(2)]
        y_in = [sig(f"y_in{s}", 3, 16) for s in range(2)]
        gated = sig("gated", 1)
        proj_made = sig("proj_made", 1)
        var_ready = sig("var_ready", 2)
        sd_ready = sig("sd_ready", 2)
        var2_ready = sig("var2_ready", 1)
        sd2_ready = sig("sd2_ready", 1)
        xn_ready = sig("xn_ready", 1)
        xT_made = sig("xT_made", 1)
        xh_ready = sig("xh_ready", KD)
        xl_ready = sig("xl_ready", KD)
        h_made = sig("h_made", KF)
        g_ready = sig("g_ready", KF)
        gh_ready = sig("gh_ready", KF)
        gl_ready = sig("gl_ready", KF)
        o2_made = sig("o2_made", 1)
        o2_ready = sig("o2_ready", 1)
        res_ready = sig("res_ready", 1)
        res_stored = sig("res_stored", 1, 16)
        own_dve, own_pool = sem("own_dve"), sem("own_pool")

        def rows(eng, body):
            with eng.Fori(0, B // 2 - 1) as i:
                for s in range(2):
                    body(i * 2 + s, s, i, False)
            for s in range(2):
                body(B - 2 + s, s, B // 2 - 1, s == 1)

        with nc.Block() as block:
            @block.sync
            def _(sp):
                for dst, src in ((ident, a["ident"]), (b1, a["b1"])):
                    sp.dma_start(dst.ap(), src).then_inc(consts_in, 16)
                sp.dma_start(b2.ap(), a["b2"].to_broadcast([P, D])).then_inc(consts_in, 16)
                sp.dma_start(w_out.ap(), a["w_outT"].rearrange("(k p) o -> p k o", p=P)).then_inc(consts_in, 16)
                for s in (*x_in, *y_in, res_stored):
                    sp.sem_inc(s.sem, s.given * s.step)

                def load(b, s, pair, before):
                    sp.wait_ge(gated.sem, gated.at(before, 0))
                    sp.wait_ge(proj_made.sem, proj_made.at(before, 0))
                    for dst, name in ((y, "yT"), (gate, "gateT"), (svg, "svgT")):
                        src = dram[name][b]
                        if name == "yT":
                            src = src.rearrange("g c t -> (g c) t").rearrange("(k p) t -> p k t", p=P)
                        sp.dma_start(dst[s].ap(), src).then_inc(y_in[s].sem, y_in[s].step)
                    sp.wait_ge(res_ready.sem, res_ready.at(before, 0))
                    sp.dma_start(x[s].ap(), a["x"][b].rearrange("(t p) d -> p t d", p=P)).then_inc(x_in[s].sem, x_in[s].step)

                for s in range(2):
                    for dst, name in ((y, "yT"), (gate, "gateT"), (svg, "svgT")):
                        src = dram[name][s]
                        if name == "yT":
                            src = src.rearrange("g c t -> (g c) t").rearrange("(k p) t -> p k t", p=P)
                        sp.dma_start(dst[s].ap(), src).then_inc(y_in[s].sem, y_in[s].step)
                    sp.dma_start(x[s].ap(), a["x"][s].rearrange("(t p) d -> p t d", p=P)).then_inc(x_in[s].sem, x_in[s].step)
                    if s == 0:
                        sp.dma_start(w1.ap(), a["w1T"].rearrange("(k p) o -> p k o", p=P)).then_inc(weights_in, 16)
                        sp.dma_start(w2.ap(), a["w2T"].rearrange("(k p) o -> p k o", p=P)).then_inc(weights_in, 16)

                def store(b):
                    sp.wait_ge(res_ready.sem, res_ready.at(b, 0))
                    sp.dma_start(out[b].rearrange("(t p) d -> p t d", p=P), res.ap()).then_inc(res_stored.sem, res_stored.step)

                with sp.Fori(0, B // 2 - 1) as i:
                    for s in range(2):
                        store(i * 2 + s)
                        load(i * 2 + s + 2, s, i + 1, i * 2 + s)
                for s in range(2):
                    store(B - 2 + s)
                sp.wait_ge(res_stored.sem, res_stored.at(B - 1, 0))

            @block.gpsimd
            def _(pool):
                pool.sem_inc(gated.sem, gated.given * gated.step)
                own = Own(own_pool)

                def body(b, s, i, last):
                    pool.wait_ge(y_in[s].sem, y_in[s].at(i, 2))
                    pool.tensor_tensor(y[s].ap(), y[s].ap(), gate[s].ap(), ALU.mult).then_inc(own.sem, own.one())
                    pool.wait_ge(own.sem, own.n)
                    pool.tensor_tensor(y[s].ap(), y[s].ap(), svg[s].ap(), ALU.add).then_inc(gated.sem, gated.step)
                    pool.wait_ge(own.sem, own.n)
                    pool.sem_clear(own.sem)
                    own.n = 0
                rows(pool, body)

            @block.tensor
            def _(pe):
                for s in (proj_made, xT_made, h_made, o2_made):
                    pe.sem_inc(s.sem, s.given * s.step)
                pe.wait_ge(consts_in, 64)

                def project_out(b, s):
                    pe.wait_ge(gated.sem, gated.at(b, 0))
                    pe.wait_ge(xn_ready.sem, xn_ready.at(b, -1))
                    for t in range(TT):
                        for k in range(KI):
                            mm = pe.matmul(ps_o[t // 2][:, t % 2, :], y[s][:, k, t * P:(t + 1) * P], w_out[:, k, :],
                                           start=(k == 0), stop=(k == KI - 1), skip_group_check=True)
                    mm.then_inc(proj_made.sem, proj_made.step)

                project_out(0, 0)
                pe.wait_ge(const_set, 4)
                pe.matmul(ps_h[0][:, 0:2], ones.ap(), total.ap(), start=True, stop=True).then_inc(sums_made, 1)
                pe.wait_ge(ternary_ready, 2)

                def body(b, s, i, last):
                    pe.wait_ge(xn_ready.sem, xn_ready.at(b, 0))
                    pe.wait_ge(xl_ready.sem, xl_ready.at(b, -1))
                    for k in range(KD):
                        for t in range(TT):
                            mm = pe.transpose(ps_x[k][:, t * P:(t + 1) * P], xn[:, t, k * P:(k + 1) * P], ident.ap())
                    mm.then_inc(xT_made.sem, xT_made.step)
                    pe.wait_ge(xl_ready.sem, xl_ready.at(b, KD - 1))
                    for f in range(KF):
                        pe.wait_ge(g_ready.sem, g_ready.at(b, f - 2))
                        for k in range(KD):
                            for part in (xh, xl):
                                mm = pe.matmul(ps_h[f % 2].ap(), t1[:, k, f * P:(f + 1) * P], part[:, k, :],
                                               start=(k == 0 and part is xh), stop=(k == KD - 1 and part is xl))
                        mm.then_inc(h_made.sem, h_made.step)
                    if not last:
                        project_out(b + 1, 1 - s)
                    pe.wait_ge(gl_ready.sem, gl_ready.at(b, KF - 1))
                    pe.wait_ge(o2_ready.sem, o2_ready.at(b, -1))
                    for t in range(TT):
                        for f in range(KF):
                            for part in (gh, gl):
                                mm = pe.matmul(ps_2[t // 2][:, t % 2, :], part[:, f, t * P:(t + 1) * P], t2[:, f, :],
                                               start=(f == 0 and part is gh), stop=(f == KF - 1 and part is gl),
                                               skip_group_check=True)
                    mm.then_inc(o2_made.sem, o2_made.step)
                rows(pe, body)

            @block.scalar
            def _(act):
                for s in (sd_ready, sd2_ready, xh_ready, g_ready, gh_ready):
                    act.sem_inc(s.sem, s.given * s.step)
                act.wait_ge(consts_in, 64)
                act.wait_ge(const_set, 4)

                def deviation(b, n):
                    act.wait_ge(var_ready.sem, var_ready.at(b, n))
                    act.activation(sd[n].ap(), mv[n][:, :, 1], ACT.Sqrt, bias=eps.ap()).then_inc(sd_ready.sem, sd_ready.step)

                deviation(0, 0)
                deviation(0, 1)

                def body(b, s, i, last):
                    act.wait_ge(xT_made.sem, xT_made.at(b, 0))
                    act.wait_ge(h_made.sem, h_made.at(b, -1))
                    for k in range(KD):
                        act.activation(xh[:, k, :], ps_x[k].ap(), ACT.Copy).then_inc(xh_ready.sem, xh_ready.step)
                    act.wait_ge(o2_made.sem, o2_made.at(b, -1))
                    for f in range(KF):
                        act.wait_ge(h_made.sem, h_made.at(b, f))
                        act.wait_ge(gl_ready.sem, gl_ready.at(b, f - 2))
                        act.wait_ge(gh_ready.sem, gh_ready.at(b, f - 2))
                        act.activation(g[f % 2].ap(), ps_h[f % 2].ap(), ACT.Gelu, bias=b1[:, f:f + 1]).then_inc(g_ready.sem, g_ready.step)
                        act.wait_ge(g_ready.sem, g_ready.at(b, f))
                        act.activation(gh[:, f, :], g[f % 2].ap(), ACT.Copy).then_inc(gh_ready.sem, gh_ready.step)
                    if not last:
                        deviation(b + 1, 0)
                        deviation(b + 1, 1)
                    act.wait_ge(var2_ready.sem, var2_ready.at(b, 0))
                    act.activation(sd[2].ap(), mv[2][:, :, 1], ACT.Sqrt, bias=eps.ap()).then_inc(sd2_ready.sem, sd2_ready.step)
                rows(act, body)

            @block.vector
            def _(dve):
                for s in (var_ready, var2_ready, xn_ready, xl_ready, gl_ready, o2_ready, res_ready):
                    dve.sem_inc(s.sem, s.given * s.step)
                own = Own(own_dve)
                dve.memset(ones.ap(), 1.0).then_inc(const_set, 1)
                dve.memset(eps.ap(), LN_EPS).then_inc(const_set, 1)
                dve.wait_ge(weights_in, 32)
                flat = [w.ap().rearrange("p k o -> p (k o)") for w in (w1, w2)]
                for n in range(2):
                    dve.tensor_reduce(total[:, n:n + 1], flat[n], AX.X, ALU.add,
                                      apply_absolute_value=True).then_inc(const_set, 1)
                dve.wait_ge(sums_made, 1)
                dve.tensor_scalar(half.ap(), ps_h[0][:, 0:2], 1.0 / (D * FF), NORM_EPS, ALU.mult, ALU.max).then_inc(own.sem, own.one())
                dve.wait_ge(own.sem, own.n)
                dve.tensor_scalar(nhalf.ap(), half.ap(), -0.5, None, ALU.mult).then_inc(own.sem, own.one())
                dve.wait_ge(own.sem, own.n)
                dve.tensor_scalar(half.ap(), half.ap(), 0.5, None, ALU.mult).then_inc(own.sem, own.one())
                dve.wait_ge(own.sem, own.n)
                for n, (w, tern) in enumerate(((flat[0], t1), (flat[1], t2))):
                    dve.tensor_scalar(above.ap(), w, half[:, n:n + 1], None, ALU.is_gt).then_inc(own.sem, own.one())
                    dve.tensor_scalar(below.ap(), w, nhalf[:, n:n + 1], None, ALU.is_lt).then_inc(own.sem, own.one())
                    dve.wait_ge(own.sem, own.n)
                    dve.tensor_tensor(tern.ap().rearrange("p k o -> p (k o)"), above.ap(), below.ap(),
                                      ALU.subtract).then_inc(ternary_ready, 1)
                    dve.wait_ge(ternary_ready, n + 1)
                dve.wait_ge(own.sem, own.n)
                dve.sem_clear(own.sem)
                own.n = 0

                def moments(src, n, signal):
                    for t in range(TT):
                        dve.bn_stats(stats[:, t, :], src(t)).then_inc(own.sem, own.one())
                    dve.wait_ge(own.sem, own.n)
                    for t in range(TT):
                        ins = dve.bn_aggr(mv[n][:, t, :], stats[:, t, :])
                        ins.then_inc(own.sem, own.one()) if t < TT - 1 else ins.then_inc(signal.sem, signal.step)

                def normalise(dst, src, n, count=None):
                    for t in range(TT):
                        ins = dve.tensor_scalar(dst[:, t, :], src(t), mv[n][:, t, 0:1], rstd[n][:, t:t + 1],
                                                ALU.subtract, ALU.mult)
                        ins.then_inc(own.sem, own.one()) if count is None or t < TT - 1 else ins.then_inc(count.sem, count.step)

                def first_norms(b, s, i):
                    dve.wait_ge(proj_made.sem, proj_made.at(b, 0))
                    moments(lambda t: ps_o[t // 2][:, t % 2, :], 0, var_ready)
                    dve.wait_ge(sd_ready.sem, sd_ready.at(b, 0))
                    dve.reciprocal(rstd[0].ap(), sd[0].ap()).then_inc(own.sem, own.one())
                    dve.wait_ge(own.sem, own.n)
                    normalise(on, lambda t: ps_o[t // 2][:, t % 2, :], 0)
                    dve.wait_ge(own.sem, own.n)
                    dve.wait_ge(x_in[s].sem, x_in[s].at(i, 0))
                    dve.tensor_tensor(x[s].ap(), x[s].ap(), on.ap(), ALU.add).then_inc(own.sem, own.one())
                    dve.wait_ge(own.sem, own.n)
                    moments(lambda t: x[s][:, t, :], 1, var_ready)
                    dve.wait_ge(sd_ready.sem, sd_ready.at(b, 1))
                    dve.reciprocal(rstd[1].ap(), sd[1].ap()).then_inc(own.sem, own.one())
                    dve.wait_ge(own.sem, own.n)
                    dve.wait_ge(xT_made.sem, xT_made.at(b, -1))
                    normalise(xn, lambda t: x[s][:, t, :], 1, xn_ready)

                first_norms(0, 0, 0)
                dve.wait_ge(own.sem, own.n)
                dve.sem_clear(own.sem)
                own.n = 0

                def body(b, s, i, last):
                    dve.wait_ge(h_made.sem, h_made.at(b, -1))
                    for k in range(KD):
                        dve.wait_ge(xh_ready.sem, xh_ready.at(b, k))
                        dve.tensor_tensor(xl[:, k, :], ps_x[k].ap(), xh[:, k, :].bitcast(F32), ALU.subtract).then_inc(xl_ready.sem, xl_ready.step)
                    dve.wait_ge(o2_made.sem, o2_made.at(b, -1))
                    for f in range(KF):
                        dve.wait_ge(gh_ready.sem, gh_ready.at(b, f))
                        dve.tensor_tensor(gl[:, f, :], g[f % 2].ap(), gh[:, f, :].bitcast(F32), ALU.subtract).then_inc(gl_ready.sem, gl_ready.step)
                    if not last:
                        first_norms(b + 1, 1 - s, i + s)
                    dve.wait_ge(o2_made.sem, o2_made.at(b, 0))
                    for half_ in range(2):
                        ins = dve.tensor_tensor(o2[:, 2 * half_:2 * half_ + 2, :], ps_2[half_].ap(),
                                                b2.ap().unsqueeze(1).to_broadcast([P, 2, D]), ALU.add)
                        ins.then_inc(o2_ready.sem, o2_ready.step) if half_ else ins.then_inc(own.sem, own.one())
                    dve.wait_ge(own.sem, own.n)
                    dve.wait_ge(o2_ready.sem, o2_ready.at(b, 0))
                    moments(lambda t: o2[:, t, :], 2, var2_ready)
                    dve.wait_ge(sd2_ready.sem, sd2_ready.at(b, 0))
                    dve.reciprocal(rstd[2].ap(), sd[2].ap()).then_inc(own.sem, own.one())
                    dve.wait_ge(own.sem, own.n)
                    normalise(o2, lambda t: o2[:, t, :], 2)
                    dve.wait_ge(own.sem, own.n)
                    dve.wait_ge(res_stored.sem, res_stored.at(b, -1))
                    dve.tensor_tensor(res.ap(), x[s].ap(), o2.ap(), ALU.add).then_inc(res_ready.sem, res_ready.step)
                    dve.wait_ge(own.sem, own.n)
                    dve.sem_clear(own.sem)
                    own.n = 0
                rows(dve, body)


def build(nc, a, out):
    def scratch(name, *shape):
        return nc.dram_tensor("scratch_" + name, shape, F32, kind="Internal").ap()

    dram = {
        "n_alpha": scratch("n_alpha", B, H, T), "beta": scratch("beta", B, H, T), "dt": scratch("dt", B, H, T),
        "e_inv": scratch("e_inv", B, H, T), "e_end": scratch("e_end", B, H, TT),
        "valT": scratch("valT", B, P, KI, T), "gateT": scratch("gateT", B, P, KI, T),
        "svgT": scratch("svgT", B, P, KI, T), "u": scratch("u", B, P, TT, DI),
        "norm": scratch("norm", 2, NJ * HP, T), "yT": scratch("yT", B, HG, HP * DH, T),
    }
    project(nc, a, dram)
    mix(nc, a, dram)
    ffn(nc, a, dram, out)


_OUTS = [((B, T, D), "float32")]


def kernel(L0_attn_x, L0_attn_W_in, L0_attn_dw_weight, L0_attn_dw_bias, L0_attn_W_bc, L0_attn_W_out, L0_attn_skip,
           L0_attn_A_log, L0_attn_dt_bias, L0_ffn_W1, L0_ffn_b1, L0_ffn_W2, L0_ffn_b2):
    import numpy as np
    import concourse.bacc as _bacc
    from concourse.bass_utils import run_bass_kernel_spmd as _run

    def tiles(v):
        v = np.asarray(v)
        return v.reshape(-1, P, *v.shape[1:]).swapaxes(0, 1)

    w_in = np.asarray(L0_attn_W_in)
    steps = w_in[2 * DI:].reshape(H, 2, D)
    w_bc = np.asarray(L0_attn_W_bc).reshape(HG, HP, NJ, N, KI, P)
    p = np.arange(P)
    arrays = {
        "x": L0_attn_x,
        "w_inT": np.concatenate([w_in[:2 * DI], steps[:, 0], steps[:, 1]]).T,
        "taps": tiles(L0_attn_dw_weight), "dw_bias": tiles(L0_attn_dw_bias), "skip": tiles(L0_attn_skip),
        "dt_bias": np.asarray(L0_attn_dt_bias).reshape(H, 1),
        "w_bcT": w_bc.transpose(0, 2, 5, 4, 1, 3).reshape(HG, NJ, P, KI * P),
        "a_log": np.asarray(L0_attn_A_log).reshape(HG, P).T,
        "w_outT": np.asarray(L0_attn_W_out).T,
        "w1T": np.asarray(L0_ffn_W1).T, "b1": tiles(L0_ffn_b1),
        "w2T": np.asarray(L0_ffn_W2).T, "b2": np.asarray(L0_ffn_b2).reshape(1, D),
        "ident": np.eye(P, dtype=np.float32),
        "head_sum": (p[:, None] // N == np.arange(N)[None]).astype(np.float32),
        "causal": (p[:, None] <= p[None]).astype(np.float32),
        "head_block": np.repeat((p[:, None] // N == np.arange(HP)[None]).astype(np.float32), DH, axis=1),
    }
    arrays = {k: np.ascontiguousarray(v) for k, v in arrays.items()}
    nc = _bacc.Bacc("TRN2", target_bir_lowering=False, num_devices=1)
    a = {k: nc.dram_tensor("in_" + k, v.shape, mybir.dt.from_np(v.dtype), kind="ExternalInput").ap()
         for k, v in arrays.items()}
    out = nc.dram_tensor("out_0", _OUTS[0][0], F32, kind="ExternalOutput").ap()
    build(nc, a, out)
    r = _run(nc, [{"in_" + k: v for k, v in arrays.items()}], core_ids=[0])
    return r.results[0]["out_0"]
```

```python
from contextlib import ExitStack

import concourse.bass as bass
from concourse import mybir

F32 = mybir.dt.float32
ALU = mybir.AluOpType
ACT = mybir.ActivationFunctionType
AX = mybir.AxisListType

P = 128
B, T, D = 8, 512, 256
TT = T // P
KD = D // P
DI = 512
KI = DI // P
H, N, DH = 32, 32, 16
HP = P // N
HG = H // HP
NJ = 4
TAPS = 4
FF = 1024
KF = FF // P
C = P
LN_EPS = 1e-5
NORM_EPS = 1e-8
DT_MIN, DT_MAX, K_MAX = 1e-4, 0.1, 0.5
EXP_CAP = 2e4
TINY = 1e-12


class Signal:

    def __init__(self, ctx, nc, name, per, step=1, credited=True):
        self.sem, self.per, self.step = ctx.enter_context(nc.semaphore(name)), per, step
        self.given = per if credited else 0

    def at(self, b, item):
        return (b * self.per + self.given + item + 1) * self.step


class Own:

    def __init__(self, sem):
        self.sem, self.n = sem, 0

    def one(self):
        self.n += 1
        return 1


def over_rows(eng, body):
    with eng.Fori(0, B - 1) as b:
        body(b, False)
    body(B - 1, True)


def project(nc, a, dram):
    with ExitStack() as ctx:
        def sb(name, shape):
            return ctx.enter_context(nc.sbuf_tensor(name, shape, F32))

        def sem(name):
            return ctx.enter_context(nc.semaphore(name))

        ident = sb("p_ident", [P, P])
        w_in = sb("w_in", [P, KD, 2 * DI + 2 * H])
        taps = sb("taps", [P, KI, TAPS])
        dw_bias = sb("dw_bias", [P, KI])
        skip = sb("skip", [P, KI])
        dt_bias = sb("dt_bias", [P, 1])
        x = sb("p_x", [P, TT, D])
        stats = sb("p_stats", [P, TT, 6])
        mv = sb("p_mv", [P, TT, 2])
        sd = sb("p_sd", [P, TT])
        rstd = sb("p_rstd", [P, TT])
        xn = sb("p_xn", [P, TT, D])
        xnT = sb("p_xnT", [P, KD, T])
        vraw = sb("vraw", [P, KI, T + TAPS - 1])
        conv = sb("conv", [P, KI, T])
        val = sb("val", [P, KI, T])
        gate = sb("gate", [P, KI, T])
        svg = sb("svg", [P, KI, T])
        u = sb("p_u", [P, TT, DI])
        logits = sb("logits", [2 * H, T])
        compact = sb("p_compact", [P, 2, C])
        ez, ek, lz, w, dt, kd, zero, e_inv, n_alpha, beta = (
            sb(name, [P, C]) for name in ("ez", "ek", "lz", "w", "dt", "kd", "zero", "e_inv", "n_alpha", "beta"))
        E = sb("E", [P, C + 1])
        eps = sb("p_eps", [P, 1])
        ps_x = [ctx.enter_context(nc.psum_tensor(f"ps_x{k}", [P, T], F32)) for k in range(KD)]
        BANKS = 3
        ps_w = [ctx.enter_context(nc.psum_tensor(f"ps_w{k}", [P, T], F32)) for k in range(BANKS)]
        ps_l = ctx.enter_context(nc.psum_tensor("ps_l", [P, T], F32))
        ps_u = [ctx.enter_context(nc.psum_tensor(f"ps_u{k}", [P, T], F32)) for k in range(2)]

        def sig(name, per, step=1, credited=True):
            return Signal(ctx, nc, "p_" + name, per, step, credited)

        consts_in = sem("p_consts_in")
        const_set = sem("p_const_set")
        x_in = sig("x_in", 1, 16, credited=False)
        xn_ready = sig("xn_ready", TT)
        var_ready = sig("var_ready", 1)
        sd_ready = sig("sd_ready", 1)
        xT_made = sig("xT_made", 1)
        xnT_ready = sig("xnT_ready", KD)
        logit_made = sig("logit_made", 1)
        logit_ready = sig("logit_ready", 1)
        compact_in = sig("compact_in", 2, 16)
        exps_ready = sig("exps_ready", 3)
        one_ez_ready = sig("one_ez_ready", 1)
        tile_made = sig("tile_made", 2 * KI)
        vraw_ready = sig("vraw_ready", KI)
        gate_ready = sig("gate_ready", KI)
        conv_ready = sig("conv_ready", KI)
        val_ready = sig("val_ready", KI)
        svg_ready = sig("svg_ready", KI)
        steps_ready = sig("steps_ready", 1)
        u_made = sig("u_made", TT)
        u_ready = sig("u_ready", TT)
        steps_stored = sig("steps_stored", 5, 16)
        val_stored = sig("val_stored", 1, 16)
        gate_stored = sig("gate_stored", 1, 16)
        svg_stored = sig("svg_stored", 1, 16)
        u_stored = sig("u_stored", 1, 16)
        own_dve = sem("p_own_dve")

        with nc.Block() as block:
            @block.sync
            def _(sp):
                for dst, src in ((ident, a["ident"]), (taps, a["taps"]), (dw_bias, a["dw_bias"]),
                                 (skip, a["skip"]), (dt_bias, a["dt_bias"])):
                    sp.dma_start(dst.ap(), src).then_inc(consts_in, 16)
                sp.dma_start(w_in.ap(), a["w_inT"].rearrange("(k p) o -> p k o", p=P)).then_inc(consts_in, 16)
                for s in (compact_in, steps_stored, val_stored, gate_stored, svg_stored, u_stored):
                    sp.sem_inc(s.sem, s.given * s.step)
                with sp.Fori(0, B) as b:
                    sp.wait_ge(logit_ready.sem, logit_ready.at(b, 0))
                    for n in range(2):
                        sp.dma_start(compact[:, n, :], logits[n * H:(n + 1) * H, :].rearrange("h (c t) -> h c t", c=TT)
                                     ).then_inc(compact_in.sem, compact_in.step)
                    sp.wait_ge(gate_ready.sem, gate_ready.at(b, KI - 1))
                    sp.dma_start(dram["gateT"][b], gate.ap()).then_inc(gate_stored.sem, gate_stored.step)
                    sp.wait_ge(val_ready.sem, val_ready.at(b, KI - 1))
                    sp.dma_start(dram["valT"][b], val.ap()).then_inc(val_stored.sem, val_stored.step)
                    sp.wait_ge(steps_ready.sem, steps_ready.at(b, 0))
                    for name, src in (("n_alpha", n_alpha.ap()), ("beta", beta.ap()), ("dt", dt.ap()),
                                      ("e_inv", e_inv.ap())):
                        sp.dma_start(dram[name][b].rearrange("h (c t) -> (h c) t", c=TT), src
                                     ).then_inc(steps_stored.sem, steps_stored.step)
                    sp.dma_start(dram["e_end"][b].rearrange("h (c o) -> (h c) o", o=1), e_inv[:, C - 1:C]
                                 ).then_inc(steps_stored.sem, steps_stored.step)
                    sp.wait_ge(svg_ready.sem, svg_ready.at(b, KI - 1))
                    sp.dma_start(dram["svgT"][b], svg.ap()).then_inc(svg_stored.sem, svg_stored.step)
                    sp.wait_ge(u_ready.sem, u_ready.at(b, TT - 1))
                    sp.dma_start(dram["u"][b], u.ap()).then_inc(u_stored.sem, u_stored.step)
                for s in (steps_stored, val_stored, gate_stored, svg_stored, u_stored):
                    sp.wait_ge(s.sem, s.at(B - 1, s.per - 1))

            @block.gpsimd
            def _(pool):
                with pool.Fori(0, B) as b:
                    pool.wait_ge(xn_ready.sem, xn_ready.at(b, -1))
                    pool.dma_start(x.ap(), a["x"][b].rearrange("(t p) d -> p t d", p=P)).then_inc(x_in.sem, x_in.step)

            @block.tensor
            def _(pe):
                for s in (xT_made, logit_made, tile_made, u_made):
                    pe.sem_inc(s.sem, s.given * s.step)
                pe.wait_ge(consts_in, 96)

                def transpose_xn(b):
                    pe.wait_ge(xn_ready.sem, xn_ready.at(b, TT - 1))
                    pe.wait_ge(xnT_ready.sem, xnT_ready.at(b, -1))
                    for k in range(KD):
                        for t in range(TT):
                            mm = pe.transpose(ps_x[k][:, t * P:(t + 1) * P], xn[:, t, k * P:(k + 1) * P], ident.ap())
                    mm.then_inc(xT_made.sem, xT_made.step)

                def tile(b, i):
                    if i < KI + BANKS and i >= BANKS:
                        pe.wait_ge(vraw_ready.sem, vraw_ready.at(b, i - BANKS))
                    elif i >= BANKS:
                        pe.wait_ge(gate_ready.sem, gate_ready.at(b, i - BANKS - KI))
                    else:
                        pe.wait_ge(gate_ready.sem, gate_ready.at(b, -1))
                    col = (DI + i * P) if i < KI else (i - KI) * P
                    for k in range(KD):
                        mm = pe.matmul(ps_w[i % BANKS].ap(), w_in[:, k, col:col + P], xnT[:, k, :],
                                       start=(k == 0), stop=(k == KD - 1))
                    mm.then_inc(tile_made.sem, tile_made.step)

                def body(b, last):
                    pe.wait_ge(xnT_ready.sem, xnT_ready.at(b, KD - 1))
                    pe.wait_ge(logit_ready.sem, logit_ready.at(b, -1))
                    for k in range(KD):
                        mm = pe.matmul(ps_l[0:2 * H, :], w_in[:, k, 2 * DI:2 * DI + 2 * H], xnT[:, k, :],
                                       start=(k == 0), stop=(k == KD - 1))
                    mm.then_inc(logit_made.sem, logit_made.step)
                    for i in range(2 * KI - 1):
                        tile(b, i)
                    if not last:
                        transpose_xn(b + 1)
                    tile(b, 2 * KI - 1)
                    for t in range(TT):
                        pe.wait_ge(val_ready.sem, val_ready.at(b, KI - 1))
                        pe.wait_ge(u_ready.sem, u_ready.at(b, t - 2))
                        for k in range(KI):
                            mm = pe.transpose(ps_u[t % 2][:, k * P:(k + 1) * P], val[:, k, t * P:(t + 1) * P], ident.ap())
                        mm.then_inc(u_made.sem, u_made.step)

                transpose_xn(0)
                over_rows(pe, body)

            @block.scalar
            def _(act):
                for s in (sd_ready, xnT_ready, logit_ready, exps_ready, vraw_ready, gate_ready, val_ready, u_ready):
                    act.sem_inc(s.sem, s.given * s.step)
                act.wait_ge(consts_in, 96)
                act.wait_ge(const_set, 4)

                def deviation(b):
                    act.wait_ge(var_ready.sem, var_ready.at(b, 0))
                    act.activation(sd.ap(), mv[:, :, 1], ACT.Sqrt, bias=eps.ap()).then_inc(sd_ready.sem, sd_ready.step)

                def copy_xnT(b):
                    act.wait_ge(xT_made.sem, xT_made.at(b, 0))
                    act.wait_ge(tile_made.sem, tile_made.at(b, -1))
                    for k in range(KD):
                        act.activation(xnT[:, k, :], ps_x[k].ap(), ACT.Copy).then_inc(xnT_ready.sem, xnT_ready.step)

                def body(b, last):
                    if not last:
                        deviation(b + 1)
                    act.wait_ge(logit_made.sem, logit_made.at(b, 0))
                    act.wait_ge(compact_in.sem, compact_in.at(b, -1))
                    act.activation(logits.ap(), ps_l[0:2 * H, :], ACT.Copy).then_inc(logit_ready.sem, logit_ready.step)
                    for i in range(KI):
                        act.wait_ge(tile_made.sem, tile_made.at(b, i))
                        act.wait_ge(conv_ready.sem, conv_ready.at(b, -1))
                        act.activation(vraw[:, i, TAPS - 1:], ps_w[i % BANKS].ap(), ACT.Copy).then_inc(vraw_ready.sem, vraw_ready.step)
                    act.wait_ge(compact_in.sem, compact_in.at(b, 1))
                    act.wait_ge(steps_ready.sem, steps_ready.at(b, -1))
                    act.activation(ez.ap(), compact[:, 0, :], ACT.Exp, bias=dt_bias.ap()).then_inc(exps_ready.sem, exps_ready.step)
                    act.activation(ek.ap(), compact[:, 1, :], ACT.Exp, scale=-1.0).then_inc(exps_ready.sem, exps_ready.step)
                    act.wait_ge(one_ez_ready.sem, one_ez_ready.at(b, 0))
                    act.activation(lz.ap(), w.ap(), ACT.Ln).then_inc(exps_ready.sem, exps_ready.step)
                    act.wait_ge(gate_stored.sem, gate_stored.at(b, -1))
                    act.wait_ge(svg_ready.sem, svg_ready.at(b, -1))
                    for i in range(KI):
                        act.wait_ge(tile_made.sem, tile_made.at(b, KI + i))
                        act.activation(gate[:, i, :], ps_w[(KI + i) % BANKS].ap(), ACT.Silu).then_inc(gate_ready.sem, gate_ready.step)
                    act.wait_ge(val_stored.sem, val_stored.at(b, -1))
                    act.wait_ge(u_made.sem, u_made.at(b, -1))
                    for i in range(KI):
                        act.wait_ge(conv_ready.sem, conv_ready.at(b, i))
                        act.activation(val[:, i, :], conv[:, i, :], ACT.Silu).then_inc(val_ready.sem, val_ready.step)
                    if not last:
                        copy_xnT(b + 1)
                    act.wait_ge(u_stored.sem, u_stored.at(b, -1))
                    for t in range(TT):
                        act.wait_ge(u_made.sem, u_made.at(b, t))
                        act.activation(u[:, t, :], ps_u[t % 2].ap(), ACT.Copy).then_inc(u_ready.sem, u_ready.step)

                deviation(0)
                copy_xnT(0)
                over_rows(act, body)

            @block.vector
            def _(dve):
                for s in (var_ready, xn_ready, one_ez_ready, steps_ready, conv_ready, svg_ready):
                    dve.sem_inc(s.sem, s.given * s.step)
                dve.memset(vraw.ap(), 0.0).then_inc(const_set, 1)
                dve.memset(zero.ap(), 0.0).then_inc(const_set, 1)
                dve.memset(E.ap(), 1.0).then_inc(const_set, 1)
                dve.memset(eps.ap(), LN_EPS).then_inc(const_set, 1)
                dve.wait_ge(consts_in, 96)
                dve.wait_ge(const_set, 4)
                own = Own(own_dve)

                def layernorm(b):
                    dve.wait_ge(x_in.sem, x_in.at(b, 0))
                    dve.wait_ge(sd_ready.sem, sd_ready.at(b, -1))
                    for t in range(TT):
                        dve.bn_stats(stats[:, t, :], x[:, t, :]).then_inc(own.sem, own.one())
                    dve.wait_ge(own.sem, own.n)
                    for t in range(TT):
                        ins = dve.bn_aggr(mv[:, t, :], stats[:, t, :])
                        ins.then_inc(own.sem, own.one()) if t < TT - 1 else ins.then_inc(var_ready.sem, var_ready.step)
                    dve.wait_ge(sd_ready.sem, sd_ready.at(b, 0))
                    dve.reciprocal(rstd.ap(), sd.ap()).then_inc(own.sem, own.one())
                    dve.wait_ge(own.sem, own.n)
                    dve.wait_ge(xT_made.sem, xT_made.at(b, -1))
                    for t in range(TT):
                        dve.tensor_scalar(xn[:, t, :], x[:, t, :], mv[:, t, 0:1], rstd[:, t:t + 1],
                                          ALU.subtract, ALU.mult).then_inc(xn_ready.sem, xn_ready.step)

                def convolve(b, taps_):
                    for k in taps_:
                        for i in range(KI):
                            if k == 0:
                                dve.wait_ge(vraw_ready.sem, vraw_ready.at(b, i))
                            src = vraw[:, i, k:k + T]
                            if k == 0:
                                dve.tensor_scalar(conv[:, i, :], src, taps[:, i, 0:1], dw_bias[:, i:i + 1],
                                                  ALU.mult, ALU.add).then_inc(own.sem, own.one())
                            else:
                                ins = dve.scalar_tensor_tensor(out=conv[:, i, :], in0=src, scalar=taps[:, i, k:k + 1],
                                                               in1=conv[:, i, :], op0=ALU.mult, op1=ALU.add)
                                ins.then_inc(conv_ready.sem, conv_ready.step) if k == TAPS - 1 else ins.then_inc(own.sem, own.one())
                        if k < TAPS - 1:
                            dve.wait_ge(own.sem, own.n)

                def one_plus_exp(b):
                    dve.wait_ge(exps_ready.sem, exps_ready.at(b, 0))
                    dve.tensor_scalar(ez.ap(), ez.ap(), EXP_CAP, None, ALU.min).then_inc(own.sem, own.one())
                    dve.wait_ge(own.sem, own.n)
                    dve.tensor_scalar(w.ap(), ez.ap(), 1.0, None, ALU.add).then_inc(one_ez_ready.sem, one_ez_ready.step)

                def step_sizes(b):
                    dve.wait_ge(one_ez_ready.sem, one_ez_ready.at(b, 0))
                    dve.wait_ge(steps_stored.sem, steps_stored.at(b, -1))
                    dve.tensor_scalar(kd.ap(), w.ap(), 1.0, TINY, ALU.subtract, ALU.max).then_inc(own.sem, own.one())
                    dve.wait_ge(own.sem, own.n)
                    dve.reciprocal(dt.ap(), kd.ap()).then_inc(own.sem, own.one())
                    dve.wait_ge(own.sem, own.n)
                    dve.tensor_tensor(dt.ap(), dt.ap(), ez.ap(), ALU.mult).then_inc(own.sem, own.one())
                    dve.wait_ge(exps_ready.sem, exps_ready.at(b, 2))
                    dve.tensor_scalar(kd.ap(), ek.ap(), 1.0, 1.0 / K_MAX, ALU.add, ALU.mult).then_inc(own.sem, own.one())
                    dve.wait_ge(own.sem, own.n)
                    dve.tensor_tensor(dt.ap(), dt.ap(), lz.ap(), ALU.mult).then_inc(own.sem, own.one())
                    dve.reciprocal(kd.ap(), kd.ap()).then_inc(own.sem, own.one())
                    dve.wait_ge(own.sem, own.n)
                    dve.tensor_scalar(dt.ap(), dt.ap(), DT_MIN, DT_MAX, ALU.max, ALU.min).then_inc(own.sem, own.one())
                    dve.wait_ge(own.sem, own.n)
                    dve.tensor_tensor(kd.ap(), kd.ap(), dt.ap(), ALU.mult).then_inc(own.sem, own.one())
                    dve.wait_ge(own.sem, own.n)
                    dve.tensor_scalar(kd.ap(), kd.ap(), 1.0, None, ALU.add).then_inc(own.sem, own.one())
                    dve.wait_ge(own.sem, own.n)
                    dve.tensor_tensor_scan(E[:, 1:], kd.ap(), zero.ap(), 1.0, ALU.mult, ALU.add).then_inc(own.sem, own.one())
                    dve.wait_ge(own.sem, own.n)
                    dve.reciprocal(e_inv.ap(), E[:, 1:]).then_inc(own.sem, own.one())
                    dve.tensor_tensor(beta.ap(), dt.ap(), E[:, 0:C], ALU.mult).then_inc(own.sem, own.one())
                    dve.wait_ge(own.sem, own.n)
                    dve.scalar_tensor_tensor(out=n_alpha.ap(), in0=dt.ap(), scalar=-1.0, in1=e_inv.ap(),
                                             op0=ALU.mult, op1=ALU.mult).then_inc(steps_ready.sem, steps_ready.step)

                def body(b, last):
                    if not last:
                        layernorm(b + 1)
                    dve.wait_ge(val_ready.sem, val_ready.at(b, -1))
                    convolve(b, range(TAPS // 2))
                    one_plus_exp(b)
                    convolve(b, range(TAPS // 2, TAPS))
                    step_sizes(b)
                    dve.wait_ge(svg_stored.sem, svg_stored.at(b, -1))
                    dve.wait_ge(gate_ready.sem, gate_ready.at(b, KI - 1))
                    for i in range(KI):
                        dve.wait_ge(val_ready.sem, val_ready.at(b, i))
                        dve.scalar_tensor_tensor(out=svg[:, i, :], in0=val[:, i, :], scalar=skip[:, i:i + 1],
                                                 in1=gate[:, i, :], op0=ALU.mult, op1=ALU.mult).then_inc(svg_ready.sem, svg_ready.step)
                    dve.wait_ge(own.sem, own.n)
                    dve.sem_clear(own.sem)
                    own.n = 0

                layernorm(0)
                dve.wait_ge(own.sem, own.n)
                dve.sem_clear(own.sem)
                own.n = 0
                over_rows(dve, body)


def mix(nc, a, dram):
    LAST = HG - 1
    HALF = HG // 2
    SEG = NJ * HP * T // P
    STEPS = (33, 33, 33, 29)
    MID_STEPS, LATE_STEPS = 18, 6
    assert sum(STEPS) == C
    with ExitStack() as ctx:
        def sb(name, shape):
            return ctx.enter_context(nc.sbuf_tensor("m_" + name, shape, F32))

        def ps(name):
            return ctx.enter_context(nc.psum_tensor("m_ps_" + name, [P, T], F32))

        def sem(name):
            return ctx.enter_context(nc.semaphore("m_" + name))

        def sig(name, per, step=1, credited=True):
            return Signal(ctx, nc, "m_" + name, per, step, credited)

        ident = sb("ident", [P, P])
        head_sum = sb("head_sum", [P, N])
        causal = sb("causal", [P, C])
        head_block = sb("head_block", [P, HP, DH])
        carry = sb("carry", [P, TT, C])
        A = sb("A", [P, HG])
        one = sb("one", [P, 1])
        psi = sb("psi", [P, 2, 2, HG, TT, C + 1])
        shear = sb("shear", [P, 2, HG, T])
        prod = sb("prod", [P, 2, 2, HALF * TT])
        e_end = sb("e_end", [P, HG, TT])
        w_bc = sb("w_bc", [P, NJ, KI, P])
        valT = sb("valT", [P, KI, T])
        u = sb("u", [P, 2, TT, HP * DH])
        raw = [sb(f"raw{s}", [P, NJ, T]) for s in range(2)]
        sq = sb("sq", [P, 2, T])
        scale = sb("scale", [P, NJ, T])
        rows_ = sb("rows", [P, T])
        compact = sb("compact", [P, SEG])
        factor = sb("factor", [P, SEG])
        k = [sb(f"k{s}", [P, 2, T]) for s in range(2)]
        q = [sb(f"q{s}", [P, 2, T]) for s in range(2)]
        k_head = sb("k_head", [P, HP, 2, T])
        kx = sb("kx", [P, 2, T])
        qx = sb("qx", [P, 2, T])
        g = sb("g", [P, HP, T])
        kT = sb("kT", [P, 2, (TT - 1) * P])
        dX = sb("dX", [P, TT - 1, 2, DH])
        X = sb("X", [P, TT - 1, 2, DH])
        tmp = sb("tmp", [P, 2, DH])
        Xb = sb("Xb", [P, TT - 1, 2, HP, N])
        end = sb("end", [P, TT])
        coef = sb("coef", [P, 2, 2, TT])
        y = sb("y", [P, T])
        ps_a = [ps(f"a{n}") for n in range(2)]
        ps_s = ps("s")
        ps_g = [ps(f"g{n}") for n in range(2)]
        ps_k = [ps(f"k{n}") for n in range(2)]
        ps_y = ps("y")
        KW = (TT - 1) * P
        ps_dX = ps_k[0][:, KW:KW + (TT - 1) * 2 * DH]

        consts_in = sem("consts_in")
        const_set = sem("const_set")
        w_in = [sig(f"w_in{j}", HG, 16) for j in range(NJ)]
        val_in = sig("val_in", 1, 16)
        u_in = [sig(f"u_in{s}", HG // 2, 16) for s in range(2)]
        n_alpha_in = [sig(f"n_alpha_in{n}", HP, 16) for n in range(2)]
        beta_in = [sig(f"beta_in{n}", HP, 16) for n in range(HG)]
        e_end_in = sig("e_end_in", HP, 16)
        factor_in = sig("factor_in", 3 * HG, 16)
        beta_scaled = sig("beta_scaled", HG)
        stepped = sig("stepped", 2)
        ab_ready = sig("ab_ready", HG)
        log_ready = sig("log_ready", HG)
        sum_ready = sig("sum_ready", HG)
        det_ready = sig("det_ready", HG)
        a_made = sig("a_made", HG * NJ)
        raw_ready = sig("raw_ready", HG * NJ)
        sq_ready = sig("sq_ready", HG * NJ)
        sums_made = sig("sums_made", HG * NJ)
        norm_ready = sig("norm_ready", HG)
        rows_ready = sig("rows_ready", HG)
        compact_in = sig("compact_in", HG * NJ, 16)
        rows_stored = sig("rows_stored", HG, 16)
        scale_in = sig("scale_in", HG * HP, 16)
        b_scaled = sig("b_scaled", HG * 2)
        cz_scaled = sig("cz_scaled", HG)
        cx_scaled = sig("cx_scaled", HG)
        kx_ready = sig("kx_ready", HG)
        qx_ready = sig("qx_ready", HG)
        raw_used = sig("raw_used", HG)
        k_ready = sig("k_ready", HG)
        k_head_ready = sig("k_head_ready", HG * HP)
        q_ready = sig("q_ready", HG)
        g_made = sig("g_made", HG * HP)
        g_ready = sig("g_ready", HG * HP)
        kT_made = sig("kT_made", HG * 2)
        kT_ready = sig("kT_ready", HG * 2)
        dX_made = sig("dX_made", HG)
        dX_ready = sig("dX_ready", HG)
        coef_ready = sig("coef_ready", HG)
        X_ready = sig("X_ready", HG * (TT - 1))
        Xb_ready = sig("Xb_ready", HG * (TT - 1))
        y_made = sig("y_made", HG)
        y_ready = sig("y_ready", HG)
        y_stored = sig("y_stored", HG * HP, 16)
        steps_dve, own_dve, own_pool = sem("steps_dve"), sem("own_dve"), sem("own_pool")

        def chunks(v):
            return v.rearrange("p (c t) -> p c t", c=TT)

        def spread(src, parts=N):
            return src.unsqueeze(0).to_broadcast([parts, *src.shape])

        with nc.Block() as block:
            @block.sync
            def _(sp):
                for dst, name in ((ident, "ident"), (head_sum, "head_sum"), (causal, "causal"), (A, "a_log")):
                    sp.dma_start(dst.ap(), a[name]).then_inc(consts_in, 16)
                sp.dma_start(head_block.ap().rearrange("p h d -> p (h d)"), a["head_block"]).then_inc(consts_in, 16)
                for s in (*w_in, val_in, *u_in, *n_alpha_in, *beta_in, e_end_in, factor_in, compact_in, rows_stored,
                          scale_in):
                    sp.sem_inc(s.sem, s.given * s.step)

                def heads(name, b, h, groups):
                    return dram[name][b].rearrange("(g h) t -> h g t", h=HP)[h, groups]

                def load_u(b, group):
                    heads_of_group = slice(group * HP * DH, (group + 1) * HP * DH)
                    sp.dma_start(u[:, group % 2], dram["u"][b][:, :, heads_of_group]
                                 ).then_inc(u_in[group % 2].sem, u_in[group % 2].step)

                def load_n_alpha(b, half):
                    groups = slice(half * HALF, (half + 1) * HALF)
                    for h in range(HP):
                        sp.dma_start(shear[h * N:(h + 1) * N, 1, groups, :],
                                     spread(heads("n_alpha", b, h, groups))).then_inc(n_alpha_in[half].sem, n_alpha_in[half].step)

                def load_beta(b, group):
                    for h in range(HP):
                        sp.dma_start(shear[h * N:(h + 1) * N, 0, group, :],
                                                           spread(dram["beta"][b, group * HP + h])).then_inc(beta_in[group].sem, beta_in[group].step)

                def load_e_end(b):
                    for h in range(HP):
                        sp.dma_start(e_end[h * N:(h + 1) * N, :, :], spread(heads("e_end", b, h, slice(0, HG)))).then_inc(e_end_in.sem, e_end_in.step)

                def load_factor(b, group):
                    for j, name in enumerate(("beta", "dt", "e_inv")):
                        src = dram[name][b, group * HP:(group + 1) * HP, :].rearrange("h (s t) -> (h s) t", t=SEG)
                        sp.dma_start(factor[j * N:(j + 1) * N, :], src).then_inc(factor_in.sem, factor_in.step)

                def compact_norms(b, group):
                    sp.wait_ge(norm_ready.sem, norm_ready.at(b, group))
                    for j in range(NJ):
                        sp.dma_start(compact[j * N:(j + 1) * N, :],
                                     rows_[j * N:j * N + HP, :].rearrange("h (s t) -> h s t", t=SEG)
                                     ).then_inc(compact_in.sem, compact_in.step)

                def spread_scales(b, group, u_):
                    sp.wait_ge(rows_ready.sem, rows_ready.at(b, group))
                    sp.dma_start(dram["norm"][u_].rearrange("r (s t) -> (r s) t", t=SEG),
                                 compact.ap()).then_inc(rows_stored.sem, rows_stored.step)
                    sp.wait_ge(rows_stored.sem, rows_stored.at(b, group))
                    sp.wait_ge(cz_scaled.sem, cz_scaled.at(b, group - 1))
                    sp.wait_ge(cx_scaled.sem, cx_scaled.at(b, group - 1))
                    for h in range(HP):
                        src = dram["norm"][u_].rearrange("(j h) t -> h j t", h=HP)[h]
                        sp.dma_start(scale[h * N:(h + 1) * N, :, :], spread(src)).then_inc(scale_in.sem, scale_in.step)

                load_n_alpha(0, 0)
                for group in range(HALF):
                    load_beta(0, group)
                for j in range(NJ):
                    sp.dma_start(w_bc[:, j, :, :].rearrange("p k m -> p (k m)"), a["w_bcT"][0, j]).then_inc(w_in[j].sem, w_in[j].step)
                sp.dma_start(valT.ap(), dram["valT"][0]).then_inc(val_in.sem, val_in.step)
                sp.wait_ge(const_set, 6)
                load_factor(0, 0)
                load_n_alpha(0, 1)
                for group in range(HALF, HG):
                    load_beta(0, group)
                load_e_end(0)
                load_u(0, 0)
                compact_norms(0, 0)
                spread_scales(0, 0, 0)

                def body(b, last):
                    for group in range(HG):
                        ahead = not (last and group == LAST)
                        if ahead:
                            nb, ng = (b, group + 1) if group < LAST else (b + 1, 0)
                            sp.wait_ge(rows_ready.sem, rows_ready.at(b, group))
                            load_factor(nb, ng)
                        if not last:
                            if group % HALF == HALF - 1:
                                sp.wait_ge(ab_ready.sem, ab_ready.at(b, group))
                                load_n_alpha(b + 1, group // HALF)
                            if group == LAST - 1:
                                sp.wait_ge(a_made.sem, a_made.at(b, HG * NJ - 1))
                                sp.dma_start(valT.ap(), dram["valT"][b + 1]).then_inc(val_in.sem, val_in.step)
                            sp.wait_ge(cx_scaled.sem, cx_scaled.at(b, group))
                            sp.wait_ge(coef_ready.sem, coef_ready.at(b, group))
                            load_beta(b + 1, group)
                        if ahead:
                            sp.wait_ge(y_made.sem, y_made.at(b, group - 1))
                            load_u(nb, ng)
                            compact_norms(b, group + 1)
                            spread_scales(b, group + 1, (group + 1) % 2)
                    if not last:
                        load_e_end(b + 1)
                over_rows(sp, body)

            @block.gpsimd
            def _(pool):
                for s in (ab_ready, cx_scaled, kx_ready, qx_ready, Xb_ready):
                    pool.sem_inc(s.sem, s.given * s.step)
                own = Own(own_pool)
                pool.wait_ge(consts_in, 80)
                pool.wait_ge(const_set, 6)

                def det_steps(b, group):
                    if group % HALF == 0:
                        pool.wait_ge(stepped.sem, stepped.at(b, group // HALF))
                    g_ = group % HG
                    pool.tensor_tensor(shear[:, 0, g_, :], shear[:, 0, g_, :], shear[:, 1, g_, :],
                                       ALU.mult).then_inc(ab_ready.sem, ab_ready.step)

                det_steps(0, 0)

                def body(b, last):
                    for group in range(HG):
                        s = group % 2
                        r4 = raw[s]
                        pool.wait_ge(b_scaled.sem, b_scaled.at(b, group * 2))
                        pool.wait_ge(k_ready.sem, k_ready.at(b, group - 1))
                        for row in range(2):
                            ins = pool.tensor_tensor(chunks(kx[:, row, :]), chunks(r4[:, 1, :]),
                                                     psi[:, row, 1, group, :, 1:], ALU.mult)
                            ins.then_inc(own.sem, own.one()) if row == 0 else ins.then_inc(kx_ready.sem, kx_ready.step)
                        pool.wait_ge(scale_in.sem, scale_in.at(b, (group + 1) * HP - 1))
                        pool.wait_ge(raw_ready.sem, raw_ready.at(b, group * NJ + 3))
                        pool.tensor_tensor(r4[:, 3, :], r4[:, 3, :], scale[:, 3, :], ALU.mult).then_inc(own.sem, own.one())
                        pool.wait_ge(det_ready.sem, det_ready.at(b, group))
                        pool.wait_ge(own.sem, own.n)
                        pool.tensor_tensor(r4[:, 3, :], r4[:, 3, :], shear[:, 0, group, :],
                                           ALU.mult).then_inc(cx_scaled.sem, cx_scaled.step)
                        pool.wait_ge(cx_scaled.sem, cx_scaled.at(b, group))
                        pool.wait_ge(q_ready.sem, q_ready.at(b, group - 1))
                        for row in range(2):
                            ins = pool.tensor_tensor(chunks(qx[:, row, :]), chunks(r4[:, 3, :]),
                                                     psi[:, row, 0, group, :, 1:], ALU.mult)
                            ins.then_inc(own.sem, own.one()) if row == 0 else ins.then_inc(qx_ready.sem, qx_ready.step)
                        if not (last and group == LAST):
                            det_steps(b, group + 1)
                        for c in range(TT - 1):
                            pool.wait_ge(X_ready.sem, X_ready.at(b, group * (TT - 1) + c))
                            pool.wait_ge(y_made.sem, y_made.at(b, group - 1))
                            for part in range(2):
                                ins = pool.tensor_tensor(
                                    Xb[:, c, part, :, 0:DH], X[:, c, part, :].unsqueeze(1).to_broadcast([P, HP, DH]),
                                    head_block.ap(), ALU.mult)
                                ins.then_inc(own.sem, own.one()) if part == 0 else ins.then_inc(Xb_ready.sem, Xb_ready.step)
                    pool.wait_ge(own.sem, own.n)
                    pool.sem_clear(own.sem)
                    own.n = 0
                over_rows(pool, body)

            @block.tensor
            def _(pe):
                for s in (a_made, sums_made, g_made, kT_made, dX_made, y_made):
                    pe.sem_inc(s.sem, s.given * s.step)
                pe.wait_ge(consts_in, 80)
                pe.wait_ge(const_set, 6)

                def products(b, group, js):
                    for j in js:
                        pe.wait_ge(w_in[j].sem, w_in[j].at(b, group))
                        if group % HG == 0 and j == 0:
                            pe.wait_ge(val_in.sem, val_in.at(b, group // HG))
                        pe.wait_ge(raw_ready.sem, raw_ready.at(b, group * NJ + j - 2))
                        for kt in range(KI):
                            mm = pe.matmul(ps_a[j % 2].ap(), w_bc[:, j, kt, :], valT[:, kt, :],
                                           start=(kt == 0), stop=(kt == KI - 1))
                        mm.then_inc(a_made.sem, a_made.step)
                        if j:
                            sum_squares(b, group, j - 1)

                def sum_squares(b, group, j):
                    pe.wait_ge(sq_ready.sem, sq_ready.at(b, group * NJ + j))
                    pe.wait_ge(norm_ready.sem, norm_ready.at(b, group - 1))
                    pe.matmul(ps_s[j * N:(j + 1) * N, :], head_sum.ap(), sq[:, j % 2, :],
                              start=True, stop=True, skip_group_check=True).then_inc(sums_made.sem, sums_made.step)

                def scores(b, group, h, s):
                    pe.wait_ge(g_ready.sem, g_ready.at(b, group * HP + h - 2))
                    pe.wait_ge(k_head_ready.sem, k_head_ready.at(b, group * HP + h))
                    for c in range(TT):
                        cols = slice(c * C, (c + 1) * C)
                        for part in range(2):
                            mm = pe.matmul(ps_g[h % 2][:, cols], k_head[:, h, part, cols], q[s][:, part, cols],
                                           start=(part == 0), stop=(part == 1), skip_group_check=True)
                    mm.then_inc(g_made.sem, g_made.step)

                def inner(b, group, ahead):
                    s = group % 2
                    pe.wait_ge(k_ready.sem, k_ready.at(b, group))
                    pe.wait_ge(kT_ready.sem, kT_ready.at(b, group * 2 - 1))
                    pe.wait_ge(dX_ready.sem, dX_ready.at(b, group - 1))
                    for part in range(2):
                        for c in range(TT - 1):
                            mm = pe.transpose(ps_k[part][:, c * P:(c + 1) * P],
                                              k[s][:, part, c * C:(c + 1) * C], ident.ap())
                        mm.then_inc(kT_made.sem, kT_made.step)
                    if ahead:
                        sum_squares(b, group + 1, NJ - 1)
                    pe.wait_ge(q_ready.sem, q_ready.at(b, group))
                    for h in range(2):
                        scores(b, group, h, s)
                    pe.wait_ge(kT_ready.sem, kT_ready.at(b, group * 2 + 1))
                    pe.wait_ge(u_in[s].sem, u_in[s].at(b, group // 2))
                    for c in range(TT - 1):
                        for part in range(2):
                            for h in range(HP):
                                col = KW + (c * 2 + part) * DH
                                mm = pe.matmul(ps_k[0][h * N:(h + 1) * N, col:col + DH],
                                               kT[:, part, c * P + h * N:c * P + (h + 1) * N],
                                               u[:, s, c, h * DH:(h + 1) * DH], start=True, stop=True,
                                               skip_group_check=True)
                    mm.then_inc(dX_made.sem, dX_made.step)
                    for h in range(2, HP):
                        scores(b, group, h, s)

                def outputs(b, group):
                    s = group % 2
                    pe.wait_ge(g_ready.sem, g_ready.at(b, group * HP + HP - 1))
                    pe.wait_ge(y_ready.sem, y_ready.at(b, group - 1))
                    for c in range(TT):
                        cols = slice(c * C, (c + 1) * C)
                        for h in range(HP):
                            pe.matmul(ps_y[h * N:h * N + DH, cols], u[:, s, c, h * DH:(h + 1) * DH], g[:, h, cols],
                                      start=(c == 0), stop=False, skip_group_check=True)
                    for c in range(1, TT):
                        cols = slice(c * C, (c + 1) * C)
                        pe.wait_ge(Xb_ready.sem, Xb_ready.at(b, group * (TT - 1) + c - 1))
                        for part in range(2):
                            mm = pe.matmul(ps_y[:, cols], Xb[:, c - 1, part, :, :].rearrange("p h d -> p (h d)"),
                                           q[s][:, part, cols], start=False, stop=(part == 1),
                                           skip_group_check=True)
                    mm.then_inc(y_made.sem, y_made.step)

                products(0, 0, range(NJ))
                sum_squares(0, 0, NJ - 1)
                products(0, 1, range(NJ))
                inner(0, 0, True)

                def body(b, last):
                    for group in range(HG):
                        more = not (last and group >= LAST - 1)
                        if more:
                            products(b, group + 2, (0, 1))
                        outputs(b, group)
                        if more:
                            products(b, group + 2, (2, 3))
                        if not (last and group == LAST):
                            inner(b, group + 1, more)
                over_rows(pe, body)

            @block.scalar
            def _(act):
                for s in (beta_scaled, log_ready, det_ready, raw_ready, sq_ready, norm_ready, kT_ready, y_ready,
                          y_stored, k_head_ready):
                    act.sem_inc(s.sem, s.given * s.step)
                act.wait_ge(consts_in, 80)
                act.wait_ge(const_set, 6)
                own_a = sem("own_act")
                act.activation(A.ap(), A.ap(), ACT.Exp).then_inc(own_a, 1)
                act.wait_ge(own_a, 1)

                def scale_beta(b, group):
                    act.wait_ge(beta_in[group].sem, beta_in[group].at(b, HP - 1))
                    act.activation(shear[:, 0, group, :], shear[:, 0, group, :], ACT.Copy,
                                                  scale=A[:, group:group + 1]).then_inc(beta_scaled.sem, beta_scaled.step)

                def split_head(b, group, h):
                    act.wait_ge(k_ready.sem, k_ready.at(b, group))
                    act.wait_ge(g_made.sem, g_made.at(b, (group - 1) * HP + h))
                    rows = slice(h * N, (h + 1) * N)
                    act.activation(k_head[rows, h], k[group % 2][rows], ACT.Copy).then_inc(k_head_ready.sem, k_head_ready.step)

                def evacuate(b, group, j, loads=True):
                    s = group % 2
                    if j == 0:
                        act.wait_ge(raw_used.sem, raw_used.at(b, group - 2))
                        act.wait_ge(kx_ready.sem, kx_ready.at(b, group - 2))
                        act.wait_ge(qx_ready.sem, qx_ready.at(b, group - 2))
                    act.wait_ge(a_made.sem, a_made.at(b, group * NJ + j))
                    act.wait_ge(sums_made.sem, sums_made.at(b, group * NJ + j - 2))
                    act.activation(sq[:, j % 2, :], ps_a[j % 2].ap(), ACT.Square).then_inc(sq_ready.sem, sq_ready.step)
                    act.activation(raw[s][:, j, :], ps_a[j % 2].ap(), ACT.Copy).then_inc(raw_ready.sem, raw_ready.step)
                    if loads:
                        act.dma_start(w_bc[:, j, :, :].rearrange("p k m -> p (k m)"),
                                      a["w_bcT"][(group + 1) % HG, j]).then_inc(w_in[j].sem, w_in[j].step)

                def norms(b, group):
                    act.wait_ge(sums_made.sem, sums_made.at(b, group * NJ + NJ - 1))
                    act.wait_ge(compact_in.sem, compact_in.at(b, group * NJ - 1))
                    act.activation(rows_.ap(), ps_s.ap(), ACT.Sqrt).then_inc(norm_ready.sem, norm_ready.step)

                def copy_kT(b, group):
                    for part in range(2):
                        act.wait_ge(kT_made.sem, kT_made.at(b, group * 2 + part))
                        act.wait_ge(dX_made.sem, dX_made.at(b, group - 1))
                        act.activation(kT[:, part, :], ps_k[part][:, 0:KW], ACT.Copy).then_inc(kT_ready.sem, kT_ready.step)

                def store_y(b, group):
                    act.wait_ge(y_made.sem, y_made.at(b, group))
                    act.wait_ge(y_stored.sem, y_stored.at(b, group * HP - 1))
                    act.activation(y.ap(), ps_y.ap(), ACT.Copy).then_inc(y_ready.sem, y_ready.step)
                    act.wait_ge(y_ready.sem, y_ready.at(b, group))
                    for h in range(HP):
                        act.dma_start(dram["yT"][b, group, h * DH:(h + 1) * DH, :],
                                      y[h * N:h * N + DH, :]).then_inc(y_stored.sem, y_stored.step)

                def det_log(b, group):
                    act.wait_ge(ab_ready.sem, ab_ready.at(b, group))
                    act.activation(shear[:, 0, group % HG, :], shear[:, 0, group % HG, :], ACT.Ln,
                                   bias=one[:, :], scale=-1.0).then_inc(log_ready.sem, log_ready.step)

                def det_inverse(b, group):
                    act.wait_ge(sum_ready.sem, sum_ready.at(b, group))
                    act.activation(shear[:, 0, group % HG, :], shear[:, 0, group % HG, :], ACT.Exp,
                                   scale=-1.0).then_inc(det_ready.sem, det_ready.step)

                for group in range(HALF):
                    scale_beta(0, group)
                for j in range(NJ):
                    evacuate(0, 0, j)
                norms(0, 0)
                for group in range(HALF, HG):
                    scale_beta(0, group)
                det_log(0, 0)
                det_inverse(0, 0)
                for j in range(NJ):
                    evacuate(0, 1, j)
                for h in range(HP):
                    split_head(0, 0, h)
                copy_kT(0, 0)
                norms(0, 1)
                det_log(0, 1)

                def body(b, last):
                    for group in range(HG):
                        unit = group + 1
                        more = not (last and group >= LAST - 1)
                        here = not (last and group == LAST)
                        if not last:
                            scale_beta(b + 1, group)
                        if more:
                            evacuate(b, group + 2, 0, not (last and group == LAST - 2))
                        if here:
                            det_inverse(b, unit)
                        if more:
                            evacuate(b, group + 2, 1, not (last and group == LAST - 2))
                        store_y(b, group)
                        if more:
                            evacuate(b, group + 2, 2, not (last and group == LAST - 2))
                        if here:
                            split_head(b, unit, 0)
                            split_head(b, unit, 1)
                        if more:
                            evacuate(b, group + 2, 3, not (last and group == LAST - 2))
                        if more:
                            norms(b, group + 2)
                        if here:
                            copy_kT(b, unit)
                            split_head(b, unit, 2)
                            split_head(b, unit, 3)
                        if more:
                            det_log(b, group + 2)
                over_rows(act, body)
                act.wait_ge(y_stored.sem, y_stored.at(B - 1, HG * HP - 1))

            @block.vector
            def _(dve):
                for s in (stepped, sum_ready, rows_ready, b_scaled, cz_scaled, raw_used, k_ready, q_ready, g_ready, dX_ready,
                          coef_ready, X_ready):
                    dve.sem_inc(s.sem, s.given * s.step)
                dve.memset(one.ap(), 1.0).then_inc(const_set, 1)
                dve.memset(Xb.ap(), 0.0).then_inc(const_set, 1)
                dve.memset(k_head.ap(), 0.0).then_inc(const_set, 1)
                dve.memset(factor.ap(), 1.0).then_inc(const_set, 1)
                dve.memset(ps_y.ap(), 0.0).then_inc(const_set, 1)
                dve.memset(carry.ap(), 1.0).then_inc(const_set, 1)
                own = Own(own_dve)
                dve.wait_ge(const_set, 6)
                dve.memset(carry[:, :, 0:1], 0.0).then_inc(own.sem, own.one())
                for row in range(2):
                    for comp in range(2):
                        dve.memset(psi[:, row, comp, :, :, 0:1], 1.0 if row == comp else 0.0).then_inc(own.sem, own.one())
                dve.wait_ge(own.sem, own.n)
                dve.sem_clear(own.sem)
                own.n = 0
                steps = Own(steps_dve)
                psi_t = [psi.ap().rearrange("p r k g c t -> p r k (g c) t")[:, :, :, n * HALF * TT:(n + 1) * HALF * TT, :]
                         for n in range(2)]
                shear_t = [shear.ap().rearrange("p k g (c t) -> p k (g c) t", c=TT)[:, :, n * HALF * TT:(n + 1) * HALF * TT, :]
                           for n in range(2)]

                def start_psi(b, half):
                    dve.wait_ge(n_alpha_in[half].sem, n_alpha_in[half].at(b, HP - 1))
                    dve.wait_ge(beta_scaled.sem, beta_scaled.at(b, half * HALF + HALF - 1))
                    dve.wait_ge(kx_ready.sem, kx_ready.at(b - 1, half * HALF + HALF - 1))
                    dve.wait_ge(qx_ready.sem, qx_ready.at(b - 1, half * HALF + HALF - 1))

                def step_psi(b, half, first, last):
                    for i in range(first, last):
                        t = i // 2
                        if i:
                            dve.wait_ge(steps.sem, steps.n)
                        if i % 2 == 0:
                            dve.tensor_tensor(prod.ap(), psi_t[half][:, :, :, :, t],
                                              shear_t[half][:, :, :, t].unsqueeze(1).to_broadcast([P, 2, 2, HALF * TT]),
                                              ALU.mult).then_inc(steps.sem, steps.one())
                        else:
                            ins = dve.tensor_tensor(psi_t[half][:, :, :, :, t + 1], psi_t[half][:, :, :, :, t],
                                                    prod[:, :, ::-1, :], ALU.add)
                            ins.then_inc(steps.sem, steps.one()) if t < C - 1 else ins.then_inc(stepped.sem, stepped.step)

                def step_rows(b, half, t):
                    before = steps.n
                    for row in range(2):
                        if t:
                            dve.wait_ge(steps.sem, before if row else before - 1)
                        dve.tensor_tensor(prod[:, row], psi_t[half][:, row, :, :, t], shear_t[half][:, :, :, t],
                                          ALU.mult).then_inc(steps.sem, steps.one())
                    for row in range(2):
                        dve.wait_ge(steps.sem, before + 1 + row)
                        ins = dve.tensor_tensor(psi_t[half][:, row, :, :, t + 1], psi_t[half][:, row, :, :, t],
                                                prod[:, row, ::-1, :], ALU.add)
                        ins.then_inc(steps.sem, steps.one()) if row == 0 or t < C - 1 else ins.then_inc(stepped.sem, stepped.step)

                def log_sum(b, group):
                    dve.wait_ge(log_ready.sem, log_ready.at(b, group))
                    dve.tensor_tensor_scan(shear[:, 0, group % HG, :], carry.ap().rearrange("p c t -> p (c t)"),
                                           shear[:, 0, group % HG, :], 0.0, ALU.mult, ALU.add).then_inc(sum_ready.sem, sum_ready.step)

                def clear_counts():
                    dve.wait_ge(own.sem, own.n)
                    dve.sem_clear(own.sem)
                    own.n = 0
                    dve.wait_ge(steps.sem, steps.n)
                    dve.sem_clear(steps.sem)
                    steps.n = 0

                def scales(b, group, between):
                    dve.wait_ge(compact_in.sem, compact_in.at(b, (group + 1) * NJ - 1))
                    dve.tensor_scalar(compact.ap(), compact.ap(), NORM_EPS, None, ALU.add).then_inc(own.sem, own.one())
                    between(1)
                    dve.wait_ge(own.sem, own.n)
                    dve.reciprocal(compact.ap(), compact.ap()).then_inc(own.sem, own.one())
                    between(1)
                    dve.wait_ge(factor_in.sem, factor_in.at(b, 3 * (group + 1) - 1))
                    dve.wait_ge(own.sem, own.n)
                    dve.tensor_tensor(compact.ap(), compact.ap(), factor.ap(), ALU.mult).then_inc(rows_ready.sem, rows_ready.step)
                    between(1)

                start_psi(0, 0)
                for t in range(C):
                    if t == C // 2:
                        scales(0, 0, lambda n: None)
                    step_rows(0, 0, t)
                log_sum(0, 0)
                clear_counts()

                def body(b, last):
                    dve.wait_ge(e_end_in.sem, e_end_in.at(b, HP - 1))
                    for group in range(HG):
                        s = group % 2
                        r4 = raw[s]
                        psi_b, half, slot = (b, 1, group) if group < HALF else (b + 1, 0, group - HALF)
                        done, end_at = 2 * sum(STEPS[:slot]), 2 * sum(STEPS[:slot + 1])
                        if last and half == 0:
                            done = end_at

                        def advance(n):
                            nonlocal done
                            n = min(n, end_at - done)
                            if n and done == 0:
                                start_psi(psi_b, half)
                            step_psi(psi_b, half, done, done + n)
                            done += n

                        def advance_rows(n):
                            nonlocal done
                            if done < end_at:
                                advance(done % 2)
                            for i in range(min(n, end_at - done) // 2):
                                if i == 0:
                                    dve.wait_ge(steps.sem, steps.n)
                                if done == 0:
                                    start_psi(psi_b, half)
                                step_rows(psi_b, half, done // 2)
                                done += 2

                        dve.wait_ge(scale_in.sem, scale_in.at(b, (group + 1) * HP - 1))
                        for j in range(2):
                            dve.wait_ge(raw_ready.sem, raw_ready.at(b, group * NJ + 1 - j))
                            ins = dve.tensor_tensor(r4[:, 1 - j, :], r4[:, 1 - j, :], scale[:, 1 - j, :], ALU.mult)
                            ins.then_inc(b_scaled.sem, b_scaled.step)
                            advance(1)
                        dve.wait_ge(b_scaled.sem, b_scaled.at(b, group * 2 + 1))
                        dve.wait_ge(kT_made.sem, kT_made.at(b, 2 * (group - 2) + 1))
                        dve.wait_ge(g_made.sem, g_made.at(b, (group - 1) * HP - 1))
                        dve.wait_ge(y_made.sem, y_made.at(b, group - 2))
                        for row in range(2):
                            dve.tensor_tensor(chunks(k[s][:, row, :]), chunks(r4[:, 0, :]),
                                                  psi[:, row, 0, group, :, 0:C], ALU.mult).then_inc(own.sem, own.one())
                            advance(2)
                        dve.wait_ge(kx_ready.sem, kx_ready.at(b, group))
                        dve.wait_ge(own.sem, own.n)
                        dve.tensor_tensor(k[s].ap(), k[s].ap(), kx.ap(), ALU.add).then_inc(k_ready.sem, k_ready.step)
                        advance(1)
                        dve.wait_ge(raw_ready.sem, raw_ready.at(b, group * NJ + 2))
                        dve.tensor_tensor(r4[:, 2, :], r4[:, 2, :], scale[:, 2, :], ALU.mult).then_inc(own.sem, own.one())
                        advance(1)
                        dve.wait_ge(det_ready.sem, det_ready.at(b, group))
                        dve.wait_ge(own.sem, own.n)
                        dve.tensor_tensor(r4[:, 2, :], r4[:, 2, :], shear[:, 0, group, :],
                                          ALU.mult).then_inc(cz_scaled.sem, cz_scaled.step)
                        advance(1)
                        dve.wait_ge(cz_scaled.sem, cz_scaled.at(b, group))
                        for row in range(2):
                            ins = dve.tensor_tensor(chunks(q[s][:, 1 - row, :]), chunks(r4[:, 2, :]),
                                                    psi[:, row, 1, group, :, 1:], ALU.mult)
                            ins.then_inc(own.sem, own.one()) if row == 0 else ins.then_inc(raw_used.sem, raw_used.step)
                            advance(1)
                        dve.wait_ge(raw_used.sem, raw_used.at(b, group))
                        dve.wait_ge(own.sem, own.n)
                        dve.wait_ge(qx_ready.sem, qx_ready.at(b, group))
                        dve.tensor_tensor(q[s][:, 0, :], q[s][:, 0, :], qx[:, 1, :], ALU.subtract).then_inc(own.sem, own.one())
                        advance(1)
                        dve.tensor_tensor(q[s][:, 1, :], qx[:, 0, :], q[s][:, 1, :], ALU.subtract).then_inc(q_ready.sem, q_ready.step)
                        advance(1)
                        dve.wait_ge(det_ready.sem, det_ready.at(b, group))
                        det_end = chunks(shear[:, 0, group, :])[:, :, C - 1]
                        dve.tensor_tensor(end.ap(), det_end, e_end[:, group, :], ALU.mult).then_inc(own.sem, own.one())
                        advance(1)
                        dve.wait_ge(own.sem, own.n)
                        for comp, by in ((1, end.ap()), (0, det_end)):
                            ins = dve.tensor_tensor(coef[:, comp, :, :], psi[:, :, comp, group, :, C],
                                                    by.unsqueeze(1).to_broadcast([P, 2, TT]), ALU.mult)
                            ins.then_inc(own.sem, own.one()) if comp else ins.then_inc(coef_ready.sem, coef_ready.step)
                            advance(1)

                        def mask(h):
                            dve.wait_ge(g_made.sem, g_made.at(b, group * HP + h))
                            dve.wait_ge(y_made.sem, y_made.at(b, group - 1))
                            dve.tensor_tensor(chunks(g[:, h, :]), chunks(ps_g[h % 2].ap()),
                                              causal.ap().unsqueeze(1).to_broadcast([P, TT, C]),
                                              ALU.mult).then_inc(g_ready.sem, g_ready.step)
                            advance(1)

                        advance_rows(MID_STEPS)
                        for h in range(2):
                            mask(h)
                        advance_rows(LATE_STEPS)
                        if not (last and group == LAST):
                            scales(b, group + 1, advance)
                        dve.wait_ge(dX_made.sem, dX_made.at(b, group))
                        dve.tensor_copy(dX.ap().rearrange("p c r d -> p (c r d)"), ps_dX).then_inc(dX_ready.sem, dX_ready.step)
                        advance(1)
                        for h in range(2, HP):
                            mask(h)
                        dve.wait_ge(dX_ready.sem, dX_ready.at(b, group))
                        dve.wait_ge(coef_ready.sem, coef_ready.at(b, group))
                        dve.wait_ge(Xb_ready.sem, Xb_ready.at(b, group * (TT - 1) - 1))
                        for c in range(TT - 1):
                            if c:
                                dve.wait_ge(X_ready.sem, X_ready.at(b, group * (TT - 1) + c - 1))
                                dve.tensor_tensor(dX[:, c], dX[:, c], X[:, c - 1], ALU.add).then_inc(own.sem, own.one())
                                advance(2)
                                dve.wait_ge(own.sem, own.n)
                            for part in range(2):
                                comp, row = (1, 0) if part == 0 else (0, 1)
                                dve.tensor_scalar(tmp[:, part, :], dX[:, c, 1 - part, :],
                                                      coef[:, comp, row, c:c + 1], None, ALU.mult).then_inc(own.sem, own.one())
                                advance(1)
                            dve.wait_ge(own.sem, own.n)
                            for part in range(2):
                                comp, row = (1, 1) if part == 0 else (0, 0)
                                ins = dve.scalar_tensor_tensor(
                                    out=X[:, c, part, :], in0=dX[:, c, part, :], scalar=coef[:, comp, row, c:c + 1],
                                    in1=tmp[:, part, :], op0=ALU.mult, op1=ALU.subtract)
                                ins.then_inc(own.sem, own.one()) if part == 0 else ins.then_inc(X_ready.sem, X_ready.step)
                                advance(1)
                            dve.wait_ge(own.sem, own.n)
                        if not (last and group == LAST):
                            log_sum(b, group + 1)
                        advance_rows(end_at - done)
                    clear_counts()
                over_rows(dve, body)


def ffn(nc, a, dram, out):
    F32R = mybir.dt.float32r
    with ExitStack() as ctx:
        def sb(name, shape, dt=F32):
            return ctx.enter_context(nc.sbuf_tensor("f_" + name, shape, dt))

        def sem(name):
            return ctx.enter_context(nc.semaphore("f_" + name))

        def sig(name, per, step=1, credited=True):
            return Signal(ctx, nc, "f_" + name, per, step, credited)

        ident = sb("ident", [P, P])
        ones = sb("ones", [P, P])
        w_out = sb("w_out", [P, KI, D])
        w1 = sb("w1", [P, KD, FF])
        w2 = sb("w2", [P, KF, D])
        above = sb("above", [P, KD * FF])
        below = sb("below", [P, KD * FF])
        t1 = sb("t1", [P, KD, FF], F32R)
        t2 = sb("t2", [P, KF, D], F32R)
        b1 = sb("b1", [P, KF])
        b2 = sb("b2", [P, D])
        eps = sb("eps", [P, 1])
        total = sb("total", [P, 2])
        half = sb("half", [P, 2])
        nhalf = sb("nhalf", [P, 2])
        y = [sb(f"y{s}", [P, KI, T]) for s in range(2)]
        gate = [sb(f"gate{s}", [P, KI, T]) for s in range(2)]
        svg = [sb(f"svg{s}", [P, KI, T]) for s in range(2)]
        x = [sb(f"x{s}", [P, TT, D]) for s in range(2)]
        x1 = [sb(f"x1{s}", [P, TT, D]) for s in range(2)]
        proj = sb("proj", [P, TT, D])
        stats = sb("stats", [P, TT, 6])
        mv = [sb(f"mv{n}", [P, TT, 2]) for n in range(3)]
        sd = [sb(f"sd{n}", [P, TT]) for n in range(3)]
        rstd = [sb(f"rstd{n}", [P, TT]) for n in range(3)]
        on = sb("on", [P, TT, D])
        xn = sb("xn", [P, TT, D])
        xh = sb("xh", [P, KD, T], F32R)
        xl = sb("xl", [P, KD, T], F32R)
        g = sb("g", [P, KF, T])
        gh = sb("gh", [P, KF, T], F32R)
        gl = sb("gl", [P, KF, T], F32R)
        o2 = sb("o2", [P, TT, D])
        res = sb("res", [P, TT, D])
        ps_o = [ctx.enter_context(nc.psum_tensor(f"f_ps_o{k}", [P, 2, D], F32)) for k in range(2)]
        ps_x = [ctx.enter_context(nc.psum_tensor(f"f_ps_x{k}", [P, T], F32)) for k in range(KD)]
        ps_h = [ctx.enter_context(nc.psum_tensor(f"f_ps_h{k}", [P, T], F32)) for k in range(2)]
        ps_2 = [ctx.enter_context(nc.psum_tensor(f"f_ps_2{k}", [P, 2, D], F32)) for k in range(2)]

        consts_in = sem("consts_in")
        weights_in = sem("weights_in")
        const_set = sem("const_set")
        sums_made = sem("sums_made")
        ternary_ready = sem("ternary_ready")
        x_in = [sig(f"x_in{s}", 1, 16) for s in range(2)]
        y_in = [sig(f"y_in{s}", 3, 16) for s in range(2)]
        gated = sig("gated", 1)
        proj_made = sig("proj_made", 1)
        proj_ready = sig("proj_ready", 2)
        proj_used = sig("proj_used", 1)
        x1_ready = sig("x1_ready", 1)
        var_ready = sig("var_ready", 2)
        sd_ready = sig("sd_ready", 2)
        var2_ready = sig("var2_ready", 1)
        sd2_ready = sig("sd2_ready", 1)
        xn_ready = sig("xn_ready", 1)
        xT_made = sig("xT_made", 1)
        xh_ready = sig("xh_ready", KD)
        xl_ready = sig("xl_ready", KD)
        h_made = sig("h_made", KF)
        g_ready = sig("g_ready", KF)
        gh_ready = sig("gh_ready", KF)
        gl_ready = sig("gl_ready", KF)
        o2_made = sig("o2_made", 1)
        o2_ready = sig("o2_ready", 1)
        res_ready = sig("res_ready", 1)
        res_stored = sig("res_stored", 1, 16)
        own_dve, own_pool = sem("own_dve"), sem("own_pool")

        def rows(eng, body):
            for s in range(2):
                body(s, s, 0, 3)
            with eng.Fori(1, B // 2 - 1) as i:
                for s in range(2):
                    body(i * 2 + s, s, i, 3)
            for s in range(2):
                body(B - 2 + s, s, B // 2 - 1, 1 - s)

        with nc.Block() as block:
            @block.sync
            def _(sp):
                for dst, src in ((ident, a["ident"]), (b1, a["b1"])):
                    sp.dma_start(dst.ap(), src).then_inc(consts_in, 16)
                sp.dma_start(b2.ap(), a["b2"].to_broadcast([P, D])).then_inc(consts_in, 16)
                for s in (*x_in, *y_in):
                    sp.sem_inc(s.sem, s.given * s.step)

                def load_gates(b, s):
                    for dst, name in ((gate, "gateT"), (svg, "svgT")):
                        sp.dma_start(dst[s].ap(), dram[name][b]).then_inc(y_in[s].sem, y_in[s].step)

                def load_y(b, s):
                    src = dram["yT"][b].rearrange("g c t -> (g c) t").rearrange("(k p) t -> p k t", p=P)
                    sp.dma_start(y[s].ap(), src).then_inc(y_in[s].sem, y_in[s].step)

                def load_x(b, s):
                    sp.dma_start(x[s].ap(), a["x"][b].rearrange("(t p) d -> p t d", p=P)).then_inc(x_in[s].sem, x_in[s].step)

                for s in range(2):
                    load_y(s, s)
                    load_gates(s, s)
                    if s == 0:
                        sp.dma_start(w1.ap(), a["w1T"].rearrange("(k p) o -> p k o", p=P)).then_inc(weights_in, 16)
                        sp.dma_start(w2.ap(), a["w2T"].rearrange("(k p) o -> p k o", p=P)).then_inc(weights_in, 16)
                        sp.dma_start(w_out.ap(), a["w_outT"].rearrange("(k p) o -> p k o", p=P)).then_inc(consts_in, 16)
                    load_x(s, s)
                with sp.Fori(0, B // 2 - 1) as i:
                    for s in range(2):
                        sp.wait_ge(gated.sem, gated.at(i * 2 + s, 0))
                        load_gates(i * 2 + s + 2, s)
                        sp.wait_ge(proj_made.sem, proj_made.at(i * 2 + s, 0))
                        load_y(i * 2 + s + 2, s)
                        sp.wait_ge(x1_ready.sem, x1_ready.at(i * 2 + s, 0))
                        load_x(i * 2 + s + 2, s)

            @block.gpsimd
            def _(pool):
                pool.sem_inc(gated.sem, gated.given * gated.step)
                own = Own(own_pool)

                def body(b, s, i, left):
                    pool.wait_ge(y_in[s].sem, y_in[s].at(i, 2))
                    pool.tensor_tensor(y[s].ap(), y[s].ap(), gate[s].ap(), ALU.mult).then_inc(own.sem, own.one())
                    pool.wait_ge(own.sem, own.n)
                    pool.tensor_tensor(y[s].ap(), y[s].ap(), svg[s].ap(), ALU.add).then_inc(gated.sem, gated.step)
                    pool.wait_ge(own.sem, own.n)
                    pool.sem_clear(own.sem)
                    own.n = 0
                rows(pool, body)

            @block.tensor
            def _(pe):
                for s in (proj_made, xT_made, h_made, o2_made):
                    pe.sem_inc(s.sem, s.given * s.step)
                pe.wait_ge(consts_in, 64)

                def project_out(b, s, t):
                    if t == 0:
                        pe.wait_ge(gated.sem, gated.at(b, 0))
                        pe.wait_ge(proj_ready.sem, proj_ready.at(b, -1))
                    for k in range(KI):
                        mm = pe.matmul(ps_o[t // 2][:, t % 2, :], y[s][:, k, t * P:(t + 1) * P], w_out[:, k, :],
                                       start=(k == 0), stop=(k == KI - 1), skip_group_check=True)
                    if t == TT - 1:
                        mm.then_inc(proj_made.sem, proj_made.step)

                def transpose_xn(b):
                    pe.wait_ge(xn_ready.sem, xn_ready.at(b, 0))
                    pe.wait_ge(xl_ready.sem, xl_ready.at(b, -1))
                    for k in range(KD):
                        for t in range(TT):
                            mm = pe.transpose(ps_x[k][:, t * P:(t + 1) * P], xn[:, t, k * P:(k + 1) * P], ident.ap())
                    mm.then_inc(xT_made.sem, xT_made.step)

                for t in range(TT):
                    project_out(0, 0, t)
                    if t == 0:
                        pe.wait_ge(const_set, 4)
                        pe.matmul(ps_h[0][:, 0:2], ones.ap(), total.ap(), start=True, stop=True).then_inc(sums_made, 1)
                for t in range(TT):
                    project_out(1, 1, t)
                transpose_xn(0)
                pe.wait_ge(ternary_ready, 2)

                def body(b, s, i, left):
                    pe.wait_ge(xl_ready.sem, xl_ready.at(b, KD - 1))
                    for f in range(KF):
                        pe.wait_ge(g_ready.sem, g_ready.at(b, f - 2))
                        for k in range(KD):
                            for part in (xh, xl):
                                mm = pe.matmul(ps_h[f % 2].ap(), t1[:, k, f * P:(f + 1) * P], part[:, k, :],
                                               start=(k == 0 and part is xh), stop=(k == KD - 1 and part is xl))
                        mm.then_inc(h_made.sem, h_made.step)
                    if left > 1:
                        for t in range(TT):
                            project_out(b + 2, s, t)
                    if left:
                        transpose_xn(b + 1)
                    pe.wait_ge(gl_ready.sem, gl_ready.at(b, KF - 1))
                    pe.wait_ge(o2_ready.sem, o2_ready.at(b, -1))
                    for t in range(TT):
                        for f in range(KF):
                            for part in (gh, gl):
                                mm = pe.matmul(ps_2[t // 2][:, t % 2, :], part[:, f, t * P:(t + 1) * P], t2[:, f, :],
                                               start=(f == 0 and part is gh), stop=(f == KF - 1 and part is gl),
                                               skip_group_check=True)
                    mm.then_inc(o2_made.sem, o2_made.step)
                rows(pe, body)

            @block.scalar
            def _(act):
                for s in (sd_ready, sd2_ready, proj_ready, xh_ready, g_ready, gh_ready, res_stored):
                    act.sem_inc(s.sem, s.given * s.step)
                act.wait_ge(consts_in, 64)
                act.wait_ge(const_set, 4)

                def deviation(b, n):
                    act.wait_ge(var_ready.sem, var_ready.at(b, n))
                    act.activation(sd[n].ap(), mv[n][:, :, 1], ACT.Sqrt, bias=eps.ap()).then_inc(sd_ready.sem, sd_ready.step)

                def copy_projection(b):
                    act.wait_ge(proj_made.sem, proj_made.at(b, 0))
                    act.wait_ge(proj_used.sem, proj_used.at(b, -1))
                    for n in range(2):
                        act.activation(proj[:, 2 * n:2 * n + 2, :], ps_o[n].ap(), ACT.Copy).then_inc(proj_ready.sem, proj_ready.step)

                def high_part(b):
                    act.wait_ge(xT_made.sem, xT_made.at(b, 0))
                    act.wait_ge(h_made.sem, h_made.at(b, -1))
                    for k in range(KD):
                        act.activation(xh[:, k, :], ps_x[k].ap(), ACT.Copy).then_inc(xh_ready.sem, xh_ready.step)

                def store(b):
                    act.wait_ge(res_ready.sem, res_ready.at(b, 0))
                    act.dma_start(out[b].rearrange("(t p) d -> p t d", p=P), res.ap()).then_inc(res_stored.sem, res_stored.step)

                copy_projection(0)
                deviation(0, 0)
                deviation(0, 1)
                copy_projection(1)
                high_part(0)
                deviation(1, 0)

                def body(b, s, i, left):
                    act.wait_ge(o2_made.sem, o2_made.at(b, -1))
                    for f in range(KF):
                        act.wait_ge(h_made.sem, h_made.at(b, f))
                        act.wait_ge(gl_ready.sem, gl_ready.at(b - 1, f))
                        act.activation(g[:, f, :], ps_h[f % 2].ap(), ACT.Gelu, bias=b1[:, f:f + 1]).then_inc(g_ready.sem, g_ready.step)
                        act.wait_ge(g_ready.sem, g_ready.at(b, f))
                        act.activation(gh[:, f, :], g[:, f, :], ACT.Copy).then_inc(gh_ready.sem, gh_ready.step)
                    if not (isinstance(b, int) and b == 0):
                        store(b - 1)
                    if left:
                        deviation(b + 1, 1)
                    if left > 1:
                        copy_projection(b + 2)
                    if left:
                        high_part(b + 1)
                    if left > 1:
                        deviation(b + 2, 0)
                    act.wait_ge(var2_ready.sem, var2_ready.at(b, 0))
                    act.activation(sd[2].ap(), mv[2][:, :, 1], ACT.Sqrt, bias=eps.ap()).then_inc(sd2_ready.sem, sd2_ready.step)
                rows(act, body)
                store(B - 1)
                act.wait_ge(res_stored.sem, res_stored.at(B - 1, 0))

            @block.vector
            def _(dve):
                for s in (var_ready, var2_ready, proj_used, x1_ready, xn_ready, xl_ready, gl_ready, o2_ready, res_ready):
                    dve.sem_inc(s.sem, s.given * s.step)
                own = Own(own_dve)
                dve.memset(ones.ap(), 1.0).then_inc(const_set, 1)
                dve.memset(eps.ap(), LN_EPS).then_inc(const_set, 1)
                def moments(src, n, signal):
                    for t in range(TT):
                        dve.bn_stats(stats[:, t, :], src(t)).then_inc(own.sem, own.one())
                    dve.wait_ge(own.sem, own.n)
                    for t in range(TT):
                        ins = dve.bn_aggr(mv[n][:, t, :], stats[:, t, :])
                        ins.then_inc(own.sem, own.one()) if t < TT - 1 else ins.then_inc(signal.sem, signal.step)

                def normalise(dst, src, n, count=None):
                    for t in range(TT):
                        ins = dve.tensor_scalar(dst[:, t, :], src(t), mv[n][:, t, 0:1], rstd[n][:, t:t + 1],
                                                ALU.subtract, ALU.mult)
                        ins.then_inc(own.sem, own.one()) if count is None or t < TT - 1 else ins.then_inc(count.sem, count.step)

                def projection_moments(b):
                    dve.wait_ge(proj_ready.sem, proj_ready.at(b, 1))
                    moments(lambda t: proj[:, t, :], 0, var_ready)

                def first_residual(b, s, i):
                    dve.wait_ge(sd_ready.sem, sd_ready.at(b, 0))
                    dve.reciprocal(rstd[0].ap(), sd[0].ap()).then_inc(own.sem, own.one())
                    dve.wait_ge(own.sem, own.n)
                    normalise(on, lambda t: proj[:, t, :], 0, proj_used)
                    dve.wait_ge(own.sem, own.n)
                    dve.wait_ge(proj_used.sem, proj_used.at(b, 0))
                    dve.wait_ge(x_in[s].sem, x_in[s].at(i, 0))
                    dve.tensor_tensor(x1[s].ap(), x[s].ap(), on.ap(), ALU.add).then_inc(x1_ready.sem, x1_ready.step)
                    dve.wait_ge(x1_ready.sem, x1_ready.at(b, 0))
                    moments(lambda t: x1[s][:, t, :], 1, var_ready)

                def second_norm(b, s):
                    dve.wait_ge(sd_ready.sem, sd_ready.at(b, 1))
                    dve.reciprocal(rstd[1].ap(), sd[1].ap()).then_inc(own.sem, own.one())
                    dve.wait_ge(own.sem, own.n)
                    dve.wait_ge(xT_made.sem, xT_made.at(b, -1))
                    normalise(xn, lambda t: x1[s][:, t, :], 1, xn_ready)

                def low_part(b):
                    dve.wait_ge(h_made.sem, h_made.at(b, -1))
                    for k in range(KD):
                        dve.wait_ge(xh_ready.sem, xh_ready.at(b, k))
                        dve.tensor_tensor(xl[:, k, :], ps_x[k].ap(), xh[:, k, :].bitcast(F32), ALU.subtract).then_inc(xl_ready.sem, xl_ready.step)

                dve.wait_ge(weights_in, 32)
                flat = [w.ap().rearrange("p k o -> p (k o)") for w in (w1, w2)]
                for n in range(2):
                    dve.tensor_reduce(total[:, n:n + 1], flat[n], AX.X, ALU.add,
                                      apply_absolute_value=True).then_inc(const_set, 1)
                dve.wait_ge(sums_made, 1)
                dve.tensor_scalar(half.ap(), ps_h[0][:, 0:2], 1.0 / (D * FF), NORM_EPS, ALU.mult, ALU.max).then_inc(own.sem, own.one())
                dve.wait_ge(own.sem, own.n)
                dve.tensor_scalar(nhalf.ap(), half.ap(), -0.5, None, ALU.mult).then_inc(own.sem, own.one())
                dve.wait_ge(own.sem, own.n)
                dve.tensor_scalar(half.ap(), half.ap(), 0.5, None, ALU.mult).then_inc(own.sem, own.one())
                dve.wait_ge(own.sem, own.n)
                for n, (w, tern) in enumerate(((flat[0], t1), (flat[1], t2))):
                    dve.tensor_scalar(above.ap(), w, half[:, n:n + 1], None, ALU.is_gt).then_inc(own.sem, own.one())
                    dve.tensor_scalar(below.ap(), w, nhalf[:, n:n + 1], None, ALU.is_lt).then_inc(own.sem, own.one())
                    dve.wait_ge(own.sem, own.n)
                    dve.tensor_tensor(tern.ap().rearrange("p k o -> p (k o)"), above.ap(), below.ap(),
                                      ALU.subtract).then_inc(ternary_ready, 1)
                    dve.wait_ge(ternary_ready, n + 1)
                projection_moments(0)
                first_residual(0, 0, 0)
                second_norm(0, 0)
                projection_moments(1)
                low_part(0)
                dve.wait_ge(own.sem, own.n)
                dve.sem_clear(own.sem)
                own.n = 0

                def body(b, s, i, left):
                    dve.wait_ge(o2_made.sem, o2_made.at(b, -1))
                    for f in range(KF):
                        dve.wait_ge(gh_ready.sem, gh_ready.at(b, f))
                        dve.tensor_tensor(gl[:, f, :], g[:, f, :], gh[:, f, :].bitcast(F32), ALU.subtract).then_inc(gl_ready.sem, gl_ready.step)
                        if left and f == KF // 2 - 1:
                            first_residual(b + 1, 1 - s, i + s)
                    if left:
                        second_norm(b + 1, 1 - s)
                    if left > 1:
                        projection_moments(b + 2)
                    if left:
                        low_part(b + 1)
                    dve.wait_ge(o2_made.sem, o2_made.at(b, 0))
                    for half_ in range(2):
                        ins = dve.tensor_tensor(o2[:, 2 * half_:2 * half_ + 2, :], ps_2[half_].ap(),
                                                b2.ap().unsqueeze(1).to_broadcast([P, 2, D]), ALU.add)
                        ins.then_inc(o2_ready.sem, o2_ready.step) if half_ else ins.then_inc(own.sem, own.one())
                    dve.wait_ge(own.sem, own.n)
                    dve.wait_ge(o2_ready.sem, o2_ready.at(b, 0))
                    moments(lambda t: o2[:, t, :], 2, var2_ready)
                    dve.wait_ge(sd2_ready.sem, sd2_ready.at(b, 0))
                    dve.reciprocal(rstd[2].ap(), sd[2].ap()).then_inc(own.sem, own.one())
                    dve.wait_ge(own.sem, own.n)
                    normalise(o2, lambda t: o2[:, t, :], 2)
                    dve.wait_ge(own.sem, own.n)
                    dve.wait_ge(res_stored.sem, res_stored.at(b, -1))
                    dve.tensor_tensor(res.ap(), x1[s].ap(), o2.ap(), ALU.add).then_inc(res_ready.sem, res_ready.step)
                    dve.wait_ge(own.sem, own.n)
                    dve.sem_clear(own.sem)
                    own.n = 0
                rows(dve, body)


def build(nc, a, out):
    def scratch(name, *shape):
        return nc.dram_tensor("scratch_" + name, shape, F32, kind="Internal").ap()

    dram = {
        "n_alpha": scratch("n_alpha", B, H, T), "beta": scratch("beta", B, H, T), "dt": scratch("dt", B, H, T),
        "e_inv": scratch("e_inv", B, H, T), "e_end": scratch("e_end", B, H, TT),
        "valT": scratch("valT", B, P, KI, T), "gateT": scratch("gateT", B, P, KI, T),
        "svgT": scratch("svgT", B, P, KI, T), "u": scratch("u", B, P, TT, DI),
        "norm": scratch("norm", 2, NJ * HP, T), "yT": scratch("yT", B, HG, HP * DH, T),
    }
    project(nc, a, dram)
    mix(nc, a, dram)
    ffn(nc, a, dram, out)


_OUTS = [((B, T, D), "float32")]


def kernel(L0_attn_x, L0_attn_W_in, L0_attn_dw_weight, L0_attn_dw_bias, L0_attn_W_bc, L0_attn_W_out, L0_attn_skip,
           L0_attn_A_log, L0_attn_dt_bias, L0_ffn_W1, L0_ffn_b1, L0_ffn_W2, L0_ffn_b2):
    import numpy as np
    import concourse.bacc as _bacc
    from concourse.bass_utils import run_bass_kernel_spmd as _run

    def tiles(v):
        v = np.asarray(v)
        return v.reshape(-1, P, *v.shape[1:]).swapaxes(0, 1)

    w_in = np.asarray(L0_attn_W_in)
    steps = w_in[2 * DI:].reshape(H, 2, D)
    w_bc = np.asarray(L0_attn_W_bc).reshape(HG, HP, NJ, N, KI, P)
    p = np.arange(P)
    arrays = {
        "x": L0_attn_x,
        "w_inT": np.concatenate([w_in[:2 * DI], steps[:, 0], steps[:, 1]]).T,
        "taps": tiles(L0_attn_dw_weight), "dw_bias": tiles(L0_attn_dw_bias), "skip": tiles(L0_attn_skip),
        "dt_bias": np.repeat(np.asarray(L0_attn_dt_bias), TT).reshape(P, 1),
        "w_bcT": w_bc.transpose(0, 2, 5, 4, 1, 3).reshape(HG, NJ, P, KI * P),
        "a_log": np.asarray(L0_attn_A_log).reshape(HG, P).T,
        "w_outT": np.asarray(L0_attn_W_out).T,
        "w1T": np.asarray(L0_ffn_W1).T, "b1": tiles(L0_ffn_b1),
        "w2T": np.asarray(L0_ffn_W2).T, "b2": np.asarray(L0_ffn_b2).reshape(1, D),
        "ident": np.eye(P, dtype=np.float32),
        "head_sum": (p[:, None] // N == np.arange(N)[None]).astype(np.float32),
        "causal": (p[:, None] <= p[None]).astype(np.float32),
        "head_block": np.repeat((p[:, None] // N == np.arange(HP)[None]).astype(np.float32), DH, axis=1),
    }
    arrays = {k: np.ascontiguousarray(v) for k, v in arrays.items()}
    nc = _bacc.Bacc("TRN2", target_bir_lowering=False, num_devices=1)
    a = {k: nc.dram_tensor("in_" + k, v.shape, mybir.dt.from_np(v.dtype), kind="ExternalInput").ap()
         for k, v in arrays.items()}
    out = nc.dram_tensor("out_0", _OUTS[0][0], F32, kind="ExternalOutput").ap()
    build(nc, a, out)
    r = _run(nc, [{"in_" + k: v for k, v in arrays.items()}], core_ids=[0])
    return r.results[0]["out_0"]
```
